# Optimizing a Trainium2 kernel written in Bass

```python
import numpy as np
import jax
import jax.numpy as jnp

def _softmax(x, axis=-1):
    return jax.nn.softmax(x, axis=axis)

def _gelu(x):
    return jax.nn.gelu(x, approximate=True)

def _silu(x):
    return jax.nn.silu(x)

def _sigmoid(x):
    return jax.nn.sigmoid(x)

def _layernorm(x, axis=-1, eps=1e-05):
    m = jnp.mean(x, axis=axis, keepdims=True)
    v = jnp.var(x, axis=axis, keepdims=True)
    return (x - m) / jnp.sqrt(v + eps)

def _scatter_add(tgt, idx, src, axis=0):
    return tgt.at[idx].add(src)

def _segment_sum(src, seg, n):
    return jax.ops.segment_sum(src, seg, n)
kernel_name = 'mk_gnn_resnorm_d4_gnn_r8_edce85'

def setup_inputs(seed: int=0):
    np.random.seed(seed)
    _w = jnp.asarray

    def _rec_inputs():
        import jax
        import jax.numpy as jnp
        _gk = jax.random.key(seed)
        x = -0.0001006 + 1 * jax.random.normal(jax.random.fold_in(_gk, 1), (12500, 48), jnp.float32)
        src = jax.random.randint(jax.random.fold_in(_gk, 2), (200000,), 0, 12500, jnp.int32)
        dst = jax.random.randint(jax.random.fold_in(_gk, 3), (200000,), 0, 12500, jnp.int32)
        _o = jnp.argsort(dst, stable=True)
        src = src[_o]
        dst = dst[_o]
        edge_attr_16 = 0.000196303 + 1.00016 * jax.random.normal(jax.random.fold_in(_gk, 12), (200000, 16), jnp.float32)
        edge_weight = jax.random.uniform(jax.random.fold_in(_gk, 14), (200000,), jnp.float32, 0.0, 1)
        return (x, src, dst, edge_attr_16, edge_weight)
    x, src, dst, edge_attr_16, edge_weight = _rec_inputs()

    def _L0_gnn_setup():
        import jax, jax.numpy as jnp
        import numpy as np
        K = 10
        ALPHA = 0.1
        N_NODES = 12500
        N_EDGES = 200000
        D_FEAT = 48
        key = jax.random.key(seed)
        k1, k2, k3, k4 = jax.random.split(key, 4)
        feat = jax.random.normal(k1, (N_NODES, D_FEAT), dtype=jnp.float32)
        edge_weight = jax.random.uniform(k2, (N_EDGES,), dtype=jnp.float32)
        src = jax.random.randint(k3, (N_EDGES,), 0, N_NODES, dtype=jnp.int32)
        dst = jax.random.randint(k4, (N_EDGES,), 0, N_NODES, dtype=jnp.int32)
        return {'feat': feat, 'edge_weight': edge_weight, 'src': src, 'dst': dst}
    _L0_gnn_all = _L0_gnn_setup()
    _L0_gnn_in = {k: v for k, v in _L0_gnn_all.items() if k in ()}
    del _L0_gnn_all

    def _L1_gnn_setup():
        import jax, jax.numpy as jnp
        import numpy as np
        N_NODES = 12500
        N_EDGES = 200000
        N_FEAT = 48
        N_EDGE_FEAT = 16
        HIDDEN = 128
        key = jax.random.key(seed)
        ks = jax.random.split(key, 8)
        tot = 2 * N_FEAT + N_EDGE_FEAT
        s1 = 1.0 / np.sqrt(tot)
        s2 = 1.0 / np.sqrt(HIDDEN)
        return {'x': jax.random.normal(ks[0], (N_NODES, N_FEAT), dtype=jnp.float32), 'edge_index': jax.random.randint(ks[1], (2, N_EDGES), 0, N_NODES, dtype=jnp.int64), 'edge_feat': jax.random.normal(ks[2], (N_EDGES, N_EDGE_FEAT), dtype=jnp.float32), 'W1': jax.random.normal(ks[3], (tot, HIDDEN), dtype=jnp.float32) * s1, 'b1': jnp.zeros((HIDDEN,), dtype=jnp.float32), 'W2': jax.random.normal(ks[4], (HIDDEN, HIDDEN), dtype=jnp.float32) * s2, 'b2': jnp.zeros((HIDDEN,), dtype=jnp.float32), 'W3': jax.random.normal(ks[5], (HIDDEN, N_FEAT), dtype=jnp.float32) * s2, 'b3': jnp.zeros((N_FEAT,), dtype=jnp.float32)}
    _L1_gnn_all = _L1_gnn_setup()
    _L1_gnn_in = {k: v for k, v in _L1_gnn_all.items() if k in ('W1', 'b1', 'W2', 'b2', 'W3', 'b3')}
    del _L1_gnn_all

    def _L2_gnn_setup():
        import jax, jax.numpy as jnp
        import numpy as np
        N_NODES = 6250
        N_EDGES = 200000
        D_IN = 48
        D_OUT = 48
        key = jax.random.key(seed)
        k1, k2, k3, k4 = jax.random.split(key, 4)
        features = jax.random.normal(k1, (N_NODES, D_IN), dtype=jnp.float32)
        src = jax.random.randint(k2, (N_EDGES,), 0, N_NODES, dtype=jnp.int64)
        dst = jax.random.randint(k3, (N_EDGES,), 0, N_NODES, dtype=jnp.int64)
        std = np.sqrt(2.0 / (D_IN + D_OUT))
        W = jax.random.normal(k4, (D_OUT, D_IN), dtype=jnp.float32) * std
        b = jnp.zeros((D_OUT,), dtype=jnp.float32)
        return {'features': features, 'src': src, 'dst': dst, 'W': W, 'b': b}
    _L2_gnn_all = _L2_gnn_setup()
    _L2_gnn_in = {k: v for k, v in _L2_gnn_all.items() if k in ('W', 'b')}
    del _L2_gnn_all

    def _L3_gnn_setup():
        import jax, jax.numpy as jnp
        import numpy as np
        N_NODES = 12500
        N_EDGES = 200000
        IN_CH = 48
        OUT_CH = 48
        BN_EPS = 1e-05
        key = jax.random.key(seed)
        k1, k2, k3, k4 = jax.random.split(key, 4)
        x = jax.random.normal(k1, (N_NODES, IN_CH), dtype=jnp.float32)
        edge_index = jax.random.randint(k2, (2, N_EDGES), 0, N_NODES, dtype=jnp.int32)
        W = jax.random.normal(k3, (IN_CH, OUT_CH), dtype=jnp.float32) * (1.0 / np.sqrt(IN_CH))
        b = jnp.zeros((OUT_CH,), dtype=jnp.float32)
        gamma = jnp.ones((OUT_CH,), dtype=jnp.float32)
        beta = jnp.zeros((OUT_CH,), dtype=jnp.float32)
        return {'x': x, 'edge_index': edge_index, 'W': W, 'b': b, 'gamma': gamma, 'beta': beta}
    _L3_gnn_all = _L3_gnn_setup()
    _L3_gnn_in = {k: v for k, v in _L3_gnn_all.items() if k in ('W', 'b', 'gamma', 'beta')}
    del _L3_gnn_all
    return {'x': x, 'src': src, 'dst': dst, 'edge_attr_16': edge_attr_16, 'edge_weight': edge_weight, 'L1_gnn_W1': _L1_gnn_in['W1'], 'L1_gnn_b1': _L1_gnn_in['b1'], 'L1_gnn_W2': _L1_gnn_in['W2'], 'L1_gnn_b2': _L1_gnn_in['b2'], 'L1_gnn_W3': _L1_gnn_in['W3'], 'L1_gnn_b3': _L1_gnn_in['b3'], 'L2_gnn_W': _L2_gnn_in['W'], 'L2_gnn_b': _L2_gnn_in['b'], 'L3_gnn_W': _L3_gnn_in['W'], 'L3_gnn_b': _L3_gnn_in['b'], 'L3_gnn_gamma': _L3_gnn_in['gamma'], 'L3_gnn_beta': _L3_gnn_in['beta']}

def reference(x, src, dst, edge_attr_16, edge_weight, L1_gnn_W1, L1_gnn_b1, L1_gnn_W2, L1_gnn_b2, L1_gnn_W3, L1_gnn_b3, L2_gnn_W, L2_gnn_b, L3_gnn_W, L3_gnn_b, L3_gnn_gamma, L3_gnn_beta):
    import jax
    import jax.numpy as jnp

    def _L0_gnn_ref(feat, edge_weight, src, dst):
        import jax, jax.numpy as jnp
        import numpy as np
        K = 10
        ALPHA = 0.1
        N_NODES = 12500
        N_EDGES = 200000
        D_FEAT = 48
        n = feat.shape[0]
        feat_0 = feat

        def step(f, _):
            msg = f[src] * edge_weight[:, None]
            agg = jax.ops.segment_sum(msg, dst, num_segments=n)
            f = (1.0 - ALPHA) * agg + ALPHA * feat_0
            return (f, None)
        out, _ = jax.lax.scan(step, feat, None, length=K)
        return out

    def _L1_gnn_ref(x, edge_index, edge_feat, W1, b1, W2, b2, W3, b3):
        import jax, jax.numpy as jnp
        import numpy as np
        N_NODES = 12500
        N_EDGES = 200000
        N_FEAT = 48
        N_EDGE_FEAT = 16
        HIDDEN = 128
        source = edge_index[0]
        target = edge_index[1]
        edge = jnp.concatenate([x[source], x[target], edge_feat], axis=-1)
        h = jax.nn.relu(edge @ W1 + b1)
        h = jax.nn.relu(h @ W2 + b2)
        message = h @ W3 + b3
        n = x.shape[0]
        msum = jax.ops.segment_sum(message, target, num_segments=n)
        cnt = jax.ops.segment_sum(jnp.ones((target.shape[0],), dtype=x.dtype), target, num_segments=n)
        update = msum / jnp.maximum(cnt, 1.0)[:, None]
        return x + update

    def _L2_gnn_ref(features, src, dst, W, b):
        import jax, jax.numpy as jnp
        import numpy as np
        N_NODES = 6250
        N_EDGES = 200000
        D_IN = 48
        D_OUT = 48
        n = features.shape[0]
        ones = jnp.ones(src.shape[0], dtype=features.dtype)
        out_deg = jax.ops.segment_sum(ones, src, num_segments=n)
        in_deg = jax.ops.segment_sum(ones, dst, num_segments=n)
        ci = jax.lax.rsqrt(jnp.maximum(out_deg, 1.0))
        cj = jax.lax.rsqrt(jnp.maximum(in_deg, 1.0))
        msg = features[src] * ci[src][:, None]
        agg = jax.ops.segment_sum(msg, dst, num_segments=n) * cj[:, None]
        h = jnp.where(in_deg[:, None] > 0, agg, features)
        out = jax.nn.relu(h @ W.T + b)
        return out

    def _L3_gnn_ref(x, edge_index, W, b, gamma, beta):
        import jax, jax.numpy as jnp
        import numpy as np
        N_NODES = 12500
        N_EDGES = 200000
        IN_CH = 48
        OUT_CH = 48
        BN_EPS = 1e-05
        N = x.shape[0]
        loops = jnp.arange(N, dtype=edge_index.dtype)
        src = jnp.concatenate([edge_index[0], loops])
        dst = jnp.concatenate([edge_index[1], loops])
        deg = jax.ops.segment_sum(jnp.ones_like(dst, dtype=x.dtype), dst, num_segments=N)
        dinv = jax.lax.rsqrt(deg)
        norm = dinv[src] * dinv[dst]
        h = x @ W
        msg = h[src] * norm[:, None]
        agg = jax.ops.segment_sum(msg, dst, num_segments=N) + b
        mean = jnp.mean(agg, axis=0)
        var = jnp.mean(jnp.square(agg - mean), axis=0)
        y = (agg - mean) * jax.lax.rsqrt(var + BN_EPS) * gamma + beta
        return jax.nn.relu(y)
    edge_index = jnp.stack([src, dst])
    x = _layernorm(x + _L0_gnn_ref(x, edge_weight, src, dst), axis=-1)
    x = _layernorm(x + _L1_gnn_ref(x, edge_index, edge_attr_16, L1_gnn_W1, L1_gnn_b1, L1_gnn_W2, L1_gnn_b2, L1_gnn_W3, L1_gnn_b3), axis=-1)
    x = _layernorm(x + _L2_gnn_ref(x, src, dst, L2_gnn_W, L2_gnn_b), axis=-1)
    x = _layernorm(x + _L3_gnn_ref(x, edge_index, L3_gnn_W, L3_gnn_b, L3_gnn_gamma, L3_gnn_beta), axis=-1)
    return x

_drawn_inputs = setup_inputs


def setup_inputs(seed=0):
    import zlib

    import numpy as np

    out = dict(_drawn_inputs(seed))
    spreads = {'L1_gnn_b1': (0.0, 0.1),
     'L1_gnn_b2': (0.0, 0.1),
     'L1_gnn_b3': (0.0, 0.1),
     'L2_gnn_b': (0.0, 0.1),
     'L3_gnn_b': (0.0, 0.1),
     'L3_gnn_gamma': (1.0, 0.2),
     'L3_gnn_beta': (0.0, 0.1)}
    factors = {}
    for name, (base, spread) in spreads.items():
        noise = np.random.default_rng([zlib.crc32(name.encode()), seed]).standard_normal(out[name].shape)
        drawn = base * np.exp(spread * noise) if base else spread * noise
        out[name] = jnp.asarray(drawn.astype(out[name].dtype))
    for name, factor in factors.items():
        out[name] = (out[name] * factor).astype(out[name].dtype)
    return out
```

```python
from contextlib import ExitStack

import concourse.bass as bass
from concourse import mybir

P = 128
TILES = 8
SLOTS = 4
GROUP = P * TILES
WIN = 2 * P
F32 = mybir.dt.float32
BF16 = mybir.dt.bfloat16
I32 = mybir.dt.int32
ALU = mybir.AluOpType
ACT = mybir.ActivationFunctionType
AX = mybir.AxisListType.X
HOPS = 10
START = 4
HC2 = 64
ALPHA = 0.1
EPS = 1e-5


def build(nc, x, src, dst, edge_attr, edge_weight, W1, b1, W2, b2, W3, b3, L2_W, L2_b,
          L3_W, L3_b, gamma, beta, out):
    N, D = x.shape
    E = src.shape[0]
    DE = edge_attr.shape[1]
    H = W2.shape[0]
    KE = 2 * D + DE
    NB = -(-N // P)
    NFULL = N // P
    NREST = N - NFULL * P
    GFULL = E // GROUP
    EREST = E - GFULL * GROUP
    TP = EREST // TILES
    NG = -(-E // GROUP)
    NG += -NG % SLOTS
    WINDOWS = -(-NB // 2)
    SUP = 512
    GPS = 12
    SUPS = next(n for n in range(2, 99, 2) if (NG - GPS * n) * GROUP * N // E + 100 <= SUP * n)
    DG = NG - GPS * SUPS
    CHB = 7
    CPS = NB // CHB
    RING = 4
    assert NB % CHB == 0 and 2 * CPS % RING == 0 and DG > 0 and DG % SLOTS == 0
    DENSE = SUPS * P * NB * SUP
    assert DENSE % P == 0
    HALF = TILES // 2
    HC = H + 1
    assert EREST % TILES == 0 and NB % 7 == 0 or True

    ctx = ExitStack()
    with ctx:
        def sb(name, shape, dt=F32):
            return ctx.enter_context(nc.sbuf_tensor(name, shape, dt))

        def pb(name, shape, dt=F32):
            return ctx.enter_context(nc.psum_tensor(name, shape, dt))

        sems_by_name = {}

        def sem(name):
            if name not in sems_by_name:
                sems_by_name[name] = ctx.enter_context(nc.semaphore(name))
            return sems_by_name[name]

        src_i = sb("src_i", [P, NG + SLOTS, TILES], I32)
        dst_f = sb("dst_f", [P, NG + 1, TILES])
        wgt = sb("wgt", [P, NG + 1, TILES])
        base0 = sb("base0", [P, NG + 1])
        base = sb("base", [P, NG + 1])
        base_blk = sb("base_blk", [1, NG + 1], I32)
        sweep0 = sb("sweep0", [P, 1])
        near = sb("near", [P, 1])
        sweeps_i = sb("sweeps_i", [1, 2], I32)
        addr = sb("addr", [P, DG, TILES], I32)
        xc = sb("xc", [P, NB, D])
        tmp_raw = sb("tmp", [P, max(NB * D, 2 * 2 * HALF * P + 2 * HALF * P + HALF * (3 * H + 1) + 2 * P, 2 * CHB * SUP + SUP)])
        tmp = tmp_raw[:, 0:NB * D].rearrange("p (b f) -> p b f", f=D)
        acc = sb("acc", [P, max((NB + 1) * HC, (NB + 1) * D + 2 * CHB * SUP)])
        indeg = sb("indeg", [P, NB])
        outdeg = sb("outdeg", [P, NB])
        f01_raw = sb("f01", [P, max(NB * D, SLOTS * TILES * (KE + DE))])
        f01 = f01_raw[:, 0:NB * D].rearrange("p (b f) -> p b f", f=D)
        idx = sb("idx", [P, SLOTS, TILES], I32)
        parts48 = sb("parts48", [P, SLOTS, TILES, 3 * D], BF16)
        idd = sb("idd", [P, SLOTS, TILES], I32)
        lol = sb("lol", [P, SLOTS, TILES])
        hil = sb("hil", [P, SLOTS, TILES])
        dloc = sb("dloc", [P, SLOTS, TILES])
        wl = sb("wl", [P, SLOTS, TILES])
        onehot_b = sb("onehot", [P, SLOTS, TILES, WIN], BF16)
        msg = sb("msg", [P, SLOTS, TILES, D])
        src_lo = sb("src_lo", [P, NG + 1, TILES])
        src_hi = sb("src_hi", [P, NG + 1, TILES])
        past_i = sb("past_i", [P, 1], I32)
        before = sb("before", [P, P])
        valid = sb("valid", [P, 1])
        work = onehot_b[:, :, :, :].rearrange("p u k n -> p (u k n)").bitcast(F32)
        iota_i = sb("iota_i", [P, WIN], I32)
        iota = sb("iota", [P, WIN])
        row_i = sb("row_i", [P, 1], I32)
        row = sb("row", [P, 1])
        ident = sb("ident", [P, P])
        ones = sb("ones", [P, P])

        ps = [pb(f"ps{i}", [P, 2, 512]) for i in range(3)]
        spare = pb("spare", [P, 512])
        misc = pb("misc", [P, 512])
        psD, psDT = ps[2][:, 0, :], ps[2][:, 1, :]
        sums, psT, ps1, ps2 = ps[0], ps[1][:, 0, :], ps[1][:, 1, :], ps[2][:, 0, :]
        cnt_ps = spare[:, 0:P]
        iota_ps = misc[:, 0:WIN]

        table = nc.dram_tensor("node_table", (NB * P, D), F32).ap()
        dense = nc.dram_tensor("dense", (DENSE + P, 1), F32).ap()
        dense_v = dense[0:DENSE, :].rearrange("(b p s f) a -> b p (s f a)", b=SUPS, p=P, s=NB)
        table_v = table.rearrange("(b p) f -> p b f", p=P)

        def clear(sems, gathers=()):
            for s in gathers:
                nc.gpsimd.dma_reset(range(s.num, s.num + 1))
            if gathers:
                nc.all_engine_barrier()
            for s in [*sems, *gathers]:
                nc.sync.sem_clear(s)
            nc.all_engine_barrier()

        def slot_sems(name):
            return [sem(f"{name}{u}") for u in range(SLOTS)]

        def load_nodes(eng, to, frm, done):
            n = 0
            eng.dma_start(to[:, 0:NFULL, :], frm[0:NFULL * P, :].rearrange("(b p) f -> p b f", p=P)).then_inc(done, 16)
            n += 16
            if NREST:
                eng.dma_start(to[0:NREST, NFULL, :], frm[NFULL * P:N, :]).then_inc(done, 16)
                n += 16
            return n

        i_zero, i_src, i_x, i_dst, i_wgt, i_first, i_const, i_chk, i_iota = (
            sem(n) for n in ("prep_zeroed", "src_in", "x_in", "dst_in", "wgt_in", "first_in", "prep_const",
                             "prep_check", "prep_iota"))
        i_step, i_sum, i_tab = sem("prep_step"), sem("prep_sum"), sem("table_stored")
        with nc.Block() as block:
            dst_i = acc[:, 0:(NG + 1) * TILES].bitcast(I32).rearrange("p (g k) -> p g k", k=TILES)
            first_i = work[:, 2048:2048 + NG + 1].bitcast(I32)
            first_f = work[:, 3072:3072 + NG + 1]
            chk = sb("chk", [P, 8])

            @block.sync
            def _(sp):
                sp.wait_ge(i_zero, 4)
                for arr, dr, s in ((src_i, src, i_src), (dst_i, dst, i_dst), (wgt, edge_weight, i_wgt)):
                    sp.dma_start(arr[:, 0:GFULL, :], dr[0:GFULL * GROUP].rearrange("(g p k) -> p g k", p=P, k=TILES)).then_inc(s, 16)
                    if TP:
                        sp.dma_start(arr[0:TP, GFULL, :], dr[GFULL * GROUP:E].rearrange("(p k) -> p k", k=TILES)).then_inc(s, 16)
                load_nodes(sp, xc, x, i_x)

            LOADS = 32 if TP else 16
            XLOADS = 32 if NREST else 16

            @block.scalar
            def _(act):
                act.wait_ge(i_x, XLOADS)
                act.dma_start(table_v, xc[:, :, :]).then_inc(i_tab, 16)
                act.wait_ge(i_tab, 16)

            @block.gpsimd
            def _(pool):
                nc.gpsimd.iota(iota_i[:, :], [[1, WIN]], 0, 0).then_inc(i_iota, 1)
                nc.gpsimd.iota(row_i[:, :], [[0, 1]], 0, 1).then_inc(i_iota, 1)

            @block.vector
            def _(dve):
                nc.vector.memset(src_i[:, GFULL:NG + SLOTS, :], 0).then_inc(i_zero, 1)
                nc.vector.memset(dst_i[:, GFULL:NG + 1, :], -1).then_inc(i_zero, 1)
                nc.vector.memset(wgt[:, GFULL:NG + 1, :], 0.0).then_inc(i_zero, 1)
                nc.vector.memset(xc[:, NB - 1, :], 0.0).then_inc(i_zero, 1)
                n = [0]

                def link(ins):
                    n[0] += 1
                    ins.then_inc(i_step, 1)
                    dve.wait_ge(i_step, n[0])

                link(nc.vector.memset(chk[:, :], 0.0))
                dve.wait_ge(i_iota, 2)
                link(nc.vector.tensor_copy(iota[:, :], iota_i[:, :]))
                link(nc.vector.tensor_copy(iota_ps[:, :], iota_i[:, :]))
                link(nc.vector.tensor_copy(row[:, :], row_i[:, :]))
                link(nc.vector.tensor_scalar(ident[:, :], iota[:, 0:P], row[:, 0:1], None, ALU.is_equal))
                dve.wait_ge(i_dst, LOADS)
                link(nc.vector.tensor_scalar(first_i[0:1, :], dst_i[0:1, :, 0], -P, None, ALU.bitwise_and))
                link(nc.vector.tensor_scalar(first_f[0:1, :], first_i[0:1, :], 0.0, None, ALU.max))
                nc.vector.memset(ones[:, :], 1.0).then_inc(i_const, 1)
                dve.wait_ge(i_sum, 1)
                link(nc.vector.tensor_copy(base0[:, :], ps[1][:, 0, 0:NG + 1]))
                link(nc.vector.tensor_copy(dst_f[:, :, :], dst_i))
                off = work[:, 0:(NG + 1) * TILES].rearrange("p (g k) -> p g k", k=TILES)
                link(nc.vector.tensor_tensor(off, dst_f[:, :, :], base0[:, :].unsqueeze(2).broadcast_to([P, NG + 1, TILES]), ALU.subtract))
                if GFULL:
                    full = off[:, 0:GFULL, :].rearrange("p g k -> p (g k)")
                    link(nc.vector.tensor_reduce(chk[:, 0:1], full, AX, ALU.max))
                    link(nc.vector.tensor_reduce(chk[:, 1:2], full, AX, ALU.min))
                if TP:
                    link(nc.vector.tensor_reduce(chk[0:TP, 2:3], off[0:TP, GFULL, :], AX, ALU.max))
                    link(nc.vector.tensor_reduce(chk[0:TP, 3:4], off[0:TP, GFULL, :], AX, ALU.min))
                link(nc.vector.tensor_tensor(chk[:, 4:5], chk[:, 0:1], chk[:, 2:3], ALU.max))
                link(nc.vector.tensor_tensor(chk[:, 5:6], chk[:, 1:2], chk[:, 3:4], ALU.min))
                link(nc.vector.tensor_scalar(chk[:, 4:5], chk[:, 4:5], float(WIN) - 0.5, None, ALU.is_gt))
                link(nc.vector.tensor_scalar(chk[:, 5:6], chk[:, 5:6], -0.5, None, ALU.is_lt))
                link(nc.vector.tensor_reduce(chk[:, 7:8], dst_f[:, 0:DG, :].rearrange("p g k -> p (g k)"), AX, ALU.max))
                link(nc.vector.tensor_scalar(chk[:, 7:8], chk[:, 7:8], float(SUPS * SUP) - 0.5, None, ALU.is_gt))
                nc.vector.tensor_tensor(chk[:, 6:7], chk[:, 4:5], chk[:, 5:6], ALU.add).then_inc(i_chk, 1)
                dve.wait_ge(i_sum, 2)
                link(nc.vector.tensor_scalar(near[:, :], ps[0][:, 0, 0:1], 0.5, None, ALU.is_lt))
                link(nc.vector.tensor_scalar(chk[0:1, 7:8], near[0:1, 0:1], float(1 - WINDOWS), float(WINDOWS), ALU.mult, ALU.add))
                link(nc.vector.tensor_copy(sweeps_i[:, 0:1], chk[0:1, 7:8]))
                link(nc.vector.tensor_scalar(chk[0:1, 6:7], ps[0][0:1, 0, 1:2], 0.5, None, ALU.is_lt))
                link(nc.vector.tensor_tensor(sweeps_i[:, 1:2], chk[0:1, 6:7], near[0:1, 0:1], ALU.mult))
                link(nc.vector.tensor_scalar(base0[:, :], base0[:, :], near[:, 0:1], None, ALU.mult))
                dve.wait_ge(i_wgt, LOADS)
                link(nc.vector.tensor_scalar(wgt[:, :, :], wgt[:, :, :], 1.0 - ALPHA, None, ALU.mult))
                dve.wait_ge(i_x, XLOADS)
                link(nc.vector.tensor_scalar(f01[:, :, :], xc[:, :, :], ALPHA, None, ALU.mult))
                dve.wait_ge(i_src, LOADS)
                lo_i = acc[:, 0:(NG + 1) * TILES].bitcast(I32).rearrange("p (g k) -> p g k", k=TILES)
                link(nc.vector.tensor_scalar(lo_i, src_i[:, 0:NG + 1, :], P - 1, None, ALU.bitwise_and))
                link(nc.vector.tensor_copy(src_lo[:, :, :], lo_i))
                link(nc.vector.memset(src_hi[:, GFULL:NG + 1, :], -1.0))
                for g, p in ((slice(0, GFULL), P), (slice(GFULL, GFULL + 1), TP)):
                    if p and (g.stop > g.start):
                        link(nc.vector.tensor_tensor(src_hi[0:p, g, :], src_i[0:p, g, :], src_lo[0:p, g, :], ALU.subtract))
                        link(nc.vector.tensor_scalar(src_hi[0:p, g, :], src_hi[0:p, g, :], 1.0 / P, None, ALU.mult))
                shape = [P, DG, TILES]
                a_i = work[:, 0:DG * TILES].bitcast(I32).rearrange("p (g k) -> p g k", k=TILES)
                a_f = work[:, 1024:1024 + DG * TILES].rearrange("p (g k) -> p g k", k=TILES)
                d_i = work[:, 2048:2048 + DG * TILES].bitcast(I32).rearrange("p (g k) -> p g k", k=TILES)
                link(nc.vector.tensor_copy(d_i, dst_f[:, 0:DG, :]))
                link(nc.vector.tensor_scalar(a_i, d_i, 9, None, ALU.arith_shift_right))
                link(nc.vector.tensor_copy(a_f, a_i))
                link(nc.vector.scalar_tensor_tensor(a_f, a_f, float(P), src_lo[:, 0:DG, :], ALU.mult, ALU.add))
                link(nc.vector.scalar_tensor_tensor(a_f, a_f, float(NB), src_hi[:, 0:DG, :], ALU.mult, ALU.add))
                link(nc.vector.tensor_copy(a_i, a_f))
                link(nc.vector.tensor_scalar(a_i, a_i, 9, None, ALU.logical_shift_left))
                link(nc.vector.tensor_scalar(d_i, d_i, SUP - 1, None, ALU.bitwise_and))
                link(nc.vector.tensor_tensor(addr[:, :, :], a_i, d_i, ALU.bitwise_or))
                link(nc.vector.tensor_scalar(past_i[:, :], row_i[:, :], DENSE, None, ALU.bitwise_or))
                link(nc.vector.tensor_tensor(before[:, :], iota[:, 0:P], row[:, 0:1].broadcast_to([P, P]), ALU.is_lt))
                link(nc.vector.tensor_scalar(valid[:, :], row[:, :], float(NREST or P) - 0.5, None, ALU.is_lt))

            @block.tensor
            def _(pe):
                pe.wait_ge(i_const, 1)
                nc.tensor.matmul(ps[1][:, 0, 0:NG + 1], ones[0:1, :], first_f[0:1, :], start=True, stop=True).then_inc(i_sum, 1)
                pe.wait_ge(i_chk, 1)
                nc.tensor.matmul(ps[0][:, 0, 0:2], ones[:, :], chk[:, 6:8], start=True, stop=True).then_inc(i_sum, 1)

        W1_s = sb("W1_s", [KE, H])
        W2_s = sb("W2_s", [H, H])
        W3_s = sb("W3_s", [H, D])
        L2_s = sb("L2_s", [D, D])
        L2_t = sb("L2_t", [D, D])
        L3_s = sb("L3_s", [D, D])
        b1_c = sb("b1_c", [H, 1])
        b2_r = sb("b2_r", [P, H])
        b3_r, l2b_r, l3b_r, gam_r, bet_r = (sb(n, [P, D]) for n in ("b3_r", "l2b_r", "l3b_r", "gam_r", "bet_r"))
        par, par_t = sem("params_in"), sem("params_t")
        with nc.Block() as block:
            @block.sync
            def _(sp):
                n = 0
                for to, frm in ((W1_s, W1), (W2_s, W2), (W3_s, W3), (L2_s, L2_W), (L3_s, L3_W)):
                    sp.dma_start(to[:, :], frm).then_inc(par, 16)
                    n += 16
                sp.dma_start(b1_c[:, :], b1.rearrange("(p a) -> p a", a=1)).then_inc(par, 16)
                n += 16
                for to, frm in ((b2_r, b2), (b3_r, b3), (l2b_r, L2_b), (l3b_r, L3_b), (gam_r, gamma), (bet_r, beta)):
                    sp.dma_start(to[:, :], frm.rearrange("(a f) -> a f", a=1).broadcast_to([P, frm.shape[0]])).then_inc(par, 16)
                    n += 16
                sp.wait_ge(par, n)

            @block.tensor
            def _(pe):
                pe.wait_ge(par, 16 * 12)
                nc.tensor.transpose(ps[2][0:D, 0, 0:D], L2_s[:, :], ident[0:D, 0:D]).then_inc(par_t, 1)

            @block.vector
            def _(dve):
                dve.wait_ge(par_t, 1)
                nc.vector.tensor_copy(L2_t[:, :], ps[2][0:D, 0, 0:D])

        sweeps = nc.values_load(sweeps_i[0:1, 0:1], min_val=1, max_val=WINDOWS)
        dense_ok = nc.values_load(sweeps_i[0:1, 1:2], min_val=0, max_val=1)

        chunk = [acc[:, (NB + 1) * D + r * CHB * SUP:(NB + 1) * D + (r + 1) * CHB * SUP] for r in range(2)] + [
            tmp_raw[:, r * CHB * SUP:(r + 1) * CHB * SUP] for r in range(2)]
        panel = tmp_raw[:, 2 * CHB * SUP:2 * CHB * SUP + SUP]
        fcur = xc

        def aggregate_block(weighted, with_dense=False, zero_fill=False):
            TG = 2 * GPS if with_dense else SLOTS
            first = DG if with_dense else 0
            turns = (NG - first) // TG
            idx_ready, hot_ready, gathered, summed, chunk_in, chunk_free = (slot_sems(f"agg_{n}") for n in (
                "idx", "onehot", "gathered", "summed", "chunk_in", "chunk_free"))
            step, window, taken, added, scaled, high, rest, middle, parts_ready, panel_done, panel_kept, panel_turned, panel_added, zeroed = (
                sem(f"agg_{n}") for n in ("step", "window", "slot_taken", "added", "scaled", "high", "rest", "middle", "parts",
                                          "panel_done", "panel_kept", "panel_turned", "panel_added", "zeroed"))
            nstep = 2 if weighted else 1

            with nc.Block() as block:
                def at(t, j):
                    return t * TG + j, j % SLOTS, t * (TG // SLOTS) + j // SLOTS

                def chunks_before(j):
                    return range(-(-j * CPS // GPS), -(-(j + 1) * CPS // GPS))

                if with_dense:
                    @block.sync
                    def _(sp):
                        with sp.Fori(0, turns) as t:
                            for c in range(2 * CPS):
                                r = c % RING
                                sp.wait_ge(chunk_free[r], t * (2 * CPS // RING) + (c // RING + 1))
                                sp.dma_start(chunk[r], dense_v[bass.ds(t * 2 + c // CPS, 1), :, c % CPS * CHB * SUP:(c % CPS + 1) * CHB * SUP]
                                             .rearrange("b p f -> p (b f)")).then_inc(chunk_in[r], 16)

                if zero_fill:
                    @block.sync
                    def _(sp):
                        sp.wait_ge(zeroed, 1)
                        n = 0
                        with sp.Fori(0, SUPS) as b:
                            for c in range(CPS):
                                sp.dma_start(dense_v[bass.ds(b, 1), :, c * CHB * SUP:(c + 1) * CHB * SUP]
                                             .rearrange("b p f -> p (b f)"), chunk[0]).then_inc(dense_zero, 16)
                        sp.dma_start(dense[DENSE:DENSE + P, :], chunk[0][:, 0:1]).then_inc(dense_zero, 16)
                        sp.wait_ge(dense_zero, 16 * (SUPS * CPS + 1))

                @block.scalar
                def _(act):
                    def set_indices(t, j):
                        l, u, n = at(t, j)
                        act.wait_ge(summed[u], n + 1)
                        nc.scalar.copy(idx[:, u, :], src_i[:, bass.ds(l + first, 1), :].rearrange("p a k -> p (a k)")).then_inc(idx_ready[u], 1)

                    for j in range(SLOTS - 1):
                        set_indices(0, j)
                    with act.Fori(0, turns) as t:
                        for j in range(TG):
                            set_indices(t, j + SLOTS - 1)
                            l, u, n = at(t, j)
                            if weighted:
                                act.wait_ge(scaled, l + 1)
                            else:
                                act.wait_ge(gathered[u], n * (16 * TILES) + 16 * TILES)
                            nc.scalar.copy(parts48[:, u, :, 0:D], msg[:, u, :, :]).then_inc(high, 1)
                            act.wait_ge(rest, l + 1)
                            nc.scalar.copy(parts48[:, u, :, D:2 * D], msg[:, u, :, :]).then_inc(middle, 1)
                            if with_dense and j % GPS == GPS - 1:
                                p = t * 2 + j // GPS
                                act.wait_ge(panel_done, p + 1)
                                act.wait_ge(panel_turned, p + 1)
                                nc.scalar.copy(panel[0:D, :], psD[0:D, :])
                                nc.scalar.copy(panel[HC2:HC2 + D, :], psD[HC2:HC2 + D, :]).then_inc(panel_kept, 1)

                @block.gpsimd
                def _(pool):
                    with pool.Fori(0, turns) as t:
                        for j in range(TG):
                            l, u, n = at(t, j)
                            pool.wait_ge(idx_ready[u], n + 1)
                            pool.wait_ge(summed[u], n + 1)
                            pool.sem_inc(taken, 1)
                            for k in range(TILES):
                                pool.indirect_dma_start(
                                    out=msg[:, u, k, :], out_offset=None, in_=table,
                                    in_offset=bass.IndirectOffsetOnAxis(ap=idx[:, u, k:k + 1], axis=0),
                                ).then_inc(gathered[u], 16)

                @block.vector
                def _(dve):
                    if zero_fill:
                        nc.vector.memset(chunk[0], 0.0).then_inc(zeroed, 1)
                    if with_dense:
                        nc.vector.memset(panel, 0.0).then_inc(zeroed, 1)
                    nc.vector.tensor_scalar(base[:, :], base0[:, :], sweep0[:, 0:1], None, ALU.add).then_inc(window, 1)
                    dve.wait_ge(window, 1)
                    nc.vector.tensor_scalar(base_blk[:, :], base[0:1, :], 1.0 / P, None, ALU.mult).then_inc(window, 1)
                    nc.vector.tensor_scalar(sweep0[:, :], sweep0[:, :], float(WIN), None, ALU.add).then_inc(window, 1)
                    dve.wait_ge(window, 3)

                    def make_onehots(t, j):
                        l, u, n = at(t, j)
                        g = l + first
                        dve.wait_ge(summed[u], n + 1)
                        nc.vector.tensor_scalar(dloc[:, u, :], dst_f[:, bass.ds(g, 1), :].rearrange("p a k -> p (a k)"),
                                                base[:, bass.ds(g, 1)], None, ALU.subtract).then_inc(step, 1)
                        if weighted:
                            nc.vector.tensor_copy(wl[:, u, :], wgt[:, bass.ds(g, 1), :].rearrange("p a k -> p (a k)")).then_inc(step, 1)
                        dve.wait_ge(step, (l + 1) * nstep)
                        for k in range(TILES):
                            m = nc.vector.tensor_scalar(onehot_b[:, u, k, :], iota_ps[:, :], dloc[:, u, k:k + 1], None, ALU.is_equal)
                        m.then_inc(hot_ready[u], 1)

                    def add_sums(t, j):
                        l, u, n = at(t, j)
                        blk = dve.value_load(base_blk[0:1, bass.ds(l + first, 1)], min_val=0, max_val=NB - 1)
                        here = acc[:, bass.ds(blk * D, 2 * D)].rearrange("p (a f) -> p a f", a=2)
                        dve.wait_ge(summed[u], n + 2)
                        for c in range(3):
                            dve.wait_ge(added, l * 3 + (c + START))
                            nc.vector.tensor_tensor(here, here, ps[u % 2][:, :, c * D:(c + 1) * D], ALU.add).then_inc(added, 1)

                    make_onehots(0, 0)
                    with dve.Fori(0, turns) as t:
                        for j in range(TG):
                            l, u, n = at(t, j)
                            make_onehots(t, j + 1)
                            if weighted:
                                dve.wait_ge(gathered[u], n * (16 * TILES) + 16 * TILES)
                                nc.vector.tensor_tensor(msg[:, u, :, :], msg[:, u, :, :], wl[:, u, :].unsqueeze(2).broadcast_to([P, TILES, D]),
                                                        ALU.mult).then_inc(scaled, 1)
                            if j:
                                add_sums(t, j - 1)
                            dve.wait_ge(high, l + 1)
                            nc.vector.tensor_tensor(msg[:, u, :, :], msg[:, u, :, :], parts48[:, u, :, 0:D], ALU.subtract).then_inc(rest, 1)
                            dve.wait_ge(middle, l + 1)
                            nc.vector.tensor_tensor(parts48[:, u, :, 2 * D:3 * D], msg[:, u, :, :], parts48[:, u, :, D:2 * D],
                                                    ALU.subtract).then_inc(parts_ready, 1)
                            if j == TG - 1:
                                add_sums(t, j)
                            if with_dense and j % GPS == GPS - 1:
                                p = t * 2 + j // GPS
                                there = acc[:, bass.ds(p * (SUP // P * D), SUP // P * D)].rearrange("p (a f) -> p a f", f=D)
                                turned = psDT[:, 0:SUP // P * (HC2 + D)].rearrange("p (a f) -> p a f", f=HC2 + D)
                                dve.wait_ge(panel_turned, p + 2)
                                dve.wait_ge(added, (l + (1 if j == TG - 1 else 0)) * 3 + START)
                                for c in range(2):
                                    dve.wait_ge(panel_added, p * 2 + (c + 1))
                                    nc.vector.tensor_tensor(there, there, turned[:, :, c * HC2:c * HC2 + D], ALU.add).then_inc(panel_added, 1)
                                dve.wait_ge(panel_added, p * 2 + 3)

                @block.tensor
                def _(pe):
                    pe.sem_inc(added, START)
                    for u in range(SLOTS):
                        pe.sem_inc(summed[u], 1)
                    if with_dense:
                        pe.wait_ge(zeroed, 1)
                        pe.sem_inc(panel_turned, 1)
                        pe.sem_inc(panel_added, 1)
                        pe.sem_inc(panel_kept, 1)
                        for r in range(RING):
                            pe.sem_inc(chunk_free[r], 1)
                    with pe.Fori(0, turns) as t:
                        for j in range(TG):
                            l, u, n = at(t, j)
                            if with_dense:
                                p = t * 2 + j // GPS
                                for c in chunks_before(j % GPS):
                                    cc = j // GPS * CPS + c
                                    r = cc % RING
                                    if c == 0:
                                        pe.wait_ge(panel_kept, p + 1)
                                    pe.wait_ge(chunk_in[r], t * (2 * CPS // RING * 16) + (cc // RING + 1) * 16)
                                    for i in range(CHB):
                                        sblk = c * CHB + i
                                        o = HC2 * (sblk % 2)
                                        m = nc.tensor.matmul(psD[o:o + D, :], fcur[:, sblk, :], chunk[r][:, i * SUP:(i + 1) * SUP],
                                                             start=sblk < 2, stop=sblk >= NB - 2, skip_group_check=True)
                                    m.then_inc(chunk_free[r], 1)
                                    if c == CPS - 1:
                                        pe.wait_ge(chunk_free[r], t * (2 * CPS // RING) + (cc // RING + 2))
                                        pe.sem_inc(panel_done, 1)
                            pe.wait_ge(hot_ready[u], n + 1)
                            pe.wait_ge(parts_ready, l + 1)
                            pe.wait_ge(added, l * 3 + (START - 3))
                            for k in range(TILES):
                                for h in range(2):
                                    m = nc.tensor.matmul(ps[u % 2][:, h, 0:3 * D], onehot_b[:, u, k, h * P:(h + 1) * P], parts48[:, u, k, :],
                                                         start=k == 0, stop=k == TILES - 1)
                            m.then_inc(summed[u], 1)
                            if with_dense and j % GPS == GPS - 1:
                                pe.wait_ge(panel_kept, p + 2)
                                pe.wait_ge(panel_added, p * 2 + 1)
                                for b in range(SUP // P):
                                    m = nc.tensor.transpose(psDT[:, b * (HC2 + D):(b + 1) * (HC2 + D)], panel[0:HC2 + D, b * P:(b + 1) * P],
                                                            ident[0:HC2 + D, 0:HC2 + D])
                                m.then_inc(panel_turned, 1)
            clear([*idx_ready, *hot_ready, *summed, *chunk_in, *chunk_free, step, window, taken, added, scaled, high, rest, middle,
                   parts_ready, panel_done, panel_kept, panel_turned, panel_added, zeroed], gathered)

        def aggregate(weighted):
            with nc.Fori(0, sweeps):
                aggregate_block(weighted)

        accD = acc[:, 0:NB * D].rearrange("p (b f) -> p b f", f=D)
        dense_zero, kept_acc, hop_store = sem("dense_zero"), sem("hop_kept"), sem("hop_store")

        def start_hop():
            with nc.Block() as block:
                @block.vector
                def _(dve):
                    nc.vector.memset(sweep0[:, :], 0.0)
                    nc.vector.memset(acc[:, NB * D:(NB + 1) * D], 0.0)
                    nc.vector.tensor_copy(accD, f01)

        def end_hop():
            with nc.Block() as block:
                @block.vector
                def _(dve):
                    nc.vector.memset(sweep0[:, :], 0.0)
                    nc.vector.tensor_copy(fcur[:, 0:NB // 2, :], accD[:, 0:NB // 2, :]).then_inc(kept_acc, 1)
                    dve.wait_ge(kept_acc, 2)
                    nc.vector.tensor_copy(accD[:, 0:NB // 2, :], f01[:, 0:NB // 2, :])
                    nc.vector.memset(acc[:, NB * D:(NB + 1) * D], 0.0)

                @block.scalar
                def _(act):
                    nc.scalar.copy(fcur[:, NB // 2:NB, :], accD[:, NB // 2:NB, :]).then_inc(kept_acc, 1)
                    act.wait_ge(kept_acc, 2)
                    nc.scalar.copy(accD[:, NB // 2:NB, :], f01[:, NB // 2:NB, :])

                @block.sync
                def _(sp):
                    sp.wait_ge(kept_acc, 2)
                    sp.dma_start(table_v, fcur[:, :, :]).then_inc(hop_store, 16)
                    sp.wait_ge(hop_store, 16)
            clear([kept_acc, hop_store])

        start_hop()
        with nc.If(dense_ok == 1):
            aggregate_block(True, zero_fill=True)
            end_hop()

            cols_set, diag_set, spread, found, looked, chosen, scattered_all = (sem(f"build_{n}") for n in (
                "cols", "diag", "spread", "found", "looked", "chosen", "carried"))
            carried_g, found_all = sem("build_slot_free"), sem("build_found_all")
            scattered = sem("build_scattered")
            diag = parts48[:, :, :, :].rearrange("p u k f -> p (u k f)").bitcast(F32)[:, 0:2 * 3 * P].rearrange("p (v a e) -> p v a e", v=2, a=3)
            same = msg[:, :, :, :].rearrange("p u k f -> p (u k f)")[:, 0:4 * P].rearrange("p (a e) -> p a e", a=4)
            cols = sb("cols", [P, 2, 3, TILES])
            wsum = sb("wsum", [P, 2, TILES])
            dup = sb("dup", [P, 2, TILES])
            dup_i = sb("dup_i", [P, 2, TILES], I32)
            place = sb("place", [P, 2, TILES], I32)
            with nc.Block() as block:
                @block.scalar
                def _(act):
                    with act.Fori(0, DG // 2) as t:
                        for v in range(2):
                            g = t * 2 + v
                            act.wait_ge(cols_set, g + 1)
                            for k in range(TILES):
                                act.wait_ge(spread, g * TILES + (k + 1))
                                for a in range(3):
                                    m = nc.scalar.activation(diag[:, k % 2, a, :], ident[:, :], ACT.Copy, scale=cols[:, v, a, k:k + 1])
                                m.then_inc(diag_set, 1)

                @block.tensor
                def _(pe):
                    pe.sem_inc(spread, 2)
                    pe.sem_inc(looked, 2)
                    with pe.Fori(0, DG // 2) as t:
                        for v in range(2):
                            g = t * 2 + v
                            for k in range(TILES):
                                pe.wait_ge(diag_set, g * TILES + (k + 1))
                                pe.wait_ge(looked, g * TILES + (k + 1))
                                nc.tensor.matmul(ps[k % 2][:, 0, 0:3 * P], ones[:, :], diag[:, k % 2, :, :].rearrange("p a e -> p (a e)"),
                                                 start=True, stop=True).then_inc(spread, 1)

                @block.vector
                def _(dve):
                    dve.sem_inc(chosen, 1)
                    with dve.Fori(0, DG // 2) as t:
                        for v in range(2):
                            g = t * 2 + v
                            dve.wait_ge(spread, g * TILES + 1)
                            for a, arr in ((1, dst_f), (2, wgt)):
                                nc.vector.tensor_copy(cols[:, v, a, :], arr[:, bass.ds(g, 1), :].rearrange("p a k -> p (a k)"))
                            nc.vector.tensor_copy(cols[:, v, 0, :], src_i[:, bass.ds(g, 1), :].rearrange("p a k -> p (a k)")).then_inc(cols_set, 1)
                            dve.wait_ge(carried_g, g + 1)
                            for k in range(TILES):
                                n = g * TILES + k
                                dve.wait_ge(spread, n + 3)
                                rows3 = ps[k % 2][:, 0, :]
                                nc.vector.tensor_scalar(same[:, 0, :], rows3[:, 0:P], cols[:, v, 0, k:k + 1], None, ALU.is_equal).then_inc(found, 1)
                                dve.wait_ge(found, n * 3 + 1)
                                nc.vector.scalar_tensor_tensor(same[:, 1, :], rows3[:, P:2 * P], cols[:, v, 1, k:k + 1], same[:, 0, :],
                                                               ALU.is_equal, ALU.mult).then_inc(found, 1)
                                dve.wait_ge(found, n * 3 + 2)
                                nc.vector.tensor_tensor_reduce(out=same[:, 2, :], in0=rows3[:, 2 * P:3 * P], in1=same[:, 1, :], scale=1.0, scalar=0.0,
                                                               op0=ALU.mult, op1=ALU.add, accum_out=wsum[:, v, k:k + 1]).then_inc(looked, 1)
                                nc.vector.tensor_tensor_reduce(out=same[:, 3, :], in0=before[:, :], in1=same[:, 1, :], scale=1.0, scalar=0.0,
                                                               op0=ALU.mult, op1=ALU.add, accum_out=dup[:, v, k:k + 1]).then_inc(found, 1)
                                dve.wait_ge(looked, n + 3)
                                dve.wait_ge(found, n * 3 + 3)
                            nc.vector.tensor_scalar(dup_i[:, v, :], dup[:, v, :], 0.5, None, ALU.is_gt).then_inc(chosen, 1)
                            nc.vector.tensor_copy(place[:, v, :], addr[:, bass.ds(g, 1), :].rearrange("p a k -> p (a k)")).then_inc(chosen, 1)
                            dve.wait_ge(chosen, g * 3 + 3)
                            dve.sem_inc(found_all, 1)
                            nc.vector.copy_predicated(place[:, v, :], dup_i[:, v, :], past_i[:, 0:1].broadcast_to([P, TILES])).then_inc(chosen, 1)

                @block.gpsimd
                def _(pool):
                    pool.sem_inc(carried_g, 2)
                    with pool.Fori(0, DG // 2) as t:
                        for v in range(2):
                            g = t * 2 + v
                            pool.wait_ge(chosen, g * 3 + 4)
                            for k in range(TILES):
                                pool.sem_inc(scattered_all, 1)
                                pool.indirect_dma_start(
                                    out=dense, out_offset=bass.IndirectOffsetOnAxis(ap=place[:, v, k:k + 1], axis=0),
                                    in_=wsum[:, v, k:k + 1], in_offset=None, compute_op=ALU.add).then_inc(scattered, 16)
                                pool.wait_ge(scattered, g * (16 * TILES) + (k + 1) * 16)
                            pool.sem_inc(carried_g, 1)
            clear([cols_set, diag_set, spread, found, looked, chosen, scattered_all, carried_g, found_all], [scattered])

            with nc.Fori(0, HOPS - 1):
                aggregate_block(True, with_dense=True)
                end_hop()
        with nc.Else():
            with nc.Fori(0, HOPS):
                aggregate(True)
                end_hop()

        x_back, x_again = sem("x_back"), sem("x_again")
        with nc.Block() as block:
            @block.vector
            def _(dve):
                dve.wait_ge(x_back, 1)
                nc.vector.memset(xc[:, NB - 1, :], 0.0).then_inc(x_back, 1)

            @block.scalar
            def _(act):
                nc.scalar.copy(accD, fcur[:, :, :]).then_inc(x_back, 1)

            @block.sync
            def _(sp):
                sp.wait_ge(x_back, 2)
                load_nodes(sp, xc, x, x_again)
                sp.wait_ge(x_again, 32 if NREST else 16)

        s1 = sb("ln_sum", [P, NB])
        s2 = sb("ln_var", [P, NB])

        def layernorm(y, to):
            step, sq, rt = sem("ln_step"), sem("ln_squared"), sem("ln_root")
            with nc.Block() as block:
                @block.vector
                def _(dve):
                    n = [0]

                    def link(ins):
                        n[0] += 1
                        ins.then_inc(step, 1)
                        dve.wait_ge(step, n[0])

                    wide = [P, NB, D]
                    link(nc.vector.tensor_tensor(to, xc[:, :, :], y, ALU.add))
                    link(nc.vector.tensor_reduce(s1[:, :], to, AX, ALU.add))
                    link(nc.vector.tensor_scalar(s1[:, :], s1[:, :], 1.0 / D, None, ALU.mult))
                    link(nc.vector.tensor_tensor(to, to, s1[:, :].unsqueeze(2).broadcast_to(wide), ALU.subtract))
                    dve.wait_ge(sq, 1)
                    link(nc.vector.tensor_reduce(s2[:, :], tmp[:, :, :], AX, ALU.add))
                    link(nc.vector.tensor_scalar(s2[:, :], s2[:, :], 1.0 / D, EPS, ALU.mult, ALU.add))
                    dve.wait_ge(rt, 1)
                    link(nc.vector.reciprocal(s2[:, :], s1[:, :]))
                    link(nc.vector.tensor_tensor(to, to, s2[:, :].unsqueeze(2).broadcast_to(wide), ALU.mult))

                @block.scalar
                def _(act):
                    act.wait_ge(step, 4)
                    nc.scalar.activation(tmp[:, :, :], to, ACT.Square).then_inc(sq, 1)
                    act.wait_ge(step, 6)
                    nc.scalar.activation(s1[:, :], s2[:, :], ACT.Sqrt).then_inc(rt, 1)
            clear([step, sq, rt])

        layernorm(accD, xc[:, :, :])

        def store_table(frm):
            s = sem("table_stored_again")
            with nc.Block() as block:
                @block.sync
                def _(sp):
                    sp.dma_start(table_v, frm).then_inc(s, 16)
                    sp.wait_ge(s, 16)
            clear([s])

        store_table(xc[:, :, :])

        HQ = HALF * P
        rows = f01_raw[:, 0:SLOTS * TILES * KE].rearrange("p (u k f) -> p u k f", u=SLOTS, k=TILES)
        attr = f01_raw[:, SLOTS * TILES * KE:SLOTS * TILES * (KE + DE)].rearrange("p (u k f) -> p u k f", u=SLOTS, k=TILES)
        rowsT = tmp_raw[:, 0:2 * HQ].rearrange("p (q e) -> p q e", q=2)
        h1T = tmp_raw[:, 2 * HQ:4 * HQ].rearrange("p (q e) -> p q e", q=2)
        h2pre = tmp_raw[:, 4 * HQ:5 * HQ].rearrange("p (k f) -> p k f", k=HALF)
        h2 = tmp_raw[:, 5 * HQ:6 * HQ].rearrange("p (k f) -> p k f", k=HALF)
        PARTS = 3 * H + 1
        parts = tmp_raw[:, 6 * HQ:6 * HQ + HALF * PARTS].bitcast(BF16).rearrange("p (q k f) -> p q k f", q=2, k=HALF)
        hotsrc = tmp_raw[:, 6 * HQ + HALF * PARTS:6 * HQ + HALF * PARTS + 2 * P].bitcast(BF16).rearrange("p (u a e) -> p u a e", u=2, a=2)

        gathered, attr_in, idx_ready, group_free = (slot_sems(f"l1_{n}") for n in ("gathered", "attr", "idx", "free"))
        (transposed, rowsT_ready, lin1, h1T_ready, lin2, h2pre_ready, h2_ready, rest_ready, mid_ready, parts_ready,
         hot_ready, summed_q, added, step, window, taken, attr_placed, cnt_hot, cnt_sum, cnt_added) = (
            sem(f"l1_{n}") for n in ("transposed", "rowsT", "lin1", "h1T", "lin2", "h2pre", "h2", "rest", "mid", "parts",
                                     "onehot", "summed", "added", "step", "window", "slot_taken", "attr_placed",
                                     "cnt_hot", "cnt_sum", "cnt_added"))
        QB = 2 * SLOTS
        NT = NG // SLOTS
        with nc.Block() as block:
            @block.vector
            def _(dve):
                nc.vector.memset(sweep0[:, :], 0.0)
                nc.vector.memset(acc[:, :], 0.0)
                nc.vector.memset(f01_raw[:, :], 0.0)

        with nc.Fori(0, sweeps):
            with nc.Block() as block:
                @block.sync
                def _(sp):
                    def load(g, u, p):
                        sp.dma_start(attr[0:p, u, :, :].rearrange("p k f -> p (k f)"),
                                     edge_attr[bass.ds(g * GROUP, p * TILES), :].rearrange("(p k) f -> p (k f)", k=TILES)).then_inc(attr_in[u], 16)

                    with sp.Fori(0, NT - 1) as t:
                        for u in range(SLOTS):
                            sp.wait_ge(attr_placed, t * SLOTS + (u + 1))
                            load(t * SLOTS + u, u, P)
                    for u in range(SLOTS):
                        g = (NT - 1) * SLOTS + u
                        sp.wait_ge(attr_placed, g + 1)
                        if g < GFULL:
                            load(g, u, P)
                        elif g == GFULL and TP:
                            load(g, u, TP)
                        else:
                            load(0, u, P if GFULL else TP)

                @block.gpsimd
                def _(pool):
                    with pool.Fori(0, NT) as t:
                        for u in range(SLOTS):
                            pool.wait_ge(idx_ready[u], t + 1)
                            pool.wait_ge(group_free[u], t + 1)
                            pool.sem_inc(taken, 1)
                            for k in range(TILES):
                                for c, i in ((0, idx), (D, idd)):
                                    pool.indirect_dma_start(
                                        out=rows[:, u, k, c:c + D], out_offset=None, in_=table,
                                        in_offset=bass.IndirectOffsetOnAxis(ap=i[:, u, k:k + 1], axis=0),
                                    ).then_inc(gathered[u], 16)

                @block.scalar
                def _(act):
                    act.sem_inc(rowsT_ready, START)
                    act.sem_inc(h1T_ready, START)
                    act.sem_inc(h2_ready, START)
                    act.sem_inc(mid_ready, START)

                    with act.Fori(0, NT) as t:
                        for u in range(SLOTS):
                            g = t * SLOTS + u
                            act.wait_ge(group_free[u], t + 1)
                            nc.scalar.activation(idd[:, u, :], dst_f[:, bass.ds(g, 1), :].rearrange("p a k -> p (a k)"), ACT.Relu)
                            nc.scalar.copy(idx[:, u, :], src_i[:, bass.ds(g, 1), :].rearrange("p a k -> p (a k)"))
                            act.drain().then_inc(idx_ready[u], 1)
                        for i in range(QB + 3):
                            if i < QB:
                                q = t * QB + i
                                act.wait_ge(transposed, q + START + 1)
                                act.wait_ge(lin1, q + START - 1)
                                nc.scalar.copy(rowsT[0:KE, i % 2, :], psT[0:KE, :]).then_inc(rowsT_ready, 1)
                            if 1 <= i <= QB:
                                q, j = t * QB + i - 1, (i - 1) % 2
                                act.wait_ge(lin1, q + START + 1)
                                act.wait_ge(lin2, q + START - 1)
                                nc.scalar.activation(h1T[:, j, :], ps1[:, :], ACT.Relu, bias=b1_c[:, 0:1]).then_inc(h1T_ready, 1)
                            if 2 <= i <= QB + 1:
                                q, j = t * QB + i - 2, i % 2
                                act.wait_ge(h2pre_ready, q + START + 1)
                                act.wait_ge(parts_ready, q + START)
                                act.wait_ge(summed_q, q + START - 1)
                                nc.scalar.activation(h2[:, :, :], h2pre, ACT.Relu)
                                nc.scalar.activation(parts[:, j, :, 0:H], h2pre, ACT.Relu).then_inc(h2_ready, 1)
                                act.wait_ge(rest_ready, q + START + 1)
                                nc.scalar.copy(parts[:, j, :, H:2 * H], h2[:, :, :]).then_inc(mid_ready, 1)

                @block.vector
                def _(dve):
                    dve.sem_inc(h2pre_ready, START)
                    dve.sem_inc(rest_ready, START)
                    dve.sem_inc(parts_ready, START)
                    dve.sem_inc(added, START)
                    dve.sem_inc(attr_placed, SLOTS)
                    dve.sem_inc(cnt_hot, START)
                    dve.sem_inc(cnt_added, START)
                    nc.vector.tensor_scalar(base[:, :], base0[:, :], sweep0[:, 0:1], None, ALU.add).then_inc(window, 1)
                    dve.wait_ge(window, 1)
                    nc.vector.tensor_scalar(base_blk[:, :], base[0:1, :], 1.0 / P, None, ALU.mult).then_inc(window, 1)
                    nc.vector.tensor_scalar(sweep0[:, :], sweep0[:, :], float(WIN), None, ALU.add).then_inc(window, 1)
                    nc.vector.memset(outdeg[:, :], 0.0).then_inc(window, 1)
                    nc.vector.memset(parts[:, :, :, 3 * H:3 * H + 1], 1.0).then_inc(window, 1)
                    dve.wait_ge(window, 5)

                    with dve.Fori(0, NT) as t:
                        for i in range(QB + 4):
                            if i < QB and i % 2 == 0:
                                u = i // 2
                                g = t * SLOTS + u
                                dve.wait_ge(attr_in[u], t * 16 + 16)
                                dve.wait_ge(group_free[u], t + 1)
                                nc.vector.tensor_copy(rows[:, u, :, 2 * D:KE], attr[:, u, :, :]).then_inc(attr_placed, 1)
                                nc.vector.tensor_scalar(dloc[:, u, :], dst_f[:, bass.ds(g, 1), :].rearrange("p a k -> p (a k)"),
                                                        base[:, bass.ds(g, 1)], None, ALU.subtract).then_inc(step, 1)
                                nc.vector.tensor_copy(lol[:, u, :], src_lo[:, bass.ds(g, 1), :].rearrange("p a k -> p (a k)")).then_inc(step, 1)
                                nc.vector.tensor_copy(hil[:, u, :], src_hi[:, bass.ds(g, 1), :].rearrange("p a k -> p (a k)")).then_inc(step, 1)
                                dve.wait_ge(step, g * 3 + 3)
                                for k in range(TILES):
                                    m = nc.vector.tensor_scalar(onehot_b[:, u, k, :], iota_ps[:, :], dloc[:, u, k:k + 1], None, ALU.is_equal)
                                m.then_inc(hot_ready, 1)
                                for k in range(TILES):
                                    dve.wait_ge(cnt_sum, g * TILES + (k + START - 1))
                                    nc.vector.tensor_scalar(hotsrc[:, k % 2, 0, :], iota_ps[:, 0:P], lol[:, u, k:k + 1], None, ALU.is_equal)
                                    nc.vector.tensor_scalar(hotsrc[:, k % 2, 1, :], iota_ps[:, 0:P], hil[:, u, k:k + 1], None, ALU.is_equal).then_inc(cnt_hot, 1)
                                dve.wait_ge(cnt_sum, g * TILES + (TILES + START))
                                dve.wait_ge(cnt_added, g + START)
                                nc.vector.tensor_tensor(outdeg[:, :], outdeg[:, :], cnt_ps[:, 0:NB], ALU.add).then_inc(cnt_added, 1)
                            if 2 <= i <= QB + 1:
                                q, j = t * QB + i - 2, i % 2
                                dve.wait_ge(lin2, q + START + 1)
                                dve.wait_ge(h2_ready, q + START)
                                nc.vector.tensor_tensor(h2pre, ps2.rearrange("p (k f) -> p k f", k=HALF),
                                                        b2_r[:, :].unsqueeze(1).broadcast_to([P, HALF, H]), ALU.add).then_inc(h2pre_ready, 1)
                                dve.wait_ge(h2_ready, q + START + 1)
                                nc.vector.tensor_tensor(h2, h2, parts[:, j, :, 0:H], ALU.subtract).then_inc(rest_ready, 1)
                                dve.wait_ge(mid_ready, q + START + 1)
                                nc.vector.tensor_tensor(parts[:, j, :, 2 * H:3 * H], h2, parts[:, j, :, H:2 * H], ALU.subtract).then_inc(parts_ready, 1)
                            if i >= 4 and i % 2 == 0:
                                u = (i - 4) // 2
                                g = t * SLOTS + u
                                blk = dve.value_load(base_blk[0:1, bass.ds(g, 1)], min_val=0, max_val=NB - 1)
                                here = acc[:, bass.ds(blk * HC, 2 * HC)].rearrange("p (a f) -> p a f", a=2)
                                dve.wait_ge(summed_q, g * 2 + (START + 2))
                                for c, (lo, hi) in enumerate(((0, H), (H, 2 * H), (2 * H, 3 * H + 1))):
                                    dve.wait_ge(added, g * 3 + (c + START))
                                    o = HC - (hi - lo) if c == 2 else 0
                                    nc.vector.tensor_tensor(here[:, :, o:o + hi - lo], here[:, :, o:o + hi - lo], sums[:, :, lo:hi], ALU.add).then_inc(added, 1)

                @block.tensor
                def _(pe):
                    pe.sem_inc(transposed, START)
                    pe.sem_inc(lin1, START)
                    pe.sem_inc(lin2, START)
                    pe.sem_inc(summed_q, START)
                    pe.sem_inc(cnt_sum, START)
                    for u in range(SLOTS):
                        pe.sem_inc(group_free[u], 1)
                    with pe.Fori(0, NT) as t:
                        for i in range(QB + 3):
                            if i < QB:
                                q, u, k0 = t * QB + i, i // 2, HALF * (i % 2)
                                if i % 2 == 0:
                                    pe.wait_ge(gathered[u], t * (32 * TILES) + 32 * TILES)
                                    pe.wait_ge(attr_placed, t * SLOTS + (u + SLOTS + 1))
                                pe.wait_ge(rowsT_ready, q + START)
                                for k in range(HALF):
                                    m = nc.tensor.transpose(psT[0:KE, k * P:(k + 1) * P], rows[:, u, k0 + k, :], ident[:, :])
                                m.then_inc(transposed, 1)
                                if i % 2 == 1:
                                    pe.wait_ge(transposed, q + START + 1)
                                    pe.sem_inc(group_free[u], 1)
                            if 1 <= i <= QB:
                                q, j = t * QB + i - 1, (i - 1) % 2
                                pe.wait_ge(rowsT_ready, q + START + 1)
                                pe.wait_ge(h1T_ready, q + START)
                                nc.tensor.matmul(ps1[:, :], W1_s[:, :], rowsT[0:KE, j, :], start=True, stop=True).then_inc(lin1, 1)
                            if 2 <= i <= QB + 1:
                                q, j = t * QB + i - 2, i % 2
                                pe.wait_ge(h1T_ready, q + START + 1)
                                pe.wait_ge(h2pre_ready, q + START)
                                for k in range(HALF):
                                    m = nc.tensor.matmul(ps2[:, k * H:(k + 1) * H], h1T[:, j, k * P:(k + 1) * P], W2_s[:, :], start=True, stop=True)
                                m.then_inc(lin2, 1)
                            if 3 <= i <= QB + 2:
                                q, u, j, k0 = t * QB + i - 3, (i - 3) // 2, (i - 3) % 2, HALF * ((i - 3) % 2)
                                if j == 0:
                                    g = t * SLOTS + u
                                    pe.wait_ge(hot_ready, g + 1)
                                    pe.wait_ge(added, g * 3 + START)
                                pe.wait_ge(parts_ready, q + START + 1)
                                for k in range(HALF):
                                    for h in range(2):
                                        m = nc.tensor.matmul(sums[:, h, 0:PARTS], onehot_b[:, u, k0 + k, h * P:(h + 1) * P], parts[:, j, k, :],
                                                             start=k0 + k == 0, stop=k0 + k == TILES - 1)
                                m.then_inc(summed_q, 1)
                            if i < QB and i % 2 == 0:
                                u = i // 2
                                g = t * SLOTS + u
                                pe.wait_ge(cnt_added, g + START)
                                for k in range(TILES):
                                    pe.wait_ge(cnt_hot, g * TILES + (k + START + 1))
                                    nc.tensor.matmul(cnt_ps[:, 0:NB], hotsrc[:, k % 2, 0, :], hotsrc[:, k % 2, 1, 0:NB],
                                                     start=k == 0, stop=k == TILES - 1).then_inc(cnt_sum, 1)
            clear([*attr_in, *idx_ready, *group_free, transposed, rowsT_ready, lin1, h1T_ready, lin2, h2pre_ready, h2_ready,
                   rest_ready, mid_ready, parts_ready, hot_ready, summed_q, added, step, window, taken, attr_placed,
                   cnt_hot, cnt_sum, cnt_added], gathered)


        CH = next(c for c in (7, 5, 4, 3, 2, 1) if NB % c == 0)

        def node_linear(width, frm, weight, to):
            stage = work[:, 0:CH * width].rearrange("p (c f) -> p c f", c=CH)
            stageT = work[0:width, 1024:1024 + CH * P]
            taken_pe = sem("linear_taken")
            staged, turned, kept, mapped, placed = (sem(f"linear_{n}") for n in ("staged", "turned", "kept", "mapped", "placed"))
            F = min(CH, 4)
            with nc.Block() as block:
                @block.vector
                def _(dve):
                    with dve.Fori(0, NB // CH) as c:
                        nc.vector.tensor_copy(stage, frm(c * CH, CH)).then_inc(staged, 1)
                        dve.wait_ge(mapped, c + 1)
                        nc.vector.tensor_copy(to(c * CH, CH), ps[0][:, 0, 0:CH * D].rearrange("p (c f) -> p c f", c=CH)).then_inc(placed, 1)

                @block.tensor
                def _(pe):
                    pe.sem_inc(placed, 1)
                    with pe.Fori(0, NB // CH) as c:
                        pe.wait_ge(staged, c + 1)
                        pe.sem_inc(taken_pe, 1)
                        for b in range(CH):
                            m = nc.tensor.transpose(ps[1][0:width, b // 4, b % 4 * P:(b % 4 + 1) * P], stage[:, b, :], ident[:, :])
                        m.then_inc(turned, 1)
                        pe.wait_ge(kept, c + 1)
                        pe.wait_ge(placed, c + 1)
                        for b in range(CH):
                            m = nc.tensor.matmul(ps[0][:, 0, b * D:(b + 1) * D], stageT[:, b * P:(b + 1) * P], weight[:, :], start=True, stop=True)
                        m.then_inc(mapped, 1)

                @block.scalar
                def _(act):
                    with act.Fori(0, NB // CH) as c:
                        act.wait_ge(turned, c + 1)
                        m = nc.scalar.copy(stageT[:, 0:F * P], ps[1][0:width, 0, 0:F * P])
                        if CH > F:
                            m = nc.scalar.copy(stageT[:, F * P:CH * P], ps[1][0:width, 1, 0:(CH - F) * P])
                        m.then_inc(kept, 1)
            clear([staged, turned, kept, mapped, placed, taken_pe])

        wide = [P, NB, D]

        def steps(body):
            step, asked, rooted = sem("steps_step"), sem("steps_asked"), sem("steps_rooted")
            roots = []
            with nc.Block() as block:
                @block.vector
                def _(dve):
                    n = [0]

                    def link(ins):
                        n[0] += 1
                        ins.then_inc(step, 1)
                        dve.wait_ge(step, n[0])

                    def root(v):
                        roots.append((n[0], v))
                        dve.sem_inc(asked, 1)
                        dve.wait_ge(rooted, len(roots))
                        link(nc.vector.reciprocal(v, v))

                    body(link, root)

                @block.scalar
                def _(act):
                    for i, (at, v) in enumerate(roots):
                        act.wait_ge(asked, i + 1)
                        act.wait_ge(step, at)
                        nc.scalar.activation(v, v, ACT.Sqrt).then_inc(rooted, 1)
            clear([step, asked, rooted])

        acc1 = acc[:, 0:NB * HC].rearrange("p (b f) -> p b f", f=HC)
        c1 = sb("c1", [P, NB])
        c2 = sb("c2", [P, NB])
        steps(lambda link, root: link(nc.vector.tensor_copy(indeg[:, :], acc1[:, :, H])))
        node_linear(H, lambda b, n: acc1[:, bass.ds(b, n), 0:H], W3_s, lambda b, n: f01[:, bass.ds(b, n), :])

        def over(v):
            return v.unsqueeze(2).broadcast_to(wide)

        def along(v):
            return v.unsqueeze(1).broadcast_to(wide)

        def l1_out(link, root):
            link(nc.vector.tensor_tensor(tmp, over(indeg[:, :]), along(b3_r[:, :]), ALU.mult))
            link(nc.vector.tensor_tensor(f01, f01, tmp, ALU.add))
            link(nc.vector.tensor_scalar(c1[:, :], indeg[:, :], 1.0, None, ALU.max))
            link(nc.vector.reciprocal(c1[:, :], c1[:, :]))
            link(nc.vector.tensor_tensor(f01, f01, over(c1[:, :]), ALU.mult))
            link(nc.vector.tensor_tensor(f01, f01, xc[:, :, :], ALU.add))

        steps(l1_out)
        layernorm(f01, xc[:, :, :])

        def l2_in(link, root):
            link(nc.vector.tensor_scalar(c1[:, :], outdeg[:, :], 1.0, None, ALU.max))
            root(c1[:, :])
            link(nc.vector.tensor_tensor(tmp, xc[:, :, :], over(c1[:, :]), ALU.mult))
            link(nc.vector.memset(acc[:, 0:(NB + 1) * D], 0.0))
            link(nc.vector.memset(sweep0[:, :], 0.0))

        steps(l2_in)
        store_table(tmp)
        aggregate(False)

        def l2_mid(link, root):
            link(nc.vector.tensor_scalar(c1[:, :], indeg[:, :], 1.0, None, ALU.max))
            root(c1[:, :])
            link(nc.vector.tensor_scalar(c2[:, :], indeg[:, :], 0.5, None, ALU.is_lt))
            link(nc.vector.tensor_tensor(accD, accD, over(c1[:, :]), ALU.mult))
            link(nc.vector.tensor_tensor(tmp, xc[:, :, :], over(c2[:, :]), ALU.mult))
            link(nc.vector.tensor_tensor(tmp, tmp, accD, ALU.add))

        steps(l2_mid)
        node_linear(D, lambda b, n: tmp[:, bass.ds(b, n), :], L2_t, lambda b, n: f01[:, bass.ds(b, n), :])

        def l2_out(link, root):
            link(nc.vector.tensor_tensor(f01, f01, along(l2b_r[:, :]), ALU.add))
            link(nc.vector.tensor_scalar(f01, f01, 0.0, None, ALU.max))

        steps(l2_out)
        layernorm(f01, xc[:, :, :])

        node_linear(D, lambda b, n: xc[:, bass.ds(b, n), :], L3_s, lambda b, n: f01[:, bass.ds(b, n), :])

        def l3_in(link, root):
            link(nc.vector.tensor_scalar(c2[:, :], indeg[:, :], 1.0, None, ALU.add))
            root(c2[:, :])
            link(nc.vector.tensor_tensor(accD, f01, over(c2[:, :]), ALU.mult))
            link(nc.vector.memset(acc[:, NB * D:(NB + 1) * D], 0.0))
            link(nc.vector.memset(sweep0[:, :], 0.0))

        steps(l3_in)
        store_table(accD)
        aggregate(False)

        fsum, fvar = sb("fsum", [P, D]), sb("fvar", [P, D])

        def column_sums(i, part):
            with nc.Block() as block:
                @block.tensor
                def _(pe):
                    nc.tensor.matmul(ps[i][:, 0, 0:D], ones[:, :], part[:, :], start=True, stop=True)

        def bn_mean(link, root):
            link(nc.vector.tensor_tensor(accD, accD, over(c2[:, :]), ALU.mult))
            link(nc.vector.tensor_tensor(accD, accD, along(l3b_r[:, :]), ALU.add))
            link(nc.vector.tensor_scalar(accD[:, NB - 1, :], accD[:, NB - 1, :], valid[:, 0:1], None, ALU.mult))
            link(nc.vector.tensor_reduce(fsum[:, :], accD.rearrange("p b f -> p f b"), AX, ALU.add))

        def bn_var(link, root):
            link(nc.vector.tensor_scalar(fsum[:, :], ps[0][:, 0, 0:D], 1.0 / N, None, ALU.mult))
            link(nc.vector.tensor_tensor(accD, accD, along(fsum[:, :]), ALU.subtract))
            link(nc.vector.tensor_scalar(accD[:, NB - 1, :], accD[:, NB - 1, :], valid[:, 0:1], None, ALU.mult))
            link(nc.vector.tensor_tensor(tmp, accD, accD, ALU.mult))
            link(nc.vector.tensor_reduce(fvar[:, :], tmp.rearrange("p b f -> p f b"), AX, ALU.add))

        def bn_out(link, root):
            link(nc.vector.tensor_scalar(fvar[:, :], ps[1][:, 0, 0:D], 1.0 / N, EPS, ALU.mult, ALU.add))
            root(fvar[:, :])
            link(nc.vector.tensor_tensor(fvar[:, :], fvar[:, :], gam_r[:, :], ALU.mult))
            link(nc.vector.tensor_tensor(accD, accD, along(fvar[:, :]), ALU.mult))
            link(nc.vector.tensor_tensor(accD, accD, along(bet_r[:, :]), ALU.add))
            link(nc.vector.tensor_scalar(accD, accD, 0.0, None, ALU.max))

        steps(bn_mean)
        column_sums(0, fsum)
        steps(bn_var)
        column_sums(1, fvar)
        steps(bn_out)
        layernorm(accD, xc[:, :, :])

        store = sem("out_stored")
        with nc.Block() as block:
            @block.sync
            def _(sp):
                sp.dma_start(out[0:NFULL * P, :].rearrange("(b p) f -> p b f", p=P), xc[:, 0:NFULL, :]).then_inc(store, 16)
                if NREST:
                    sp.dma_start(out[NFULL * P:N, :], xc[0:NREST, NFULL, :]).then_inc(store, 16)
                sp.wait_ge(store, 32 if NREST else 16)


_INS = ["x", "src", "dst", "edge_attr_16", "edge_weight", "L1_gnn_W1", "L1_gnn_b1", "L1_gnn_W2", "L1_gnn_b2",
        "L1_gnn_W3", "L1_gnn_b3", "L2_gnn_W", "L2_gnn_b", "L3_gnn_W", "L3_gnn_b", "L3_gnn_gamma", "L3_gnn_beta"]


def kernel(**inputs):
    import numpy as np
    import concourse.bacc as bacc
    from concourse import mybir as mb
    from concourse.bass_utils import run_bass_kernel_spmd

    nc = bacc.Bacc("TRN2", target_bir_lowering=False, num_devices=1)
    arrays, args = {}, []
    for name in _INS:
        a = np.ascontiguousarray(inputs[name])
        arrays[f"in_{name}"] = a
        args.append(nc.dram_tensor(f"in_{name}", a.shape, mb.dt.from_np(a.dtype), kind="ExternalInput").ap())
    out = nc.dram_tensor("out", inputs["x"].shape, mb.dt.float32, kind="ExternalOutput").ap()
    build(nc, *args, out)
    return run_bass_kernel_spmd(nc, [arrays], core_ids=[0]).results[0]["out"]
```

```python
from contextlib import ExitStack

import concourse.bass as bass
from concourse import mybir

P = 128
TILES = 8
SLOTS = 4
GROUP = P * TILES
WIN = 2 * P
F32 = mybir.dt.float32
BF16 = mybir.dt.bfloat16
I32 = mybir.dt.int32
ALU = mybir.AluOpType
ACT = mybir.ActivationFunctionType
AX = mybir.AxisListType.X
HOPS = 10
START = 4
HC2 = 64
ALPHA = 0.1
EPS = 1e-5


def build(nc, x, src, dst, edge_attr, edge_weight, W1, b1, W2, b2, W3, b3, L2_W, L2_b,
          L3_W, L3_b, gamma, beta, out):
    N, D = x.shape
    E = src.shape[0]
    DE = edge_attr.shape[1]
    H = W2.shape[0]
    KE = 2 * D + DE
    NB = -(-N // P)
    NFULL = N // P
    NREST = N - NFULL * P
    GFULL = E // GROUP
    EREST = E - GFULL * GROUP
    TP = EREST // TILES
    NG = -(-E // GROUP)
    NG += -NG % SLOTS
    WINDOWS = -(-NB // 2)
    SUP = 512
    GPS = 12
    SUPS = next(n for n in range(2, 99, 2) if (NG - GPS * n) * GROUP * N // E + 100 <= SUP * n)
    DG = NG - GPS * SUPS
    CHB = 7
    CPS = NB // CHB
    RING = 4
    assert NB % CHB == 0 and 2 * CPS % RING == 0 and DG > 0 and DG % SLOTS == 0
    DENSE = SUPS * P * NB * SUP
    assert DENSE % P == 0
    HALF = TILES // 2
    HC = H + 1
    assert EREST % TILES == 0 and NB % 7 == 0 or True

    ctx = ExitStack()
    with ctx:
        def sb(name, shape, dt=F32):
            return ctx.enter_context(nc.sbuf_tensor(name, shape, dt))

        def pb(name, shape, dt=F32):
            return ctx.enter_context(nc.psum_tensor(name, shape, dt))

        sems_by_name = {}

        def sem(name):
            if name not in sems_by_name:
                sems_by_name[name] = ctx.enter_context(nc.semaphore(name))
            return sems_by_name[name]

        src_i = sb("src_i", [P, NG + SLOTS, TILES], I32)
        dst_f = sb("dst_f", [P, NG + SLOTS, TILES])
        wgt = sb("wgt", [P, NG + 1, TILES])
        base0 = sb("base0", [P, NG + 1])
        base = sb("base", [P, NG + 1])
        base_blk = sb("base_blk", [1, NG + 1], I32)
        sweep0 = sb("sweep0", [P, 1])
        near = sb("near", [P, 1])
        sweeps_i = sb("sweeps_i", [1, 2], I32)
        addr = sb("addr", [P, DG, TILES], I32)
        xc = sb("xc", [P, NB, D])
        tmp_raw = sb("tmp", [P, max(NB * D, 2 * 2 * HALF * P + 2 * HALF * P + HALF * (3 * H + 1) + 2 * P, 2 * CHB * SUP + SUP)])
        tmp = tmp_raw[:, 0:NB * D].rearrange("p (b f) -> p b f", f=D)
        acc = sb("acc", [P, max((NB + 1) * HC, (NB + 1) * D + 2 * CHB * SUP)])
        indeg = sb("indeg", [P, NB])
        outdeg = sb("outdeg", [P, NB])
        f01_raw = sb("f01", [P, max(NB * D, SLOTS * TILES * (KE + DE))])
        f01 = f01_raw[:, 0:NB * D].rearrange("p (b f) -> p b f", f=D)
        idx = sb("idx", [P, SLOTS, TILES], I32)
        parts48 = sb("parts48", [P, SLOTS, TILES, 3 * D], BF16)
        idd = sb("idd", [P, SLOTS, TILES], I32)
        lol = sb("lol", [P, SLOTS, TILES])
        hil = sb("hil", [P, SLOTS, TILES])
        dloc = sb("dloc", [P, SLOTS, TILES])
        wl = sb("wl", [P, SLOTS, TILES])
        onehot_b = sb("onehot", [P, SLOTS, TILES, WIN], BF16)
        msg = sb("msg", [P, SLOTS, TILES, D])
        src_lo = sb("src_lo", [P, NG + 1, TILES])
        src_hi = sb("src_hi", [P, NG + 1, TILES])
        past_i = sb("past_i", [P, 1], I32)
        before = sb("before", [P, P])
        valid = sb("valid", [P, 1])
        work = onehot_b[:, :, :, :].rearrange("p u k n -> p (u k n)").bitcast(F32)
        iota_i = sb("iota_i", [P, WIN], I32)
        iota = sb("iota", [P, WIN])
        row_i = sb("row_i", [P, 1], I32)
        row = sb("row", [P, 1])
        ident = sb("ident", [P, P])
        ones = sb("ones", [P, P])

        ps = [pb(f"ps{i}", [P, 2, 512]) for i in range(3)]
        spare = pb("spare", [P, 512])
        misc = pb("misc", [P, 512])
        psD, psDT = ps[2][:, 0, :], ps[2][:, 1, :]
        sums, psT, ps1, ps2 = ps[0], ps[1][:, 0, :], ps[1][:, 1, :], ps[2][:, 0, :]
        cnt_ps = spare[:, 0:P]
        iota_ps = misc[:, 0:WIN]

        table = nc.dram_tensor("node_table", (NB * P, D), F32).ap()
        dense = nc.dram_tensor("dense", (DENSE + P, 1), F32).ap()
        dense_v = dense[0:DENSE, :].rearrange("(b p s f) a -> b p (s f a)", b=SUPS, p=P, s=NB)
        table_v = table.rearrange("(b p) f -> p b f", p=P)

        def clear(sems, gathers=()):
            for s in gathers:
                nc.gpsimd.dma_reset(range(s.num, s.num + 1))
            if gathers:
                nc.all_engine_barrier()
            for s in [*sems, *gathers]:
                nc.sync.sem_clear(s)
            nc.all_engine_barrier()

        def slot_sems(name):
            return [sem(f"{name}{u}") for u in range(SLOTS)]

        def load_nodes(eng, to, frm, done):
            n = 0
            eng.dma_start(to[:, 0:NFULL, :], frm[0:NFULL * P, :].rearrange("(b p) f -> p b f", p=P)).then_inc(done, 16)
            n += 16
            if NREST:
                eng.dma_start(to[0:NREST, NFULL, :], frm[NFULL * P:N, :]).then_inc(done, 16)
                n += 16
            return n

        i_zero, i_src, i_x, i_dst, i_wgt, i_first, i_const, i_chk, i_iota = (
            sem(n) for n in ("prep_zeroed", "src_in", "x_in", "dst_in", "wgt_in", "first_in", "prep_const",
                             "prep_check", "prep_iota"))
        i_step, i_sum, i_tab = sem("prep_step"), sem("prep_sum"), sem("table_stored")
        with nc.Block() as block:
            dst_i = acc[:, 0:(NG + 1) * TILES].bitcast(I32).rearrange("p (g k) -> p g k", k=TILES)
            first_i = work[:, 2048:2048 + NG + 1].bitcast(I32)
            first_f = work[:, 3072:3072 + NG + 1]
            chk = sb("chk", [P, 8])

            @block.sync
            def _(sp):
                sp.wait_ge(i_zero, 4)
                for arr, dr, s in ((src_i, src, i_src), (dst_i, dst, i_dst), (wgt, edge_weight, i_wgt)):
                    sp.dma_start(arr[:, 0:GFULL, :], dr[0:GFULL * GROUP].rearrange("(g p k) -> p g k", p=P, k=TILES)).then_inc(s, 16)
                    if TP:
                        sp.dma_start(arr[0:TP, GFULL, :], dr[GFULL * GROUP:E].rearrange("(p k) -> p k", k=TILES)).then_inc(s, 16)
                load_nodes(sp, xc, x, i_x)

            LOADS = 32 if TP else 16
            XLOADS = 32 if NREST else 16

            @block.scalar
            def _(act):
                act.wait_ge(i_x, XLOADS)
                act.dma_start(table_v, xc[:, :, :]).then_inc(i_tab, 16)
                act.wait_ge(i_tab, 16)

            @block.gpsimd
            def _(pool):
                nc.gpsimd.iota(iota_i[:, :], [[1, WIN]], 0, 0).then_inc(i_iota, 1)
                nc.gpsimd.iota(row_i[:, :], [[0, 1]], 0, 1).then_inc(i_iota, 1)

            @block.vector
            def _(dve):
                nc.vector.memset(src_i[:, GFULL:NG + SLOTS, :], 0).then_inc(i_zero, 1)
                nc.vector.memset(dst_i[:, GFULL:NG + 1, :], -1).then_inc(i_zero, 1)
                nc.vector.memset(wgt[:, GFULL:NG + 1, :], 0.0).then_inc(i_zero, 1)
                nc.vector.memset(xc[:, NB - 1, :], 0.0).then_inc(i_zero, 1)
                n = [0]

                def link(ins):
                    n[0] += 1
                    ins.then_inc(i_step, 1)
                    dve.wait_ge(i_step, n[0])

                link(nc.vector.memset(chk[:, :], 0.0))
                dve.wait_ge(i_iota, 2)
                link(nc.vector.tensor_copy(iota[:, :], iota_i[:, :]))
                link(nc.vector.tensor_copy(iota_ps[:, :], iota_i[:, :]))
                link(nc.vector.tensor_copy(row[:, :], row_i[:, :]))
                link(nc.vector.tensor_scalar(ident[:, :], iota[:, 0:P], row[:, 0:1], None, ALU.is_equal))
                dve.wait_ge(i_dst, LOADS)
                link(nc.vector.tensor_scalar(first_i[0:1, :], dst_i[0:1, :, 0], -P, None, ALU.bitwise_and))
                link(nc.vector.tensor_scalar(first_f[0:1, :], first_i[0:1, :], 0.0, None, ALU.max))
                nc.vector.memset(ones[:, :], 1.0).then_inc(i_const, 1)
                dve.wait_ge(i_sum, 1)
                link(nc.vector.tensor_copy(base0[:, :], ps[1][:, 0, 0:NG + 1]))
                link(nc.vector.memset(dst_f[:, NG:NG + SLOTS, :], -1.0))
                link(nc.vector.tensor_copy(dst_f[:, 0:NG + 1, :], dst_i))
                off = work[:, 0:(NG + 1) * TILES].rearrange("p (g k) -> p g k", k=TILES)
                link(nc.vector.tensor_tensor(off, dst_f[:, 0:NG + 1, :], base0[:, :].unsqueeze(2).broadcast_to([P, NG + 1, TILES]), ALU.subtract))
                if GFULL:
                    full = off[:, 0:GFULL, :].rearrange("p g k -> p (g k)")
                    link(nc.vector.tensor_reduce(chk[:, 0:1], full, AX, ALU.max))
                    link(nc.vector.tensor_reduce(chk[:, 1:2], full, AX, ALU.min))
                if TP:
                    link(nc.vector.tensor_reduce(chk[0:TP, 2:3], off[0:TP, GFULL, :], AX, ALU.max))
                    link(nc.vector.tensor_reduce(chk[0:TP, 3:4], off[0:TP, GFULL, :], AX, ALU.min))
                link(nc.vector.tensor_tensor(chk[:, 4:5], chk[:, 0:1], chk[:, 2:3], ALU.max))
                link(nc.vector.tensor_tensor(chk[:, 5:6], chk[:, 1:2], chk[:, 3:4], ALU.min))
                link(nc.vector.tensor_scalar(chk[:, 4:5], chk[:, 4:5], float(WIN) - 0.5, None, ALU.is_gt))
                link(nc.vector.tensor_scalar(chk[:, 5:6], chk[:, 5:6], -0.5, None, ALU.is_lt))
                link(nc.vector.tensor_reduce(chk[:, 7:8], dst_f[:, 0:DG, :].rearrange("p g k -> p (g k)"), AX, ALU.max))
                link(nc.vector.tensor_scalar(chk[:, 7:8], chk[:, 7:8], float(SUPS * SUP) - 0.5, None, ALU.is_gt))
                nc.vector.tensor_tensor(chk[:, 6:7], chk[:, 4:5], chk[:, 5:6], ALU.add).then_inc(i_chk, 1)
                dve.wait_ge(i_sum, 2)
                link(nc.vector.tensor_scalar(near[:, :], ps[0][:, 0, 0:1], 0.5, None, ALU.is_lt))
                link(nc.vector.tensor_scalar(chk[0:1, 7:8], near[0:1, 0:1], float(1 - WINDOWS), float(WINDOWS), ALU.mult, ALU.add))
                link(nc.vector.tensor_copy(sweeps_i[:, 0:1], chk[0:1, 7:8]))
                link(nc.vector.tensor_scalar(chk[0:1, 6:7], ps[0][0:1, 0, 1:2], 0.5, None, ALU.is_lt))
                link(nc.vector.tensor_tensor(sweeps_i[:, 1:2], chk[0:1, 6:7], near[0:1, 0:1], ALU.mult))
                link(nc.vector.tensor_scalar(base0[:, :], base0[:, :], near[:, 0:1], None, ALU.mult))
                dve.wait_ge(i_wgt, LOADS)
                link(nc.vector.tensor_scalar(wgt[:, :, :], wgt[:, :, :], 1.0 - ALPHA, None, ALU.mult))
                dve.wait_ge(i_x, XLOADS)
                link(nc.vector.tensor_scalar(f01[:, :, :], xc[:, :, :], ALPHA, None, ALU.mult))
                dve.wait_ge(i_src, LOADS)
                lo_i = acc[:, 0:(NG + 1) * TILES].bitcast(I32).rearrange("p (g k) -> p g k", k=TILES)
                link(nc.vector.tensor_scalar(lo_i, src_i[:, 0:NG + 1, :], P - 1, None, ALU.bitwise_and))
                link(nc.vector.tensor_copy(src_lo[:, :, :], lo_i))
                link(nc.vector.memset(src_hi[:, GFULL:NG + 1, :], -1.0))
                for g, p in ((slice(0, GFULL), P), (slice(GFULL, GFULL + 1), TP)):
                    if p and (g.stop > g.start):
                        link(nc.vector.tensor_tensor(src_hi[0:p, g, :], src_i[0:p, g, :], src_lo[0:p, g, :], ALU.subtract))
                        link(nc.vector.tensor_scalar(src_hi[0:p, g, :], src_hi[0:p, g, :], 1.0 / P, None, ALU.mult))
                shape = [P, DG, TILES]
                a_i = work[:, 0:DG * TILES].bitcast(I32).rearrange("p (g k) -> p g k", k=TILES)
                a_f = work[:, 1024:1024 + DG * TILES].rearrange("p (g k) -> p g k", k=TILES)
                d_i = work[:, 2048:2048 + DG * TILES].bitcast(I32).rearrange("p (g k) -> p g k", k=TILES)
                link(nc.vector.tensor_copy(d_i, dst_f[:, 0:DG, :]))
                link(nc.vector.tensor_scalar(a_i, d_i, 9, None, ALU.arith_shift_right))
                link(nc.vector.tensor_copy(a_f, a_i))
                link(nc.vector.scalar_tensor_tensor(a_f, a_f, float(P), src_lo[:, 0:DG, :], ALU.mult, ALU.add))
                link(nc.vector.scalar_tensor_tensor(a_f, a_f, float(NB), src_hi[:, 0:DG, :], ALU.mult, ALU.add))
                link(nc.vector.tensor_copy(a_i, a_f))
                link(nc.vector.tensor_scalar(a_i, a_i, 9, None, ALU.logical_shift_left))
                link(nc.vector.tensor_scalar(d_i, d_i, SUP - 1, None, ALU.bitwise_and))
                link(nc.vector.tensor_tensor(addr[:, :, :], a_i, d_i, ALU.bitwise_or))
                link(nc.vector.tensor_scalar(past_i[:, :], row_i[:, :], DENSE, None, ALU.bitwise_or))
                link(nc.vector.tensor_tensor(before[:, :], iota[:, 0:P], row[:, 0:1].broadcast_to([P, P]), ALU.is_lt))
                link(nc.vector.tensor_scalar(valid[:, :], row[:, :], float(NREST or P) - 0.5, None, ALU.is_lt))

            @block.tensor
            def _(pe):
                pe.wait_ge(i_const, 1)
                nc.tensor.matmul(ps[1][:, 0, 0:NG + 1], ones[0:1, :], first_f[0:1, :], start=True, stop=True).then_inc(i_sum, 1)
                pe.wait_ge(i_chk, 1)
                nc.tensor.matmul(ps[0][:, 0, 0:2], ones[:, :], chk[:, 6:8], start=True, stop=True).then_inc(i_sum, 1)

        W1_s = sb("W1_s", [KE, H])
        W2_s = sb("W2_s", [H, H])
        W3_s = sb("W3_s", [H, D])
        L2_s = sb("L2_s", [D, D])
        L2_t = sb("L2_t", [D, D])
        L3_s = sb("L3_s", [D, D])
        b1_c = sb("b1_c", [H, 1])
        b2_r = sb("b2_r", [P, H])
        b3_r, l2b_r, l3b_r, gam_r, bet_r = (sb(n, [P, D]) for n in ("b3_r", "l2b_r", "l3b_r", "gam_r", "bet_r"))
        par, par_t = sem("params_in"), sem("params_t")
        with nc.Block() as block:
            @block.sync
            def _(sp):
                n = 0
                for to, frm in ((W1_s, W1), (W2_s, W2), (W3_s, W3), (L2_s, L2_W), (L3_s, L3_W)):
                    sp.dma_start(to[:, :], frm).then_inc(par, 16)
                    n += 16
                sp.dma_start(b1_c[:, :], b1.rearrange("(p a) -> p a", a=1)).then_inc(par, 16)
                n += 16
                for to, frm in ((b2_r, b2), (b3_r, b3), (l2b_r, L2_b), (l3b_r, L3_b), (gam_r, gamma), (bet_r, beta)):
                    sp.dma_start(to[:, :], frm.rearrange("(a f) -> a f", a=1).broadcast_to([P, frm.shape[0]])).then_inc(par, 16)
                    n += 16
                sp.wait_ge(par, n)

            @block.tensor
            def _(pe):
                pe.wait_ge(par, 16 * 12)
                nc.tensor.transpose(ps[2][0:D, 0, 0:D], L2_s[:, :], ident[0:D, 0:D]).then_inc(par_t, 1)

            @block.vector
            def _(dve):
                dve.wait_ge(par_t, 1)
                nc.vector.tensor_copy(L2_t[:, :], ps[2][0:D, 0, 0:D])

        sweeps = nc.values_load(sweeps_i[0:1, 0:1], min_val=1, max_val=WINDOWS)
        dense_ok = nc.values_load(sweeps_i[0:1, 1:2], min_val=0, max_val=1)

        chunk = [acc[:, (NB + 1) * D + r * CHB * SUP:(NB + 1) * D + (r + 1) * CHB * SUP] for r in range(2)] + [
            tmp_raw[:, r * CHB * SUP:(r + 1) * CHB * SUP] for r in range(2)]
        panel = tmp_raw[:, 2 * CHB * SUP:2 * CHB * SUP + SUP]
        fcur = xc

        cols = sb("cols", [P, 2, 3, TILES])
        wsum = sb("wsum", [P, 2, TILES])
        dup = sb("dup", [P, 2, TILES])
        dup_i = sb("dup_i", [P, 2, TILES], I32)
        place = sb("place", [P, 2, TILES], I32)
        diag = tmp_raw[:, 0:2 * 3 * P].rearrange("p (v a e) -> p v a e", v=2, a=3)
        same = tmp_raw[:, 2 * 3 * P:2 * 3 * P + 4 * P].rearrange("p (a e) -> p a e", a=4)

        def aggregate_block(weighted, first=0, last=NG, with_dense=False, zero_fill=False, building=False):
            TG = 2 * GPS if with_dense else SLOTS
            turns = (last - first) // TG
            idx_ready, hot_ready, gathered, summed, chunk_in, chunk_free = (slot_sems(f"agg_{n}") for n in (
                "idx", "onehot", "gathered", "summed", "chunk_in", "chunk_free"))
            step, window, taken, added, scaled, high, rest, middle, parts_ready, panel_done, panel_kept, panel_turned, panel_added, zeroed, paced = (
                sem(f"agg_{n}") for n in ("step", "window", "slot_taken", "added", "scaled", "high", "rest", "middle", "parts",
                                          "panel_done", "panel_kept", "panel_turned", "panel_added", "zeroed", "paced"))
            cols_set, diag_set, spread, found, looked, chosen, places_set, carried, slot_free, scattered = (
                sem(f"build_{n}") for n in ("cols", "diag", "spread", "found", "looked", "chosen", "places_set", "carried", "slot_free",
                                            "scattered"))
            nstep = 2 if weighted else 1

            with nc.Block() as block:
                def at(t, j):
                    return t * TG + j, j % SLOTS, t * (TG // SLOTS) + j // SLOTS

                def chunks_before(j):
                    return range(-(-j * CPS // GPS), -(-(j + 1) * CPS // GPS))

                if with_dense:
                    @block.sync
                    def _(sp):
                        with sp.Fori(0, turns) as t:
                            for c in range(2 * CPS):
                                r = c % RING
                                sp.wait_ge(chunk_free[r], t * (2 * CPS // RING) + (c // RING + 1))
                                sp.dma_start(chunk[r], dense_v[bass.ds(t * 2 + c // CPS, 1), :, c % CPS * CHB * SUP:(c % CPS + 1) * CHB * SUP]
                                             .rearrange("b p f -> p (b f)")).then_inc(chunk_in[r], 16)

                if zero_fill:
                    @block.sync
                    def _(sp):
                        sp.wait_ge(zeroed, 1)
                        with sp.Fori(0, SUPS) as b:
                            for c in range(CPS):
                                sp.dma_start(dense_v[bass.ds(b, 1), :, c * CHB * SUP:(c + 1) * CHB * SUP]
                                             .rearrange("b p f -> p (b f)"), chunk[0]).then_inc(dense_zero[c % 2], 16)
                                if c % 2:
                                    for h in range(2):
                                        sp.wait_ge(dense_zero[h], b * (16 * CPS // 2) + 16 * (c // 2 + 1))
                                    sp.sem_inc(paced, 1)
                        sp.dma_start(dense[DENSE:DENSE + P, :], chunk[0][:, 0:1]).then_inc(dense_zero[0], 16)
                        sp.wait_ge(dense_zero[0], 16 * (SUPS * CPS // 2 + 1))

                @block.scalar
                def _(act):
                    def set_indices(t, j):
                        l, u, n = at(t, j)
                        act.wait_ge(summed[u], n + 1)
                        nc.scalar.copy(idx[:, u, :], src_i[:, bass.ds(l + first, 1), :].rearrange("p a k -> p (a k)")).then_inc(idx_ready[u], 1)

                    for j in range(SLOTS - 1):
                        set_indices(0, j)
                    with act.Fori(0, turns) as t:
                        for j in range(TG):
                            set_indices(t, j + SLOTS - 1)
                            l, u, n = at(t, j)
                            if weighted:
                                act.wait_ge(scaled, l + 1)
                            else:
                                act.wait_ge(gathered[u], n * (16 * TILES) + 16 * TILES)
                            nc.scalar.copy(parts48[:, u, :, 0:D], msg[:, u, :, :]).then_inc(high, 1)
                            act.wait_ge(rest, l + 1)
                            nc.scalar.copy(parts48[:, u, :, D:2 * D], msg[:, u, :, :]).then_inc(middle, 1)
                            if with_dense and j % GPS == GPS - 1:
                                p = t * 2 + j // GPS
                                act.wait_ge(panel_done, p + 1)
                                act.wait_ge(panel_turned, p + 1)
                                nc.scalar.copy(panel[0:D, :], psD[0:D, :])
                                nc.scalar.copy(panel[HC2:HC2 + D, :], psD[HC2:HC2 + D, :]).then_inc(panel_kept, 1)
                            if building:
                                v = j % 2
                                act.wait_ge(cols_set, l + 1)
                                for k in range(TILES):
                                    act.wait_ge(spread, l * TILES + (k + 1))
                                    for a in range(3):
                                        m = nc.scalar.activation(diag[:, k % 2, a, :], ident[:, :], ACT.Copy, scale=cols[:, v, a, k:k + 1])
                                    m.then_inc(diag_set, 1)

                @block.gpsimd
                def _(pool):
                    def claim(t, j):
                        l, u, n = at(t, j)
                        pool.wait_ge(idx_ready[u], n + 1)
                        pool.wait_ge(summed[u], n + 1)
                        pool.sem_inc(taken, 1)

                    def gather(u, k):
                        pool.indirect_dma_start(
                            out=msg[:, u, k, :], out_offset=None, in_=table,
                            in_offset=bass.IndirectOffsetOnAxis(ap=idx[:, u, k:k + 1], axis=0),
                        ).then_inc(gathered[u], 16)

                    def scatter(t, j, ahead):
                        g, v, u = t * TG + j, j % 2, (j + 2) % SLOTS
                        pool.wait_ge(chosen, g * 3 + 4)
                        for k in range(TILES):
                            pool.sem_inc(carried, 1)
                            pool.indirect_dma_start(
                                out=dense, out_offset=bass.IndirectOffsetOnAxis(ap=place[:, v, k:k + 1], axis=0),
                                in_=wsum[:, v, k:k + 1], in_offset=None, compute_op=ALU.add).then_inc(scattered, 16)
                            if ahead:
                                gather(u, k)
                            pool.wait_ge(scattered, g * (16 * TILES) + (k + 1) * 16)
                        pool.sem_inc(slot_free, 1)

                    if building:
                        pool.sem_inc(slot_free, 2)
                        for j in range(2):
                            claim(0, j)
                            for k in range(TILES):
                                gather(j, k)
                        if turns > 1:
                            with pool.Fori(0, turns - 1) as t:
                                for j in range(TG):
                                    claim(t, j + 2)
                                    scatter(t, j, True)
                        for j in range(TG):
                            if j + 2 < TG:
                                claim(turns - 1, j + 2)
                            scatter(turns - 1, j, j + 2 < TG)
                    else:
                        with pool.Fori(0, turns) as t:
                            for j in range(TG):
                                claim(t, j)
                                for k in range(TILES):
                                    gather(j % SLOTS, k)

                @block.vector
                def _(dve):
                    if zero_fill:
                        nc.vector.memset(chunk[0], 0.0).then_inc(zeroed, 1)
                    if with_dense:
                        nc.vector.memset(panel, 0.0).then_inc(zeroed, 1)
                    nc.vector.tensor_scalar(base[:, :], base0[:, :], sweep0[:, 0:1], None, ALU.add).then_inc(window, 1)
                    dve.wait_ge(window, 1)
                    nc.vector.tensor_scalar(base_blk[:, :], base[0:1, :], 1.0 / P, None, ALU.mult).then_inc(window, 1)
                    if not (with_dense or zero_fill or building):
                        nc.vector.tensor_scalar(sweep0[:, :], sweep0[:, :], float(WIN), None, ALU.add).then_inc(window, 1)
                        dve.wait_ge(window, 3)
                    dve.wait_ge(window, 2)

                    def make_onehots(t, j):
                        l, u, n = at(t, j)
                        g = l + first
                        dve.wait_ge(summed[u], n + 1)
                        nc.vector.tensor_scalar(dloc[:, u, :], dst_f[:, bass.ds(g, 1), :].rearrange("p a k -> p (a k)"),
                                                base[:, bass.ds(g, 1)], None, ALU.subtract).then_inc(step, 1)
                        if weighted:
                            nc.vector.tensor_copy(wl[:, u, :], wgt[:, bass.ds(g, 1), :].rearrange("p a k -> p (a k)")).then_inc(step, 1)
                        dve.wait_ge(step, (l + 1) * nstep)
                        for k in range(TILES):
                            m = nc.vector.tensor_scalar(onehot_b[:, u, k, :], iota_ps[:, :], dloc[:, u, k:k + 1], None, ALU.is_equal)
                        m.then_inc(hot_ready[u], 1)

                    def add_sums(t, j):
                        l, u, n = at(t, j)
                        blk = dve.value_load(base_blk[0:1, bass.ds(l + first, 1)], min_val=0, max_val=NB - 1)
                        here = acc[:, bass.ds(blk * D, 2 * D)].rearrange("p (a f) -> p a f", a=2)
                        dve.wait_ge(summed[u], n + 2)
                        for c in range(3):
                            dve.wait_ge(added, l * 3 + (c + START))
                            nc.vector.tensor_tensor(here, here, ps[u % 2][:, :, c * D:(c + 1) * D], ALU.add).then_inc(added, 1)

                    def build_group(g, v):
                        dve.wait_ge(spread, g * TILES + 1)
                        dve.sem_inc(places_set, 1)
                        for a, arr in ((1, dst_f), (2, wgt)):
                            nc.vector.tensor_copy(cols[:, v, a, :], arr[:, bass.ds(g, 1), :].rearrange("p a k -> p (a k)"))
                        nc.vector.tensor_copy(cols[:, v, 0, :], src_i[:, bass.ds(g, 1), :].rearrange("p a k -> p (a k)")).then_inc(cols_set, 1)
                        dve.wait_ge(slot_free, g + 1)
                        for k in range(TILES):
                            n = g * TILES + k
                            dve.wait_ge(spread, n + 3)
                            rows3 = ps[2][:, k % 2, :]
                            nc.vector.tensor_scalar(same[:, 0, :], rows3[:, 0:P], cols[:, v, 0, k:k + 1], None, ALU.is_equal).then_inc(found, 1)
                            dve.wait_ge(found, n * 3 + 1)
                            nc.vector.scalar_tensor_tensor(same[:, 1, :], rows3[:, P:2 * P], cols[:, v, 1, k:k + 1], same[:, 0, :],
                                                           ALU.is_equal, ALU.mult).then_inc(found, 1)
                            dve.wait_ge(found, n * 3 + 2)
                            nc.vector.tensor_tensor_reduce(out=same[:, 2, :], in0=rows3[:, 2 * P:3 * P], in1=same[:, 1, :], scale=1.0, scalar=0.0,
                                                           op0=ALU.mult, op1=ALU.add, accum_out=wsum[:, v, k:k + 1]).then_inc(looked, 1)
                            nc.vector.tensor_tensor_reduce(out=same[:, 3, :], in0=before[:, :], in1=same[:, 1, :], scale=1.0, scalar=0.0,
                                                           op0=ALU.mult, op1=ALU.add, accum_out=dup[:, v, k:k + 1]).then_inc(found, 1)
                            dve.wait_ge(looked, n + 3)
                            dve.wait_ge(found, n * 3 + 3)
                        nc.vector.tensor_scalar(dup_i[:, v, :], dup[:, v, :], 0.5, None, ALU.is_gt).then_inc(chosen, 1)
                        nc.vector.tensor_copy(place[:, v, :], addr[:, bass.ds(g, 1), :].rearrange("p a k -> p (a k)")).then_inc(chosen, 1)
                        dve.wait_ge(chosen, g * 3 + 3)
                        dve.sem_inc(places_set, 1)
                        nc.vector.copy_predicated(place[:, v, :], dup_i[:, v, :], past_i[:, 0:1].broadcast_to([P, TILES])).then_inc(chosen, 1)

                    if building:
                        dve.sem_inc(chosen, 1)
                    make_onehots(0, 0)
                    with dve.Fori(0, turns) as t:
                        for j in range(TG):
                            l, u, n = at(t, j)
                            make_onehots(t, j + 1)
                            if weighted:
                                dve.wait_ge(gathered[u], n * (16 * TILES) + 16 * TILES)
                                nc.vector.tensor_tensor(msg[:, u, :, :], msg[:, u, :, :], wl[:, u, :].unsqueeze(2).broadcast_to([P, TILES, D]),
                                                        ALU.mult).then_inc(scaled, 1)
                            if j:
                                add_sums(t, j - 1)
                            dve.wait_ge(high, l + 1)
                            nc.vector.tensor_tensor(msg[:, u, :, :], msg[:, u, :, :], parts48[:, u, :, 0:D], ALU.subtract).then_inc(rest, 1)
                            dve.wait_ge(middle, l + 1)
                            nc.vector.tensor_tensor(parts48[:, u, :, 2 * D:3 * D], msg[:, u, :, :], parts48[:, u, :, D:2 * D],
                                                    ALU.subtract).then_inc(parts_ready, 1)
                            if j == TG - 1:
                                add_sums(t, j)
                            if building:
                                build_group(l, j % 2)
                            if with_dense and j % GPS == GPS - 1:
                                p = t * 2 + j // GPS
                                there = acc[:, bass.ds(p * (SUP // P * D), SUP // P * D)].rearrange("p (a f) -> p a f", f=D)
                                turned = psDT[:, 0:SUP // P * (HC2 + D)].rearrange("p (a f) -> p a f", f=HC2 + D)
                                dve.wait_ge(panel_turned, p + 2)
                                dve.wait_ge(added, (l + (1 if j == TG - 1 else 0)) * 3 + START)
                                for c in range(2):
                                    dve.wait_ge(panel_added, p * 2 + (c + 1))
                                    nc.vector.tensor_tensor(there, there, turned[:, :, c * HC2:c * HC2 + D], ALU.add).then_inc(panel_added, 1)
                                dve.wait_ge(panel_added, p * 2 + 3)

                @block.tensor
                def _(pe):
                    pe.sem_inc(added, START)
                    for u in range(SLOTS):
                        pe.sem_inc(summed[u], 1)
                    if building:
                        pe.sem_inc(spread, 2)
                        pe.sem_inc(looked, 2)
                    if with_dense:
                        pe.wait_ge(zeroed, 1)
                        pe.sem_inc(panel_turned, 1)
                        pe.sem_inc(panel_added, 1)
                        pe.sem_inc(panel_kept, 1)
                        for r in range(RING):
                            pe.sem_inc(chunk_free[r], 1)
                    with pe.Fori(0, turns) as t:
                        for j in range(TG):
                            l, u, n = at(t, j)
                            if with_dense:
                                p = t * 2 + j // GPS
                                for c in chunks_before(j % GPS):
                                    cc = j // GPS * CPS + c
                                    r = cc % RING
                                    if c == 0:
                                        pe.wait_ge(panel_kept, p + 1)
                                    pe.wait_ge(chunk_in[r], t * (2 * CPS // RING * 16) + (cc // RING + 1) * 16)
                                    for i in range(CHB):
                                        sblk = c * CHB + i
                                        o = HC2 * (sblk % 2)
                                        m = nc.tensor.matmul(psD[o:o + D, :], fcur[:, sblk, :], chunk[r][:, i * SUP:(i + 1) * SUP],
                                                             start=sblk < 2, stop=sblk >= NB - 2, skip_group_check=True)
                                    m.then_inc(chunk_free[r], 1)
                                    if c == CPS - 1:
                                        pe.wait_ge(chunk_free[r], t * (2 * CPS // RING) + (cc // RING + 2))
                                        pe.sem_inc(panel_done, 1)
                            pe.wait_ge(hot_ready[u], n + 1)
                            pe.wait_ge(parts_ready, l + 1)
                            pe.wait_ge(added, l * 3 + (START - 3))
                            for k in range(TILES):
                                for h in range(2):
                                    m = nc.tensor.matmul(ps[u % 2][:, h, 0:3 * D], onehot_b[:, u, k, h * P:(h + 1) * P], parts48[:, u, k, :],
                                                         start=k == 0, stop=k == TILES - 1)
                            m.then_inc(summed[u], 1)
                            if building:
                                for k in range(TILES):
                                    pe.wait_ge(diag_set, l * TILES + (k + 1))
                                    pe.wait_ge(looked, l * TILES + (k + 1))
                                    nc.tensor.matmul(ps[2][:, k % 2, 0:3 * P], ones[:, :], diag[:, k % 2, :, :].rearrange("p a e -> p (a e)"),
                                                     start=True, stop=True).then_inc(spread, 1)
                            if with_dense and j % GPS == GPS - 1:
                                pe.wait_ge(panel_kept, p + 2)
                                pe.wait_ge(panel_added, p * 2 + 1)
                                for b in range(SUP // P):
                                    m = nc.tensor.transpose(psDT[:, b * (HC2 + D):(b + 1) * (HC2 + D)], panel[0:HC2 + D, b * P:(b + 1) * P],
                                                            ident[0:HC2 + D, 0:HC2 + D])
                                m.then_inc(panel_turned, 1)
            clear([*idx_ready, *hot_ready, *summed, *chunk_in, *chunk_free, step, window, taken, added, scaled, high, rest, middle,
                   parts_ready, panel_done, panel_kept, panel_turned, panel_added, zeroed, paced,
                   cols_set, diag_set, spread, found, looked, chosen, places_set, carried, slot_free], [*gathered, scattered])

        def aggregate(weighted):
            with nc.Fori(0, sweeps):
                aggregate_block(weighted)

        accD = acc[:, 0:NB * D].rearrange("p (b f) -> p b f", f=D)
        kept_acc, hop_store = sem("hop_kept"), sem("hop_store")
        dense_zero = [sem("dense_zero_even"), sem("dense_zero_odd")]

        def start_hop():
            with nc.Block() as block:
                @block.vector
                def _(dve):
                    nc.vector.memset(sweep0[:, :], 0.0)
                    nc.vector.memset(acc[:, NB * D:(NB + 1) * D], 0.0)
                    nc.vector.tensor_copy(accD, f01)

        def end_hop():
            with nc.Block() as block:
                @block.vector
                def _(dve):
                    nc.vector.memset(sweep0[:, :], 0.0)
                    nc.vector.tensor_copy(fcur[:, 0:NB // 2, :], accD[:, 0:NB // 2, :]).then_inc(kept_acc, 1)
                    dve.wait_ge(kept_acc, 2)
                    nc.vector.tensor_copy(accD[:, 0:NB // 2, :], f01[:, 0:NB // 2, :])
                    nc.vector.memset(acc[:, NB * D:(NB + 1) * D], 0.0)

                @block.scalar
                def _(act):
                    nc.scalar.copy(fcur[:, NB // 2:NB, :], accD[:, NB // 2:NB, :]).then_inc(kept_acc, 1)
                    act.wait_ge(kept_acc, 2)
                    nc.scalar.copy(accD[:, NB // 2:NB, :], f01[:, NB // 2:NB, :])

                @block.sync
                def _(sp):
                    sp.wait_ge(kept_acc, 2)
                    sp.dma_start(table_v, fcur[:, :, :]).then_inc(hop_store, 16)
                    sp.wait_ge(hop_store, 16)
            clear([kept_acc, hop_store])

        start_hop()
        with nc.If(dense_ok == 1):
            aggregate_block(True, first=DG, zero_fill=True)
            aggregate_block(True, last=DG, building=True)
            end_hop()

            with nc.Fori(0, HOPS - 1):
                aggregate_block(True, first=DG, with_dense=True)
                end_hop()
        with nc.Else():
            with nc.Fori(0, HOPS):
                aggregate(True)
                end_hop()

        x_back, x_again = sem("x_back"), sem("x_again")
        with nc.Block() as block:
            @block.vector
            def _(dve):
                dve.wait_ge(x_back, 1)
                nc.vector.memset(xc[:, NB - 1, :], 0.0).then_inc(x_back, 1)

            @block.scalar
            def _(act):
                nc.scalar.copy(accD, fcur[:, :, :]).then_inc(x_back, 1)

            @block.sync
            def _(sp):
                sp.wait_ge(x_back, 2)
                load_nodes(sp, xc, x, x_again)
                sp.wait_ge(x_again, 32 if NREST else 16)

        s1 = sb("ln_sum", [P, NB])
        s2 = sb("ln_var", [P, NB])

        def layernorm(y, to):
            step, sq, rt = sem("ln_step"), sem("ln_squared"), sem("ln_root")
            with nc.Block() as block:
                @block.vector
                def _(dve):
                    n = [0]

                    def link(ins):
                        n[0] += 1
                        ins.then_inc(step, 1)
                        dve.wait_ge(step, n[0])

                    wide = [P, NB, D]
                    link(nc.vector.tensor_tensor(to, xc[:, :, :], y, ALU.add))
                    link(nc.vector.tensor_reduce(s1[:, :], to, AX, ALU.add))
                    link(nc.vector.tensor_scalar(s1[:, :], s1[:, :], 1.0 / D, None, ALU.mult))
                    link(nc.vector.tensor_tensor(to, to, s1[:, :].unsqueeze(2).broadcast_to(wide), ALU.subtract))
                    dve.wait_ge(sq, 1)
                    link(nc.vector.tensor_reduce(s2[:, :], tmp[:, :, :], AX, ALU.add))
                    link(nc.vector.tensor_scalar(s2[:, :], s2[:, :], 1.0 / D, EPS, ALU.mult, ALU.add))
                    dve.wait_ge(rt, 1)
                    link(nc.vector.reciprocal(s2[:, :], s1[:, :]))
                    link(nc.vector.tensor_tensor(to, to, s2[:, :].unsqueeze(2).broadcast_to(wide), ALU.mult))

                @block.scalar
                def _(act):
                    act.wait_ge(step, 4)
                    nc.scalar.activation(tmp[:, :, :], to, ACT.Square).then_inc(sq, 1)
                    act.wait_ge(step, 6)
                    nc.scalar.activation(s1[:, :], s2[:, :], ACT.Sqrt).then_inc(rt, 1)
            clear([step, sq, rt])

        layernorm(accD, xc[:, :, :])

        def store_table(frm):
            s = sem("table_stored_again")
            with nc.Block() as block:
                @block.sync
                def _(sp):
                    sp.dma_start(table_v, frm).then_inc(s, 16)
                    sp.wait_ge(s, 16)
            clear([s])

        store_table(xc[:, :, :])

        HQ = HALF * P
        rows = f01_raw[:, 0:SLOTS * TILES * KE].rearrange("p (u k f) -> p u k f", u=SLOTS, k=TILES)
        attr = f01_raw[:, SLOTS * TILES * KE:SLOTS * TILES * (KE + DE)].rearrange("p (u k f) -> p u k f", u=SLOTS, k=TILES)
        rowsT = tmp_raw[:, 0:2 * HQ].rearrange("p (q e) -> p q e", q=2)
        h1T = tmp_raw[:, 2 * HQ:4 * HQ].rearrange("p (q e) -> p q e", q=2)
        h2pre = tmp_raw[:, 4 * HQ:5 * HQ].rearrange("p (k f) -> p k f", k=HALF)
        h2 = tmp_raw[:, 5 * HQ:6 * HQ].rearrange("p (k f) -> p k f", k=HALF)
        PARTS = 3 * H + 1
        parts = tmp_raw[:, 6 * HQ:6 * HQ + HALF * PARTS].bitcast(BF16).rearrange("p (q k f) -> p q k f", q=2, k=HALF)
        hotsrc = parts48[:, :, :, :].rearrange("p u k f -> p (u k f)")[:, 0:2 * TILES * 2 * P].rearrange("p (u k a e) -> p u k a e", u=2, k=TILES, a=2)

        gathered, attr_in, idx_ready, group_free = (slot_sems(f"l1_{n}") for n in ("gathered", "attr", "idx", "free"))
        (transposed, rowsT_ready, lin1, h1T_ready, lin2, h2pre_ready, h2_ready, rest_ready, mid_ready, parts_ready,
         hot_ready, summed_q, added, step, window, taken, attr_placed, cnt_hot, cnt_sum, cnt_added) = (
            sem(f"l1_{n}") for n in ("transposed", "rowsT", "lin1", "h1T", "lin2", "h2pre", "h2", "rest", "mid", "parts",
                                     "onehot", "summed", "added", "step", "window", "slot_taken", "attr_placed",
                                     "cnt_hot", "cnt_sum", "cnt_added"))
        NT = NG // SLOTS
        TG = max(n for n in range(SLOTS, 29, SLOTS) if NG % n == 0)
        USES = TG // SLOTS
        QB = 2 * TG
        with nc.Block() as block:
            @block.vector
            def _(dve):
                nc.vector.memset(sweep0[:, :], 0.0)
                nc.vector.memset(acc[:, :], 0.0)
                nc.vector.memset(f01_raw[:, :], 0.0)

        with nc.Fori(0, sweeps):
            with nc.Block() as block:
                @block.sync
                def _(sp):
                    def load(g, u, p):
                        sp.dma_start(attr[0:p, u, :, :].rearrange("p k f -> p (k f)"),
                                     edge_attr[bass.ds(g * GROUP, p * TILES), :].rearrange("(p k) f -> p (k f)", k=TILES)).then_inc(attr_in[u], 16)

                    with sp.Fori(0, NT - 1) as t:
                        for u in range(SLOTS):
                            sp.wait_ge(attr_placed, t * SLOTS + (u + 1))
                            load(t * SLOTS + u, u, P)
                    for u in range(SLOTS):
                        g = (NT - 1) * SLOTS + u
                        sp.wait_ge(attr_placed, g + 1)
                        if g < GFULL:
                            load(g, u, P)
                        elif g == GFULL and TP:
                            load(g, u, TP)
                        else:
                            load(0, u, P if GFULL else TP)

                @block.gpsimd
                def _(pool):
                    with pool.Fori(0, NT) as t:
                        for u in range(SLOTS):
                            pool.wait_ge(idx_ready[u], t * 2 + 2)
                            pool.wait_ge(group_free[u], t + 1)
                            pool.sem_inc(taken, 1)
                            for k in range(TILES):
                                for c, i in ((0, idx), (D, idd)):
                                    pool.indirect_dma_start(
                                        out=rows[:, u, k, c:c + D], out_offset=None, in_=table,
                                        in_offset=bass.IndirectOffsetOnAxis(ap=i[:, u, k:k + 1], axis=0),
                                    ).then_inc(gathered[u], 16)

                @block.scalar
                def _(act):
                    act.sem_inc(rowsT_ready, START)
                    act.sem_inc(h1T_ready, START)
                    act.sem_inc(h2_ready, START)
                    act.sem_inc(mid_ready, START)

                    def set_indices(t, j):
                        g, u = t * TG + j, j % SLOTS
                        act.wait_ge(group_free[u], t * USES + (j // SLOTS + 1))
                        nc.scalar.activation(idd[:, u, :], dst_f[:, bass.ds(g, 1), :].rearrange("p a k -> p (a k)"), ACT.Relu).then_inc(idx_ready[u], 1)
                        nc.scalar.copy(idx[:, u, :], src_i[:, bass.ds(g, 1), :].rearrange("p a k -> p (a k)")).then_inc(idx_ready[u], 1)

                    for u in range(SLOTS):
                        set_indices(0, u)
                    with act.Fori(0, NG // TG) as t:
                        for i in range(QB + 3):
                            if i >= 2 and i % 2 == 0 and i <= QB:
                                set_indices(t, i // 2 - 1 + SLOTS)
                            if i < QB:
                                q = t * QB + i
                                act.wait_ge(transposed, q + START + 1)
                                act.wait_ge(lin1, q + START - 1)
                                nc.scalar.copy(rowsT[0:KE, i % 2, :], psT[0:KE, :]).then_inc(rowsT_ready, 1)
                            if 1 <= i <= QB:
                                q, j = t * QB + i - 1, (i - 1) % 2
                                act.wait_ge(lin1, q + START + 1)
                                act.wait_ge(lin2, q + START - 1)
                                nc.scalar.activation(h1T[:, j, :], ps1[:, :], ACT.Relu, bias=b1_c[:, 0:1]).then_inc(h1T_ready, 1)
                            if 2 <= i <= QB + 1:
                                q, j = t * QB + i - 2, i % 2
                                act.wait_ge(h2pre_ready, q + START + 1)
                                act.wait_ge(parts_ready, q + START)
                                act.wait_ge(summed_q, q + START - 1)
                                nc.scalar.activation(h2[:, :, :], h2pre, ACT.Relu)
                                nc.scalar.activation(parts[:, j, :, 0:H], h2pre, ACT.Relu).then_inc(h2_ready, 1)
                                act.wait_ge(rest_ready, q + START + 1)
                                nc.scalar.copy(parts[:, j, :, H:2 * H], h2[:, :, :]).then_inc(mid_ready, 1)

                @block.vector
                def _(dve):
                    dve.sem_inc(h2pre_ready, START)
                    dve.sem_inc(rest_ready, START)
                    dve.sem_inc(parts_ready, START)
                    dve.sem_inc(added, START)
                    dve.sem_inc(attr_placed, SLOTS)
                    dve.sem_inc(cnt_hot, START)
                    dve.sem_inc(cnt_added, START)
                    nc.vector.tensor_scalar(base[:, :], base0[:, :], sweep0[:, 0:1], None, ALU.add).then_inc(window, 1)
                    dve.wait_ge(window, 1)
                    nc.vector.tensor_scalar(base_blk[:, :], base[0:1, :], 1.0 / P, None, ALU.mult).then_inc(window, 1)
                    nc.vector.tensor_scalar(sweep0[:, :], sweep0[:, :], float(WIN), None, ALU.add).then_inc(window, 1)
                    nc.vector.memset(outdeg[:, :], 0.0).then_inc(window, 1)
                    nc.vector.memset(parts[:, :, :, 3 * H:3 * H + 1], 1.0).then_inc(window, 1)
                    dve.wait_ge(window, 5)

                    with dve.Fori(0, NG // TG) as t:
                        for i in range(QB + 4):
                            if i < QB and i % 2 == 0:
                                u = i // 2 % SLOTS
                                g = t * TG + i // 2
                                uses = t * USES + i // 2 // SLOTS
                                dve.wait_ge(attr_in[u], uses * 16 + 16)
                                dve.wait_ge(group_free[u], uses + 1)
                                nc.vector.tensor_copy(rows[:, u, :, 2 * D:KE], attr[:, u, :, :]).then_inc(attr_placed, 1)
                                nc.vector.tensor_scalar(dloc[:, u, :], dst_f[:, bass.ds(g, 1), :].rearrange("p a k -> p (a k)"),
                                                        base[:, bass.ds(g, 1)], None, ALU.subtract).then_inc(step, 1)
                                nc.vector.tensor_copy(lol[:, u, :], src_lo[:, bass.ds(g, 1), :].rearrange("p a k -> p (a k)")).then_inc(step, 1)
                                nc.vector.tensor_copy(hil[:, u, :], src_hi[:, bass.ds(g, 1), :].rearrange("p a k -> p (a k)")).then_inc(step, 1)
                                dve.wait_ge(step, g * 3 + 3)
                            if 2 <= i <= QB + 1:
                                q, j = t * QB + i - 2, i % 2
                                dve.wait_ge(lin2, q + START + 1)
                                dve.wait_ge(h2_ready, q + START)
                                nc.vector.tensor_tensor(h2pre, ps2.rearrange("p (k f) -> p k f", k=HALF),
                                                        b2_r[:, :].unsqueeze(1).broadcast_to([P, HALF, H]), ALU.add).then_inc(h2pre_ready, 1)
                            if i < QB:
                                g, u = t * TG + i // 2, i // 2 % SLOTS
                                if i % 2 == 0:
                                    for k in range(TILES):
                                        m = nc.vector.tensor_scalar(onehot_b[:, u, k, :], iota_ps[:, :], dloc[:, u, k:k + 1], None, ALU.is_equal)
                                    m.then_inc(hot_ready, 1)
                                else:
                                    dve.wait_ge(cnt_sum, g + (START - 1))
                                    for k in range(TILES):
                                        nc.vector.tensor_scalar(hotsrc[:, i // 2 % 2, k, 0, :], iota_ps[:, 0:P], lol[:, u, k:k + 1], None, ALU.is_equal)
                                        m = nc.vector.tensor_scalar(hotsrc[:, i // 2 % 2, k, 1, :], iota_ps[:, 0:P], hil[:, u, k:k + 1], None, ALU.is_equal)
                                    m.then_inc(cnt_hot, 1)
                            if 2 <= i <= QB + 1:
                                dve.wait_ge(h2_ready, q + START + 1)
                                nc.vector.tensor_tensor(h2, h2, parts[:, j, :, 0:H], ALU.subtract).then_inc(rest_ready, 1)
                            if i >= 4 and i % 2 == 0:
                                g = t * TG + (i - 4) // 2
                                blk = dve.value_load(base_blk[0:1, bass.ds(g, 1)], min_val=0, max_val=NB - 1)
                                here = acc[:, bass.ds(blk * HC, 2 * HC)].rearrange("p (a f) -> p a f", a=2)
                                dve.wait_ge(summed_q, g * 2 + (START + 2))
                                for c, (lo, hi) in enumerate(((0, H), (H, 2 * H), (2 * H, 3 * H + 1))):
                                    dve.wait_ge(added, g * 3 + (c + START))
                                    o = HC - (hi - lo) if c == 2 else 0
                                    nc.vector.tensor_tensor(here[:, :, o:o + hi - lo], here[:, :, o:o + hi - lo], sums[:, :, lo:hi], ALU.add).then_inc(added, 1)
                            if 3 <= i <= QB + 1 and i % 2:
                                g = t * TG + (i - 3) // 2
                                dve.wait_ge(cnt_sum, g + (START + 1))
                                dve.wait_ge(cnt_added, g + START)
                                nc.vector.tensor_tensor(outdeg[:, :], outdeg[:, :], cnt_ps[:, 0:NB], ALU.add).then_inc(cnt_added, 1)
                            if 2 <= i <= QB + 1:
                                dve.wait_ge(mid_ready, q + START + 1)
                                nc.vector.tensor_tensor(parts[:, j, :, 2 * H:3 * H], h2, parts[:, j, :, H:2 * H], ALU.subtract).then_inc(parts_ready, 1)

                @block.tensor
                def _(pe):
                    pe.sem_inc(transposed, START)
                    pe.sem_inc(lin1, START)
                    pe.sem_inc(lin2, START)
                    pe.sem_inc(summed_q, START)
                    pe.sem_inc(cnt_sum, START)
                    for u in range(SLOTS):
                        pe.sem_inc(group_free[u], 1)
                    with pe.Fori(0, NG // TG) as t:
                        for i in range(QB + 3):
                            if i < QB:
                                q, u, k0 = t * QB + i, i // 2 % SLOTS, HALF * (i % 2)
                                if i % 2 == 0:
                                    pe.wait_ge(gathered[u], t * (USES * 32 * TILES) + (i // 2 // SLOTS + 1) * 32 * TILES)
                                    pe.wait_ge(attr_placed, t * TG + (i // 2 + SLOTS + 1))
                                pe.wait_ge(rowsT_ready, q + START)
                                for k in range(HALF):
                                    m = nc.tensor.transpose(psT[0:KE, k * P:(k + 1) * P], rows[:, u, k0 + k, :], ident[:, :])
                                m.then_inc(transposed, 1)
                                if i % 2 == 1:
                                    pe.wait_ge(transposed, q + START + 1)
                                    pe.sem_inc(group_free[u], 1)
                            if 1 <= i <= QB:
                                q, j = t * QB + i - 1, (i - 1) % 2
                                pe.wait_ge(rowsT_ready, q + START + 1)
                                pe.wait_ge(h1T_ready, q + START)
                                nc.tensor.matmul(ps1[:, :], W1_s[:, :], rowsT[0:KE, j, :], start=True, stop=True).then_inc(lin1, 1)
                            if 2 <= i <= QB + 1:
                                q, j = t * QB + i - 2, i % 2
                                pe.wait_ge(h1T_ready, q + START + 1)
                                pe.wait_ge(h2pre_ready, q + START)
                                for k in range(HALF):
                                    m = nc.tensor.matmul(ps2[:, k * H:(k + 1) * H], h1T[:, j, k * P:(k + 1) * P], W2_s[:, :], start=True, stop=True)
                                m.then_inc(lin2, 1)
                            if 3 <= i <= QB + 2:
                                q, u, j, k0 = t * QB + i - 3, (i - 3) // 2 % SLOTS, (i - 3) % 2, HALF * ((i - 3) % 2)
                                if j == 0:
                                    g = t * TG + (i - 3) // 2
                                    pe.wait_ge(hot_ready, g + 1)
                                    pe.wait_ge(added, g * 3 + START)
                                pe.wait_ge(parts_ready, q + START + 1)
                                for k in range(HALF):
                                    for h in range(2):
                                        m = nc.tensor.matmul(sums[:, h, 0:PARTS], onehot_b[:, u, k0 + k, h * P:(h + 1) * P], parts[:, j, k, :],
                                                             start=k0 + k == 0, stop=k0 + k == TILES - 1)
                                m.then_inc(summed_q, 1)
                            if 2 <= i <= QB and i % 2 == 0:
                                g, v = t * TG + i // 2 - 1, (i // 2 - 1) % 2
                                pe.wait_ge(cnt_hot, g + (START + 1))
                                pe.wait_ge(cnt_added, g + START)
                                for k in range(TILES):
                                    m = nc.tensor.matmul(cnt_ps[:, 0:NB], hotsrc[:, v, k, 0, :], hotsrc[:, v, k, 1, 0:NB],
                                                         start=k == 0, stop=k == TILES - 1)
                                m.then_inc(cnt_sum, 1)
            clear([*attr_in, *idx_ready, *group_free, transposed, rowsT_ready, lin1, h1T_ready, lin2, h2pre_ready, h2_ready,
                   rest_ready, mid_ready, parts_ready, hot_ready, summed_q, added, step, window, taken, attr_placed,
                   cnt_hot, cnt_sum, cnt_added], gathered)


        CH = next(c for c in (7, 5, 4, 3, 2, 1) if NB % c == 0)

        def node_linear(width, frm, weight, to):
            stage = work[:, 0:CH * width].rearrange("p (c f) -> p c f", c=CH)
            stageT = work[0:width, 1024:1024 + CH * P]
            taken_pe = sem("linear_taken")
            staged, turned, kept, mapped, placed = (sem(f"linear_{n}") for n in ("staged", "turned", "kept", "mapped", "placed"))
            F = min(CH, 4)
            with nc.Block() as block:
                @block.vector
                def _(dve):
                    with dve.Fori(0, NB // CH) as c:
                        nc.vector.tensor_copy(stage, frm(c * CH, CH)).then_inc(staged, 1)
                        dve.wait_ge(mapped, c + 1)
                        nc.vector.tensor_copy(to(c * CH, CH), ps[0][:, 0, 0:CH * D].rearrange("p (c f) -> p c f", c=CH)).then_inc(placed, 1)

                @block.tensor
                def _(pe):
                    pe.sem_inc(placed, 1)
                    with pe.Fori(0, NB // CH) as c:
                        pe.wait_ge(staged, c + 1)
                        pe.sem_inc(taken_pe, 1)
                        for b in range(CH):
                            m = nc.tensor.transpose(ps[1][0:width, b // 4, b % 4 * P:(b % 4 + 1) * P], stage[:, b, :], ident[:, :])
                        m.then_inc(turned, 1)
                        pe.wait_ge(kept, c + 1)
                        pe.wait_ge(placed, c + 1)
                        for b in range(CH):
                            m = nc.tensor.matmul(ps[0][:, 0, b * D:(b + 1) * D], stageT[:, b * P:(b + 1) * P], weight[:, :], start=True, stop=True)
                        m.then_inc(mapped, 1)

                @block.scalar
                def _(act):
                    with act.Fori(0, NB // CH) as c:
                        act.wait_ge(turned, c + 1)
                        m = nc.scalar.copy(stageT[:, 0:F * P], ps[1][0:width, 0, 0:F * P])
                        if CH > F:
                            m = nc.scalar.copy(stageT[:, F * P:CH * P], ps[1][0:width, 1, 0:(CH - F) * P])
                        m.then_inc(kept, 1)
            clear([staged, turned, kept, mapped, placed, taken_pe])

        wide = [P, NB, D]

        def steps(body):
            step, asked, rooted = sem("steps_step"), sem("steps_asked"), sem("steps_rooted")
            roots = []
            with nc.Block() as block:
                @block.vector
                def _(dve):
                    n = [0]

                    def link(ins):
                        n[0] += 1
                        ins.then_inc(step, 1)
                        dve.wait_ge(step, n[0])

                    def root(v):
                        roots.append((n[0], v))
                        dve.sem_inc(asked, 1)
                        dve.wait_ge(rooted, len(roots))
                        link(nc.vector.reciprocal(v, v))

                    body(link, root)

                @block.scalar
                def _(act):
                    for i, (at, v) in enumerate(roots):
                        act.wait_ge(asked, i + 1)
                        act.wait_ge(step, at)
                        nc.scalar.activation(v, v, ACT.Sqrt).then_inc(rooted, 1)
            clear([step, asked, rooted])

        acc1 = acc[:, 0:NB * HC].rearrange("p (b f) -> p b f", f=HC)
        c1 = sb("c1", [P, NB])
        c2 = sb("c2", [P, NB])
        steps(lambda link, root: link(nc.vector.tensor_copy(indeg[:, :], acc1[:, :, H])))
        node_linear(H, lambda b, n: acc1[:, bass.ds(b, n), 0:H], W3_s, lambda b, n: f01[:, bass.ds(b, n), :])

        def over(v):
            return v.unsqueeze(2).broadcast_to(wide)

        def along(v):
            return v.unsqueeze(1).broadcast_to(wide)

        def l1_out(link, root):
            link(nc.vector.tensor_tensor(tmp, over(indeg[:, :]), along(b3_r[:, :]), ALU.mult))
            link(nc.vector.tensor_tensor(f01, f01, tmp, ALU.add))
            link(nc.vector.tensor_scalar(c1[:, :], indeg[:, :], 1.0, None, ALU.max))
            link(nc.vector.reciprocal(c1[:, :], c1[:, :]))
            link(nc.vector.tensor_tensor(f01, f01, over(c1[:, :]), ALU.mult))
            link(nc.vector.tensor_tensor(f01, f01, xc[:, :, :], ALU.add))

        steps(l1_out)
        layernorm(f01, xc[:, :, :])

        def l2_in(link, root):
            link(nc.vector.tensor_scalar(c1[:, :], outdeg[:, :], 1.0, None, ALU.max))
            root(c1[:, :])
            link(nc.vector.tensor_tensor(tmp, xc[:, :, :], over(c1[:, :]), ALU.mult))
            link(nc.vector.memset(acc[:, 0:(NB + 1) * D], 0.0))
            link(nc.vector.memset(sweep0[:, :], 0.0))

        steps(l2_in)
        store_table(tmp)
        aggregate(False)

        def l2_mid(link, root):
            link(nc.vector.tensor_scalar(c1[:, :], indeg[:, :], 1.0, None, ALU.max))
            root(c1[:, :])
            link(nc.vector.tensor_scalar(c2[:, :], indeg[:, :], 0.5, None, ALU.is_lt))
            link(nc.vector.tensor_tensor(accD, accD, over(c1[:, :]), ALU.mult))
            link(nc.vector.tensor_tensor(tmp, xc[:, :, :], over(c2[:, :]), ALU.mult))
            link(nc.vector.tensor_tensor(tmp, tmp, accD, ALU.add))

        steps(l2_mid)
        node_linear(D, lambda b, n: tmp[:, bass.ds(b, n), :], L2_t, lambda b, n: f01[:, bass.ds(b, n), :])

        def l2_out(link, root):
            link(nc.vector.tensor_tensor(f01, f01, along(l2b_r[:, :]), ALU.add))
            link(nc.vector.tensor_scalar(f01, f01, 0.0, None, ALU.max))

        steps(l2_out)
        layernorm(f01, xc[:, :, :])

        node_linear(D, lambda b, n: xc[:, bass.ds(b, n), :], L3_s, lambda b, n: f01[:, bass.ds(b, n), :])

        def l3_in(link, root):
            link(nc.vector.tensor_scalar(c2[:, :], indeg[:, :], 1.0, None, ALU.add))
            root(c2[:, :])
            link(nc.vector.tensor_tensor(accD, f01, over(c2[:, :]), ALU.mult))
            link(nc.vector.memset(acc[:, NB * D:(NB + 1) * D], 0.0))
            link(nc.vector.memset(sweep0[:, :], 0.0))

        steps(l3_in)
        store_table(accD)
        aggregate(False)

        fsum, fvar = sb("fsum", [P, D]), sb("fvar", [P, D])

        def column_sums(i, part):
            with nc.Block() as block:
                @block.tensor
                def _(pe):
                    nc.tensor.matmul(ps[i][:, 0, 0:D], ones[:, :], part[:, :], start=True, stop=True)

        def bn_mean(link, root):
            link(nc.vector.tensor_tensor(accD, accD, over(c2[:, :]), ALU.mult))
            link(nc.vector.tensor_tensor(accD, accD, along(l3b_r[:, :]), ALU.add))
            link(nc.vector.tensor_scalar(accD[:, NB - 1, :], accD[:, NB - 1, :], valid[:, 0:1], None, ALU.mult))
            link(nc.vector.tensor_reduce(fsum[:, :], accD.rearrange("p b f -> p f b"), AX, ALU.add))

        def bn_var(link, root):
            link(nc.vector.tensor_scalar(fsum[:, :], ps[0][:, 0, 0:D], 1.0 / N, None, ALU.mult))
            link(nc.vector.tensor_tensor(accD, accD, along(fsum[:, :]), ALU.subtract))
            link(nc.vector.tensor_scalar(accD[:, NB - 1, :], accD[:, NB - 1, :], valid[:, 0:1], None, ALU.mult))
            link(nc.vector.tensor_tensor(tmp, accD, accD, ALU.mult))
            link(nc.vector.tensor_reduce(fvar[:, :], tmp.rearrange("p b f -> p f b"), AX, ALU.add))

        def bn_out(link, root):
            link(nc.vector.tensor_scalar(fvar[:, :], ps[1][:, 0, 0:D], 1.0 / N, EPS, ALU.mult, ALU.add))
            root(fvar[:, :])
            link(nc.vector.tensor_tensor(fvar[:, :], fvar[:, :], gam_r[:, :], ALU.mult))
            link(nc.vector.tensor_tensor(accD, accD, along(fvar[:, :]), ALU.mult))
            link(nc.vector.tensor_tensor(accD, accD, along(bet_r[:, :]), ALU.add))
            link(nc.vector.tensor_scalar(accD, accD, 0.0, None, ALU.max))

        steps(bn_mean)
        column_sums(0, fsum)
        steps(bn_var)
        column_sums(1, fvar)
        steps(bn_out)
        layernorm(accD, xc[:, :, :])

        store = sem("out_stored")
        with nc.Block() as block:
            @block.sync
            def _(sp):
                sp.dma_start(out[0:NFULL * P, :].rearrange("(b p) f -> p b f", p=P), xc[:, 0:NFULL, :]).then_inc(store, 16)
                if NREST:
                    sp.dma_start(out[NFULL * P:N, :], xc[0:NREST, NFULL, :]).then_inc(store, 16)
                sp.wait_ge(store, 32 if NREST else 16)


_INS = ["x", "src", "dst", "edge_attr_16", "edge_weight", "L1_gnn_W1", "L1_gnn_b1", "L1_gnn_W2", "L1_gnn_b2",
        "L1_gnn_W3", "L1_gnn_b3", "L2_gnn_W", "L2_gnn_b", "L3_gnn_W", "L3_gnn_b", "L3_gnn_gamma", "L3_gnn_beta"]


def kernel(**inputs):
    import numpy as np
    import concourse.bacc as bacc
    from concourse import mybir as mb
    from concourse.bass_utils import run_bass_kernel_spmd

    nc = bacc.Bacc("TRN2", target_bir_lowering=False, num_devices=1)
    arrays, args = {}, []
    for name in _INS:
        a = np.ascontiguousarray(inputs[name])
        arrays[f"in_{name}"] = a
        args.append(nc.dram_tensor(f"in_{name}", a.shape, mb.dt.from_np(a.dtype), kind="ExternalInput").ap())
    out = nc.dram_tensor("out", inputs["x"].shape, mb.dt.float32, kind="ExternalOutput").ap()
    build(nc, *args, out)
    return run_bass_kernel_spmd(nc, [arrays], core_ids=[0]).results[0]["out"]
```

```python
from contextlib import ExitStack

import concourse.bass as bass
from concourse import mybir

P = 128
TILES = 8
SLOTS = 4
GROUP = P * TILES
WIN = 2 * P
F32 = mybir.dt.float32
BF16 = mybir.dt.bfloat16
I32 = mybir.dt.int32
ALU = mybir.AluOpType
ACT = mybir.ActivationFunctionType
AX = mybir.AxisListType.X
HOPS = 10
START = 4
HC2 = 64
ALPHA = 0.1
FIRST = 1024.0
EPS = 1e-5


def build(nc, x, src, dst, edge_attr, edge_weight, W1, b1, W2, b2, W3, b3, L2_W, L2_b,
          L3_W, L3_b, gamma, beta, out):
    N, D = x.shape
    E = src.shape[0]
    DE = edge_attr.shape[1]
    H = W2.shape[0]
    KS = D + DE
    NB = -(-N // P)
    NFULL = N // P
    NREST = N - NFULL * P
    GFULL = E // GROUP
    EREST = E - GFULL * GROUP
    TP = EREST // TILES
    NG = -(-E // GROUP)
    NG += -NG % SLOTS
    WINDOWS = -(-NB // 2)
    SUP = 512
    GPS = 12
    SUPS = next(n for n in range(2, 99, 2) if (NG - GPS * n) * GROUP * N // E + 100 <= SUP * n)
    DG = NG - GPS * SUPS
    CHB = 7
    CPS = NB // CHB
    RING = 4
    assert NB % CHB == 0 and 2 * CPS % RING == 0 and DG > 0 and DG % SLOTS == 0
    DENSE = SUPS * P * NB * SUP
    FILLS = SUPS * CPS
    FTURNS = max(n for n in range(1, NG // SLOTS // 3 + 1) if FILLS % n == 0)
    SPT = next(n for n in range(1, DG * TILES + 1) if DG * TILES % n == 0 and DG * TILES // n <= NG // SLOTS - FTURNS - 1)
    CTURNS = DG * TILES // SPT
    assert DENSE % P == 0 and DG <= GFULL
    HALF = TILES // 2
    HC = H + 1
    assert EREST % TILES == 0

    ctx = ExitStack()
    with ctx:
        def sb(name, shape, dt=F32):
            return ctx.enter_context(nc.sbuf_tensor(name, shape, dt))

        def pb(name, shape, dt=F32):
            return ctx.enter_context(nc.psum_tensor(name, shape, dt))

        sems_by_name = {}

        def sem(name):
            if name not in sems_by_name:
                sems_by_name[name] = ctx.enter_context(nc.semaphore(name))
            return sems_by_name[name]

        src_i = sb("src_i", [P, NG + SLOTS, TILES], I32)
        dst_f = sb("dst_f", [P, NG + SLOTS, TILES])
        wgt = sb("wgt", [P, NG + 1, TILES])
        base0 = sb("base0", [P, NG + 1])
        base = sb("base", [P, NG + 1])
        base_blk = sb("base_blk", [1, NG + 1], I32)
        sweep0 = sb("sweep0", [P, 1])
        near = sb("near", [P, 1])
        sweeps_i = sb("sweeps_i", [1, 2], I32)
        addr = sb("addr", [P, DG, TILES], I32)
        times = sb("times", [P, DG, TILES])
        mask = sb("mask", [P, 4], I32)
        xc_raw = sb("xc", [P, (NB + 1) * D])
        xc = xc_raw[:, 0:NB * D].rearrange("p (b f) -> p b f", f=D)
        tmp_raw = sb("tmp", [P, max(NB * D, 2 * 2 * HALF * P + 2 * HALF * P + HALF * (3 * H + 1) + 2 * P, 2 * CHB * SUP + SUP)])
        tmp = tmp_raw[:, 0:NB * D].rearrange("p (b f) -> p b f", f=D)
        acc = sb("acc", [P, max((NB + 1) * HC, (NB + 1) * D + 2 * CHB * SUP)])
        indeg = sb("indeg", [P, NB])
        outdeg = sb("outdeg", [P, NB])
        f01_raw = sb("f01", [P, max(NB * D, SLOTS * TILES * (KS + DE) + 2 * HALF * P + SLOTS * 3 * D)])
        f01 = f01_raw[:, 0:NB * D].rearrange("p (b f) -> p b f", f=D)
        idx = sb("idx", [P, SLOTS, TILES], I32)
        parts48 = sb("parts48", [P, SLOTS, TILES, 3 * D], BF16)
        lol = sb("lol", [P, SLOTS, TILES])
        hil = sb("hil", [P, SLOTS, TILES])
        dloc = sb("dloc", [P, SLOTS, TILES])
        wl = sb("wl", [P, SLOTS, TILES])
        onehot_b = sb("onehot", [P, SLOTS, TILES, WIN], BF16)
        msg = sb("msg", [P, SLOTS, TILES, D])
        src_lo = sb("src_lo", [P, NG + 1, TILES])
        src_hi = sb("src_hi", [P, NG + 1, TILES])
        past_i = sb("past_i", [P, 1], I32)
        rank = sb("rank", [P, P])
        valid = sb("valid", [P, 1])
        work = onehot_b[:, :, :, :].rearrange("p u k n -> p (u k n)").bitcast(F32)
        iota_i = sb("iota_i", [P, WIN], I32)
        iota = sb("iota", [P, WIN])
        row_i = sb("row_i", [P, 1], I32)
        row = sb("row", [P, 1])
        ident = sb("ident", [P, P])
        ones = sb("ones", [P, P])

        ps = [pb(f"ps{i}", [P, 2, 512]) for i in range(3)]
        spare = pb("spare", [P, 512])
        misc = pb("misc", [P, 512])
        psD, psDT = ps[2][:, 0, :], ps[2][:, 1, :]
        sums, psT, ps1, ps2 = ps[0], ps[1][:, 0, :], ps[1][:, 1, :], ps[2][:, 0, :]
        cnt_ps = spare[:, 0:P]
        iota_ps = misc[:, 0:WIN]

        table = nc.dram_tensor("node_table", (NB * P, D), F32).ap()
        dense = nc.dram_tensor("dense", (DENSE + P, 1), F32).ap()
        dense_v = dense[0:DENSE, :].rearrange("(b p s f) a -> b p (s f a)", b=SUPS, p=P, s=NB)
        dense_z = dense[0:DENSE, :].rearrange("(c p f) a -> c p (f a)", c=FILLS, p=P)
        table_v = table.rearrange("(p b) f -> p b f", p=P)

        def clear(sems, gathers=()):
            for s in gathers:
                nc.gpsimd.dma_reset(range(s.num, s.num + 1))
            if gathers:
                nc.all_engine_barrier()
            for s in [*sems, *gathers]:
                nc.sync.sem_clear(s)
            nc.all_engine_barrier()

        def onehots(to, which):
            return nc.vector.tensor_tensor(to, iota_ps[:, 0:to.shape[2]].unsqueeze(1).broadcast_to(to.shape),
                                           which.unsqueeze(2).broadcast_to(to.shape), ALU.is_equal)

        def slot_sems(name):
            return [sem(f"{name}{u}") for u in range(SLOTS)]

        def load_nodes(eng, to, frm, done):
            n = 0
            eng.dma_start(to[:, 0:NFULL, :], frm[0:NFULL * P, :].rearrange("(b p) f -> p b f", p=P)).then_inc(done, 16)
            n += 16
            if NREST:
                eng.dma_start(to[0:NREST, NFULL, :], frm[NFULL * P:N, :]).then_inc(done, 16)
                n += 16
            return n

        i_zero, i_src, i_x, i_dst, i_wgt, i_const, i_chk, i_iota = (
            sem(n) for n in ("prep_zeroed", "src_in", "x_in", "dst_in", "wgt_in", "prep_const",
                             "prep_check", "prep_iota"))
        i_step, i_sum, i_tab = sem("prep_step"), sem("prep_sum"), sem("table_stored")
        with nc.Block() as block:
            dst_i = acc[:, 0:(NG + 1) * TILES].bitcast(I32).rearrange("p (g k) -> p g k", k=TILES)
            first_i = work[:, 2048:2048 + NG + 1].bitcast(I32)
            first_f = work[:, 3072:3072 + NG + 1]
            chk = sb("chk", [P, 8])

            @block.sync
            def _(sp):
                sp.wait_ge(i_zero, 4)
                for arr, dr, s in ((src_i, src, i_src), (dst_i, dst, i_dst), (wgt, edge_weight, i_wgt)):
                    sp.dma_start(arr[:, 0:GFULL, :], dr[0:GFULL * GROUP].rearrange("(g p k) -> p g k", p=P, k=TILES)).then_inc(s, 16)
                    if TP:
                        sp.dma_start(arr[0:TP, GFULL, :], dr[GFULL * GROUP:E].rearrange("(p k) -> p k", k=TILES)).then_inc(s, 16)
                load_nodes(sp, xc, x, i_x)

            LOADS = 32 if TP else 16
            XLOADS = 32 if NREST else 16

            @block.scalar
            def _(act):
                act.wait_ge(i_x, XLOADS)
                act.dma_start(table_v, xc[:, :, :]).then_inc(i_tab, 16)
                act.wait_ge(i_tab, 16)

            @block.gpsimd
            def _(pool):
                nc.gpsimd.iota(iota_i[:, :], [[1, WIN]], 0, 0).then_inc(i_iota, 1)
                nc.gpsimd.iota(row_i[:, :], [[0, 1]], 0, 1).then_inc(i_iota, 1)

            @block.vector
            def _(dve):
                nc.vector.memset(src_i[:, GFULL:NG + SLOTS, :], 0).then_inc(i_zero, 1)
                nc.vector.memset(dst_i[:, GFULL:NG + 1, :], -1).then_inc(i_zero, 1)
                nc.vector.memset(wgt[:, GFULL:NG + 1, :], 0.0).then_inc(i_zero, 1)
                nc.vector.memset(xc_raw[:, (NB - 1) * D:(NB + 1) * D], 0.0).then_inc(i_zero, 1)
                n = [0]

                def link(ins):
                    n[0] += 1
                    ins.then_inc(i_step, 1)
                    dve.wait_ge(i_step, n[0])

                link(nc.vector.memset(chk[:, :], 0.0))
                dve.wait_ge(i_iota, 2)
                link(nc.vector.tensor_copy(iota[:, :], iota_i[:, :]))
                link(nc.vector.tensor_copy(iota_ps[:, :], iota_i[:, :]))
                link(nc.vector.tensor_copy(row[:, :], row_i[:, :]))
                link(nc.vector.tensor_scalar(ident[:, :], iota[:, 0:P], row[:, 0:1], None, ALU.is_equal))
                dve.wait_ge(i_dst, LOADS)
                link(nc.vector.tensor_scalar(first_i[0:1, :], dst_i[0:1, :, 0], -P, None, ALU.bitwise_and))
                link(nc.vector.tensor_scalar(first_f[0:1, :], first_i[0:1, :], 0.0, None, ALU.max))
                nc.vector.memset(ones[:, :], 1.0).then_inc(i_const, 1)
                dve.wait_ge(i_sum, 1)
                link(nc.vector.tensor_copy(base0[:, :], ps[1][:, 0, 0:NG + 1]))
                link(nc.vector.memset(dst_f[:, NG:NG + SLOTS, :], -1.0))
                link(nc.vector.tensor_copy(dst_f[:, 0:NG + 1, :], dst_i))
                off = work[:, 0:(NG + 1) * TILES].rearrange("p (g k) -> p g k", k=TILES)
                link(nc.vector.tensor_tensor(off, dst_f[:, 0:NG + 1, :], base0[:, :].unsqueeze(2).broadcast_to([P, NG + 1, TILES]), ALU.subtract))
                if GFULL:
                    full = off[:, 0:GFULL, :].rearrange("p g k -> p (g k)")
                    link(nc.vector.tensor_reduce(chk[:, 0:1], full, AX, ALU.max))
                    link(nc.vector.tensor_reduce(chk[:, 1:2], full, AX, ALU.min))
                if TP:
                    link(nc.vector.tensor_reduce(chk[0:TP, 2:3], off[0:TP, GFULL, :], AX, ALU.max))
                    link(nc.vector.tensor_reduce(chk[0:TP, 3:4], off[0:TP, GFULL, :], AX, ALU.min))
                link(nc.vector.tensor_tensor(chk[:, 4:5], chk[:, 0:1], chk[:, 2:3], ALU.max))
                link(nc.vector.tensor_tensor(chk[:, 5:6], chk[:, 1:2], chk[:, 3:4], ALU.min))
                link(nc.vector.tensor_scalar(chk[:, 4:5], chk[:, 4:5], float(WIN) - 0.5, None, ALU.is_gt))
                link(nc.vector.tensor_scalar(chk[:, 5:6], chk[:, 5:6], -0.5, None, ALU.is_lt))
                link(nc.vector.tensor_reduce(chk[:, 7:8], dst_f[:, 0:DG, :].rearrange("p g k -> p (g k)"), AX, ALU.max))
                link(nc.vector.tensor_scalar(chk[:, 7:8], chk[:, 7:8], float(SUPS * SUP) - 0.5, None, ALU.is_gt))
                nc.vector.tensor_tensor(chk[:, 6:7], chk[:, 4:5], chk[:, 5:6], ALU.add).then_inc(i_chk, 1)
                dve.wait_ge(i_sum, 2)
                link(nc.vector.tensor_scalar(near[:, :], ps[0][:, 0, 0:1], 0.5, None, ALU.is_lt))
                link(nc.vector.tensor_scalar(chk[0:1, 7:8], near[0:1, 0:1], float(1 - WINDOWS), float(WINDOWS), ALU.mult, ALU.add))
                link(nc.vector.tensor_copy(sweeps_i[:, 0:1], chk[0:1, 7:8]))
                link(nc.vector.tensor_scalar(chk[0:1, 6:7], ps[0][0:1, 0, 1:2], 0.5, None, ALU.is_lt))
                link(nc.vector.tensor_tensor(sweeps_i[:, 1:2], chk[0:1, 6:7], near[0:1, 0:1], ALU.mult))
                link(nc.vector.tensor_scalar(chk[:, 5:6], ps[0][:, 0, 1:2], 0.5, None, ALU.is_lt))
                link(nc.vector.tensor_tensor(chk[:, 5:6], chk[:, 5:6], near[:, 0:1], ALU.mult))
                link(nc.vector.tensor_scalar(mask[:, 0:1], chk[:, 5:6], -1.0, None, ALU.mult))
                link(nc.vector.tensor_scalar(mask[:, 1:2], chk[:, 5:6], -1.0, None, ALU.add))
                link(nc.vector.tensor_scalar(base0[:, :], base0[:, :], near[:, 0:1], None, ALU.mult))
                dve.wait_ge(i_wgt, LOADS)
                link(nc.vector.tensor_scalar(wgt[:, :, :], wgt[:, :, :], 1.0 - ALPHA, None, ALU.mult))
                dve.wait_ge(i_x, XLOADS)
                link(nc.vector.tensor_scalar(f01[:, :, :], xc[:, :, :], ALPHA, None, ALU.mult))
                dve.wait_ge(i_src, LOADS)
                lo_i = acc[:, 0:(NG + 1) * TILES].bitcast(I32).rearrange("p (g k) -> p g k", k=TILES)
                link(nc.vector.tensor_scalar(lo_i, src_i[:, 0:NG + 1, :], P - 1, None, ALU.bitwise_and))
                link(nc.vector.tensor_copy(src_lo[:, :, :], lo_i))
                link(nc.vector.memset(src_hi[:, GFULL:NG + 1, :], -1.0))
                for g, p in ((slice(0, GFULL), P), (slice(GFULL, GFULL + 1), TP)):
                    if p and (g.stop > g.start):
                        link(nc.vector.tensor_tensor(src_hi[0:p, g, :], src_i[0:p, g, :], src_lo[0:p, g, :], ALU.subtract))
                        link(nc.vector.tensor_scalar(src_hi[0:p, g, :], src_hi[0:p, g, :], 1.0 / P, None, ALU.mult))
                        link(nc.vector.scalar_tensor_tensor(src_i[0:p, g, :], src_lo[0:p, g, :], float(NB), src_hi[0:p, g, :], ALU.mult, ALU.add))
                shape = [P, DG, TILES]
                a_i = work[:, 0:DG * TILES].bitcast(I32).rearrange("p (g k) -> p g k", k=TILES)
                a_f = work[:, 1024:1024 + DG * TILES].rearrange("p (g k) -> p g k", k=TILES)
                d_i = work[:, 2048:2048 + DG * TILES].bitcast(I32).rearrange("p (g k) -> p g k", k=TILES)
                link(nc.vector.tensor_copy(d_i, dst_f[:, 0:DG, :]))
                link(nc.vector.tensor_scalar(a_i, d_i, 9, None, ALU.arith_shift_right))
                link(nc.vector.tensor_copy(a_f, a_i))
                link(nc.vector.scalar_tensor_tensor(a_f, a_f, float(P), src_lo[:, 0:DG, :], ALU.mult, ALU.add))
                link(nc.vector.scalar_tensor_tensor(a_f, a_f, float(NB), src_hi[:, 0:DG, :], ALU.mult, ALU.add))
                link(nc.vector.tensor_copy(a_i, a_f))
                link(nc.vector.tensor_scalar(a_i, a_i, 9, None, ALU.logical_shift_left))
                link(nc.vector.tensor_scalar(d_i, d_i, SUP - 1, None, ALU.bitwise_and))
                link(nc.vector.tensor_tensor(addr[:, :, :], a_i, d_i, ALU.bitwise_or))
                link(nc.vector.tensor_scalar(past_i[:, :], row_i[:, :], DENSE, None, ALU.bitwise_or))
                link(nc.vector.tensor_tensor(mask[:, 2:3], past_i[:, :], mask[:, 1:2], ALU.bitwise_and))
                link(nc.vector.tensor_tensor(addr[:, :, :], addr[:, :, :], mask[:, 0:1].unsqueeze(2).broadcast_to(shape), ALU.bitwise_and))
                link(nc.vector.tensor_tensor(addr[:, :, :], addr[:, :, :], mask[:, 2:3].unsqueeze(2).broadcast_to(shape), ALU.bitwise_or))
                link(nc.vector.memset(times[:, :, :], 0.0))
                link(nc.vector.tensor_tensor(rank[:, :], iota[:, 0:P], row[:, 0:1].broadcast_to([P, P]), ALU.is_lt))
                link(nc.vector.tensor_scalar(rank[:, :], rank[:, :], FIRST, 1.0, ALU.mult, ALU.add))
                link(nc.vector.tensor_scalar(valid[:, :], row[:, :], float(NREST or P) - 0.5, None, ALU.is_lt))

            @block.tensor
            def _(pe):
                pe.wait_ge(i_const, 1)
                nc.tensor.matmul(ps[1][:, 0, 0:NG + 1], ones[0:1, :], first_f[0:1, :], start=True, stop=True).then_inc(i_sum, 1)
                pe.wait_ge(i_chk, 1)
                nc.tensor.matmul(ps[0][:, 0, 0:2], ones[:, :], chk[:, 6:8], start=True, stop=True).then_inc(i_sum, 1)

        W1_s = sb("W1_s", [P, H])
        ident_b = sb("ident_b", [P, P], BF16)
        W2_s = sb("W2_s", [H, H])
        W3_s = sb("W3_s", [H, D])
        L2_s = sb("L2_s", [D, D])
        L2_t = sb("L2_t", [D, D])
        L3_s = sb("L3_s", [D, D])
        b1_c = sb("b1_c", [H, 1])
        b2_r = sb("b2_r", [P, H])
        b3_r, l2b_r, l3b_r, gam_r, bet_r = (sb(n, [P, D]) for n in ("b3_r", "l2b_r", "l3b_r", "gam_r", "bet_r"))
        par, par_t = sem("params_in"), sem("params_t")
        with nc.Block() as block:
            @block.sync
            def _(sp):
                n = 0
                sp.wait_ge(par_t, 2)
                for lo, a, b in ((0, 0, D), (D, 2 * D, 2 * D + DE), (HC2, D, 2 * D)):
                    sp.dma_start(W1_s[lo:lo + b - a, :], W1[a:b, :]).then_inc(par, 16)
                    n += 16
                for to, frm in ( (W2_s, W2), (W3_s, W3), (L2_s, L2_W), (L3_s, L3_W)):
                    sp.dma_start(to[:, :], frm).then_inc(par, 16)
                    n += 16
                sp.dma_start(b1_c[:, :], b1.rearrange("(p a) -> p a", a=1)).then_inc(par, 16)
                n += 16
                for to, frm in ((b2_r, b2), (b3_r, b3), (l2b_r, L2_b), (l3b_r, L3_b), (gam_r, gamma), (bet_r, beta)):
                    sp.dma_start(to[:, :], frm.rearrange("(a f) -> a f", a=1).broadcast_to([P, frm.shape[0]])).then_inc(par, 16)
                    n += 16
                sp.wait_ge(par, n)

            @block.tensor
            def _(pe):
                pe.wait_ge(par, 16 * 14)
                nc.tensor.transpose(ps[2][0:D, 0, 0:D], L2_s[:, :], ident[0:D, 0:D]).then_inc(par_t, 1)

            @block.vector
            def _(dve):
                nc.vector.memset(W1_s[:, :], 0.0).then_inc(par_t, 1)
                nc.vector.tensor_copy(ident_b[:, :], ident[:, :]).then_inc(par_t, 1)
                dve.wait_ge(par_t, 3)
                nc.vector.tensor_copy(L2_t[:, :], ps[2][0:D, 0, 0:D])

        sweeps = nc.values_load(sweeps_i[0:1, 0:1], min_val=1, max_val=WINDOWS)
        dense_ok = nc.values_load(sweeps_i[0:1, 1:2], min_val=0, max_val=1)

        chunk = [acc[:, (NB + 1) * D + r * CHB * SUP:(NB + 1) * D + (r + 1) * CHB * SUP] for r in range(2)] + [
            tmp_raw[:, r * CHB * SUP:(r + 1) * CHB * SUP] for r in range(2)]
        panel = tmp_raw[:, 2 * CHB * SUP:2 * CHB * SUP + SUP]
        fcur = xc

        cols = sb("cols", [P, 2, 3, TILES])
        wsum = sb("wsum", [P, 2, TILES])
        count = sb("count", [P, 2, TILES])
        dup_i = sb("dup_i", [P, 2, TILES], I32)
        place = sb("place", [P, 2, TILES], I32)
        diag = tmp_raw[:, 0:2 * 3 * P].rearrange("p (v a e) -> p v a e", v=2, a=3)
        same = tmp_raw[:, 2 * 3 * P:2 * 3 * P + 4 * P].rearrange("p (a e) -> p a e", a=4)

        def aggregate_block(weighted, first=0, last=NG, feat=xc, with_dense=False, zero_fill=False, building=False):
            TG = 2 * GPS if with_dense else SLOTS
            turns = (last - first) // TG
            idx_ready, hot_ready, gathered, summed, chunk_in, chunk_free = (slot_sems(f"agg_{n}") for n in (
                "idx", "onehot", "gathered", "summed", "chunk_in", "chunk_free"))
            step, window, taken, added, scaled, high, rest, middle, parts_ready, panel_done, panel_kept, panel_turned, panel_added, zeroed, paced = (
                sem(f"agg_{n}") for n in ("step", "window", "slot_taken", "added", "scaled", "high", "rest", "middle", "parts",
                                          "panel_done", "panel_kept", "panel_turned", "panel_added", "zeroed", "paced"))
            cols_set, diag_set, spread, found, looked, chosen, places_set, carried, slot_free, scattered = (
                sem(f"build_{n}") for n in ("cols", "diag", "spread", "found", "looked", "chosen", "places_set", "carried", "slot_free",
                                            "scattered"))
            nstep = 2 if weighted else 1

            with nc.Block() as block:
                def at(t, j):
                    return t * TG + j, j % SLOTS, t * (TG // SLOTS) + j // SLOTS

                def chunks_before(j):
                    return range(-(-j * CPS // GPS), -(-(j + 1) * CPS // GPS))

                if with_dense:
                    @block.sync
                    def _(sp):
                        with sp.Fori(0, turns) as t:
                            for c in range(2 * CPS):
                                r = c % RING
                                sp.wait_ge(chunk_free[r], t * (2 * CPS // RING) + (c // RING + 1))
                                sp.dma_start(chunk[r], dense_v[bass.ds(t * 2 + c // CPS, 1), :, c % CPS * CHB * SUP:(c % CPS + 1) * CHB * SUP]
                                             .rearrange("b p f -> p (b f)")).then_inc(chunk_in[r], 16)

                if zero_fill:
                    @block.sync
                    def _(sp):
                        sp.wait_ge(zeroed, 1)
                        with sp.Fori(0, SUPS) as b:
                            for c in range(CPS):
                                sp.dma_start(dense_v[bass.ds(b, 1), :, c * CHB * SUP:(c + 1) * CHB * SUP]
                                             .rearrange("b p f -> p (b f)"), chunk[0]).then_inc(dense_zero[c % 2], 16)
                                if c % 2:
                                    for h in range(2):
                                        sp.wait_ge(dense_zero[h], b * (16 * CPS // 2) + 16 * (c // 2 + 1))
                                    sp.sem_inc(paced, 1)
                        sp.dma_start(dense[DENSE:DENSE + P, :], chunk[0][:, 0:1]).then_inc(dense_zero[0], 16)
                        sp.wait_ge(dense_zero[0], 16 * (SUPS * CPS // 2 + 1))

                @block.scalar
                def _(act):
                    def set_indices(t, j):
                        l, u, n = at(t, j)
                        act.wait_ge(summed[u], n + 1)
                        nc.scalar.copy(idx[:, u, :], src_i[:, bass.ds(l + first, 1), :].rearrange("p a k -> p (a k)")).then_inc(idx_ready[u], 1)

                    for j in range(SLOTS - 1):
                        set_indices(0, j)
                    with act.Fori(0, turns) as t:
                        for j in range(TG):
                            set_indices(t, j + SLOTS - 1)
                            l, u, n = at(t, j)
                            if weighted:
                                act.wait_ge(scaled, l + 1)
                            else:
                                act.wait_ge(gathered[u], n * (16 * TILES) + 16 * TILES)
                            nc.scalar.copy(parts48[:, u, :, 0:D], msg[:, u, :, :]).then_inc(high, 1)
                            act.wait_ge(rest, l + 1)
                            nc.scalar.copy(parts48[:, u, :, D:2 * D], msg[:, u, :, :]).then_inc(middle, 1)
                            if with_dense and j % GPS == GPS - 1:
                                p = t * 2 + j // GPS
                                act.wait_ge(panel_done, p + 1)
                                act.wait_ge(panel_turned, p + 1)
                                nc.scalar.copy(panel[0:D, :], psD[0:D, :])
                                nc.scalar.copy(panel[HC2:HC2 + D, :], psD[HC2:HC2 + D, :]).then_inc(panel_kept, 1)
                            if building:
                                v = j % 2
                                act.wait_ge(cols_set, l + 1)
                                for k in range(TILES):
                                    act.wait_ge(spread, l * TILES + (k + 1))
                                    for a in range(3):
                                        m = nc.scalar.activation(diag[:, k % 2, a, :], ident[:, :], ACT.Copy, scale=cols[:, v, a, k:k + 1])
                                    m.then_inc(diag_set, 1)

                @block.gpsimd
                def _(pool):
                    def claim(t, j):
                        l, u, n = at(t, j)
                        pool.wait_ge(idx_ready[u], n + 1)
                        pool.wait_ge(summed[u], n + 1)
                        pool.sem_inc(taken, 1)

                    def gather(u, k):
                        pool.indirect_dma_start(
                            out=msg[:, u, k, :], out_offset=None, in_=table,
                            in_offset=bass.IndirectOffsetOnAxis(ap=idx[:, u, k:k + 1], axis=0),
                        ).then_inc(gathered[u], 16)

                    def scatter(t, j, ahead):
                        g, v, u = t * TG + j, j % 2, (j + 2) % SLOTS
                        pool.wait_ge(chosen, g * 3 + 4)
                        for k in range(TILES):
                            pool.sem_inc(carried, 1)
                            pool.indirect_dma_start(
                                out=dense, out_offset=bass.IndirectOffsetOnAxis(ap=place[:, v, k:k + 1], axis=0),
                                in_=wsum[:, v, k:k + 1], in_offset=None, compute_op=ALU.add).then_inc(scattered, 16)
                            if ahead:
                                gather(u, k)
                            pool.wait_ge(scattered, g * (16 * TILES) + (k + 1) * 16)
                        pool.sem_inc(slot_free, 1)

                    if building:
                        pool.sem_inc(slot_free, 2)
                        for j in range(2):
                            claim(0, j)
                            for k in range(TILES):
                                gather(j, k)
                        if turns > 1:
                            with pool.Fori(0, turns - 1) as t:
                                for j in range(TG):
                                    claim(t, j + 2)
                                    scatter(t, j, True)
                        for j in range(TG):
                            if j + 2 < TG:
                                claim(turns - 1, j + 2)
                            scatter(turns - 1, j, j + 2 < TG)
                    else:
                        with pool.Fori(0, turns) as t:
                            for j in range(TG):
                                claim(t, j)
                                for k in range(TILES):
                                    gather(j % SLOTS, k)

                @block.vector
                def _(dve):
                    if zero_fill:
                        nc.vector.memset(chunk[0], 0.0).then_inc(zeroed, 1)
                    if with_dense:
                        nc.vector.memset(panel, 0.0).then_inc(zeroed, 1)
                    nc.vector.tensor_scalar(base[:, :], base0[:, :], sweep0[:, 0:1], None, ALU.add).then_inc(window, 1)
                    dve.wait_ge(window, 1)
                    nc.vector.tensor_scalar(base_blk[:, :], base[0:1, :], 1.0 / P, None, ALU.mult).then_inc(window, 1)
                    if not (with_dense or zero_fill or building):
                        nc.vector.tensor_scalar(sweep0[:, :], sweep0[:, :], float(WIN), None, ALU.add).then_inc(window, 1)
                        dve.wait_ge(window, 3)
                    dve.wait_ge(window, 2)

                    def make_onehots(t, j):
                        l, u, n = at(t, j)
                        g = l + first
                        dve.wait_ge(summed[u], n + 1)
                        nc.vector.tensor_scalar(dloc[:, u, :], dst_f[:, bass.ds(g, 1), :].rearrange("p a k -> p (a k)"),
                                                base[:, bass.ds(g, 1)], None, ALU.subtract).then_inc(step, 1)
                        if weighted:
                            nc.vector.tensor_copy(wl[:, u, :], wgt[:, bass.ds(g, 1), :].rearrange("p a k -> p (a k)")).then_inc(step, 1)
                        dve.wait_ge(step, (l + 1) * nstep)
                        onehots(onehot_b[:, u, :, :], dloc[:, u, :]).then_inc(hot_ready[u], 1)

                    def add_sums(t, j):
                        l, u, n = at(t, j)
                        blk = dve.value_load(base_blk[0:1, bass.ds(l + first, 1)], min_val=0, max_val=NB - 1)
                        here = acc[:, bass.ds(blk * D, 2 * D)].rearrange("p (a f) -> p a f", a=2)
                        dve.wait_ge(summed[u], n + 2)
                        for c in range(3):
                            dve.wait_ge(added, l * 3 + (c + START))
                            nc.vector.tensor_tensor(here, here, ps[u % 2][:, :, c * D:(c + 1) * D], ALU.add).then_inc(added, 1)

                    def build_group(g, v):
                        dve.wait_ge(spread, g * TILES + 1)
                        dve.sem_inc(places_set, 1)
                        for a, arr in ((1, dst_f), (2, wgt)):
                            nc.vector.tensor_copy(cols[:, v, a, :], arr[:, bass.ds(g, 1), :].rearrange("p a k -> p (a k)"))
                        nc.vector.tensor_copy(cols[:, v, 0, :], src_i[:, bass.ds(g, 1), :].rearrange("p a k -> p (a k)")).then_inc(cols_set, 1)
                        dve.wait_ge(slot_free, g + 1)
                        for k in range(TILES):
                            n = g * TILES + k
                            dve.wait_ge(spread, n + 3)
                            rows3 = ps[2][:, k % 2, :]
                            nc.vector.tensor_scalar(same[:, 0, :], rows3[:, 0:P], cols[:, v, 0, k:k + 1], None, ALU.is_equal).then_inc(found, 1)
                            dve.wait_ge(found, n * 3 + 1)
                            nc.vector.scalar_tensor_tensor(same[:, 1, :], rows3[:, P:2 * P], cols[:, v, 1, k:k + 1], same[:, 0, :],
                                                           ALU.is_equal, ALU.mult).then_inc(found, 1)
                            dve.wait_ge(found, n * 3 + 2)
                            nc.vector.tensor_tensor_reduce(out=same[:, 2, :], in0=rows3[:, 2 * P:3 * P], in1=same[:, 1, :], scale=1.0, scalar=0.0,
                                                           op0=ALU.mult, op1=ALU.add, accum_out=wsum[:, v, k:k + 1]).then_inc(looked, 1)
                            nc.vector.tensor_tensor_reduce(out=same[:, 3, :], in0=rank[:, :], in1=same[:, 1, :], scale=1.0, scalar=0.0,
                                                           op0=ALU.mult, op1=ALU.add, accum_out=count[:, v, k:k + 1]).then_inc(found, 1)
                            dve.wait_ge(looked, n + 3)
                            dve.wait_ge(found, n * 3 + 3)
                        nc.vector.tensor_scalar(dup_i[:, v, :], count[:, v, :], FIRST - 0.5, None, ALU.is_gt).then_inc(chosen, 1)
                        nc.vector.tensor_copy(place[:, v, :], addr[:, bass.ds(g, 1), :].rearrange("p a k -> p (a k)")).then_inc(chosen, 1)
                        dve.wait_ge(chosen, g * 3 + 3)
                        dve.sem_inc(places_set, 1)
                        nc.vector.copy_predicated(place[:, v, :], dup_i[:, v, :], past_i[:, 0:1].broadcast_to([P, TILES])).then_inc(chosen, 1)
                        nc.vector.tensor_copy(times[:, bass.ds(g, 1), :].rearrange("p a k -> p (a k)"), count[:, v, :])
                        dve.wait_ge(chosen, g * 3 + 4)
                        dve.sem_inc(places_set, 1)
                        nc.vector.tensor_copy(addr[:, bass.ds(g, 1), :].rearrange("p a k -> p (a k)"), place[:, v, :])

                    if building:
                        dve.sem_inc(chosen, 1)
                    make_onehots(0, 0)
                    with dve.Fori(0, turns) as t:
                        for j in range(TG):
                            l, u, n = at(t, j)
                            make_onehots(t, j + 1)
                            if weighted:
                                dve.wait_ge(gathered[u], n * (16 * TILES) + 16 * TILES)
                                nc.vector.tensor_tensor(msg[:, u, :, :], msg[:, u, :, :], wl[:, u, :].unsqueeze(2).broadcast_to([P, TILES, D]),
                                                        ALU.mult).then_inc(scaled, 1)
                            if j:
                                add_sums(t, j - 1)
                            dve.wait_ge(high, l + 1)
                            nc.vector.tensor_tensor(msg[:, u, :, :], msg[:, u, :, :], parts48[:, u, :, 0:D], ALU.subtract).then_inc(rest, 1)
                            dve.wait_ge(middle, l + 1)
                            nc.vector.tensor_tensor(parts48[:, u, :, 2 * D:3 * D], msg[:, u, :, :], parts48[:, u, :, D:2 * D],
                                                    ALU.subtract).then_inc(parts_ready, 1)
                            if j == TG - 1:
                                add_sums(t, j)
                            if building:
                                build_group(l, j % 2)
                            if with_dense and j % GPS == GPS - 1:
                                p = t * 2 + j // GPS
                                there = acc[:, bass.ds(p * (SUP // P * D), SUP // P * D)].rearrange("p (a f) -> p a f", f=D)
                                turned = psDT[:, 0:SUP // P * (HC2 + D)].rearrange("p (a f) -> p a f", f=HC2 + D)
                                dve.wait_ge(panel_turned, p + 2)
                                dve.wait_ge(added, (l + (1 if j == TG - 1 else 0)) * 3 + START)
                                for c in range(2):
                                    dve.wait_ge(panel_added, p * 2 + (c + 1))
                                    nc.vector.tensor_tensor(there, there, turned[:, :, c * HC2:c * HC2 + D], ALU.add).then_inc(panel_added, 1)
                                dve.wait_ge(panel_added, p * 2 + 3)

                @block.tensor
                def _(pe):
                    pe.sem_inc(added, START)
                    for u in range(SLOTS):
                        pe.sem_inc(summed[u], 1)
                    if building:
                        pe.sem_inc(spread, 2)
                        pe.sem_inc(looked, 2)
                    if with_dense:
                        pe.wait_ge(zeroed, 1)
                        pe.sem_inc(panel_turned, 1)
                        pe.sem_inc(panel_added, 1)
                        pe.sem_inc(panel_kept, 1)
                        for r in range(RING):
                            pe.sem_inc(chunk_free[r], 1)
                    with pe.Fori(0, turns) as t:
                        for j in range(TG):
                            l, u, n = at(t, j)
                            if with_dense:
                                p = t * 2 + j // GPS
                                for c in chunks_before(j % GPS):
                                    cc = j // GPS * CPS + c
                                    r = cc % RING
                                    if c == 0:
                                        pe.wait_ge(panel_kept, p + 1)
                                    pe.wait_ge(chunk_in[r], t * (2 * CPS // RING * 16) + (cc // RING + 1) * 16)
                                    for i in range(CHB):
                                        sblk = c * CHB + i
                                        o = HC2 * (sblk % 2)
                                        m = nc.tensor.matmul(psD[o:o + D, :], feat[:, sblk, :], chunk[r][:, i * SUP:(i + 1) * SUP],
                                                             start=sblk < 2, stop=sblk >= NB - 2, skip_group_check=True)
                                    m.then_inc(chunk_free[r], 1)
                                    if c == CPS - 1:
                                        pe.wait_ge(chunk_free[r], t * (2 * CPS // RING) + (cc // RING + 2))
                                        pe.sem_inc(panel_done, 1)
                            pe.wait_ge(hot_ready[u], n + 1)
                            pe.wait_ge(parts_ready, l + 1)
                            pe.wait_ge(added, l * 3 + (START - 3))
                            for k in range(TILES):
                                for h in range(2):
                                    m = nc.tensor.matmul(ps[u % 2][:, h, 0:3 * D], onehot_b[:, u, k, h * P:(h + 1) * P], parts48[:, u, k, :],
                                                         start=k == 0, stop=k == TILES - 1)
                            m.then_inc(summed[u], 1)
                            if building:
                                for k in range(TILES):
                                    pe.wait_ge(diag_set, l * TILES + (k + 1))
                                    pe.wait_ge(looked, l * TILES + (k + 1))
                                    nc.tensor.matmul(ps[2][:, k % 2, 0:3 * P], ones[:, :], diag[:, k % 2, :, :].rearrange("p a e -> p (a e)"),
                                                     start=True, stop=True).then_inc(spread, 1)
                            if with_dense and j % GPS == GPS - 1:
                                pe.wait_ge(panel_kept, p + 2)
                                pe.wait_ge(panel_added, p * 2 + 1)
                                for b in range(SUP // P):
                                    m = nc.tensor.transpose(psDT[:, b * (HC2 + D):(b + 1) * (HC2 + D)], panel[0:HC2 + D, b * P:(b + 1) * P],
                                                            ident[0:HC2 + D, 0:HC2 + D])
                                m.then_inc(panel_turned, 1)
            clear([*idx_ready, *hot_ready, *summed, *chunk_in, *chunk_free, step, window, taken, added, scaled, high, rest, middle,
                   parts_ready, panel_done, panel_kept, panel_turned, panel_added, zeroed, paced,
                   cols_set, diag_set, spread, found, looked, chosen, places_set, carried, slot_free], [*gathered, scattered])

        def aggregate_all(weighted):
            with nc.Fori(0, sweeps):
                aggregate_block(weighted)

        def aggregate_counted(feat):
            with nc.If(dense_ok == 1):
                aggregate_block(False, first=DG, feat=feat, with_dense=True)
            with nc.Else():
                aggregate_all(False)

        accD = acc[:, 0:NB * D].rearrange("p (b f) -> p b f", f=D)
        kept_acc, hop_store = sem("hop_kept"), sem("hop_store")
        dense_zero = [sem("dense_zero_even"), sem("dense_zero_odd")]

        def start_hop():
            with nc.Block() as block:
                @block.vector
                def _(dve):
                    nc.vector.memset(sweep0[:, :], 0.0)
                    nc.vector.memset(acc[:, NB * D:(NB + 1) * D], 0.0)
                    nc.vector.tensor_copy(accD, f01)

        def end_hop():
            with nc.Block() as block:
                @block.vector
                def _(dve):
                    nc.vector.memset(sweep0[:, :], 0.0)
                    nc.vector.tensor_copy(fcur[:, 0:NB // 2, :], accD[:, 0:NB // 2, :]).then_inc(kept_acc, 1)
                    dve.wait_ge(kept_acc, 2)
                    nc.vector.tensor_copy(accD[:, 0:NB // 2, :], f01[:, 0:NB // 2, :])
                    nc.vector.memset(acc[:, NB * D:(NB + 1) * D], 0.0)

                @block.scalar
                def _(act):
                    nc.scalar.copy(fcur[:, NB // 2:NB, :], accD[:, NB // 2:NB, :]).then_inc(kept_acc, 1)
                    act.wait_ge(kept_acc, 2)
                    nc.scalar.copy(accD[:, NB // 2:NB, :], f01[:, NB // 2:NB, :])

                @block.sync
                def _(sp):
                    sp.wait_ge(kept_acc, 2)
                    sp.dma_start(table_v, fcur[:, :, :]).then_inc(hop_store, 16)
                    sp.wait_ge(hop_store, 16)
            clear([kept_acc, hop_store])

        start_hop()
        with nc.If(dense_ok == 1):
            aggregate_block(True, first=DG, zero_fill=True)
            aggregate_block(True, last=DG, building=True)
            end_hop()

            with nc.Fori(0, HOPS - 1):
                aggregate_block(True, first=DG, with_dense=True)
                end_hop()
        with nc.Else():
            with nc.Fori(0, HOPS):
                aggregate_all(True)
                end_hop()

        x_again, x_in_again = sem("x_again"), sem("x_in_again")
        with nc.Block() as block:
            @block.vector
            def _(dve):
                nc.vector.memset(f01[:, NB - 1, :], 0.0).then_inc(x_again, 1)
                nc.vector.memset(acc[:, :], 0.0)

            @block.sync
            def _(sp):
                sp.wait_ge(x_again, 1)
                load_nodes(sp, f01, x, x_in_again)
                sp.wait_ge(x_in_again, 32 if NREST else 16)

        s1 = sb("ln_sum", [P, NB])
        s2 = sb("ln_var", [P, NB])

        def layernorm(x, y, to):
            step, sq, rt = sem("ln_step"), sem("ln_squared"), sem("ln_root")
            with nc.Block() as block:
                @block.vector
                def _(dve):
                    n = [0]

                    def link(ins):
                        n[0] += 1
                        ins.then_inc(step, 1)
                        dve.wait_ge(step, n[0])

                    wide = [P, NB, D]
                    link(nc.vector.tensor_tensor(to, x, y, ALU.add))
                    link(nc.vector.tensor_reduce(s1[:, :], to, AX, ALU.add))
                    link(nc.vector.tensor_scalar(s1[:, :], s1[:, :], 1.0 / D, None, ALU.mult))
                    link(nc.vector.tensor_tensor(to, to, s1[:, :].unsqueeze(2).broadcast_to(wide), ALU.subtract))
                    dve.wait_ge(sq, 1)
                    link(nc.vector.tensor_reduce(s2[:, :], tmp[:, :, :], AX, ALU.add))
                    link(nc.vector.tensor_scalar(s2[:, :], s2[:, :], 1.0 / D, EPS, ALU.mult, ALU.add))
                    dve.wait_ge(rt, 1)
                    link(nc.vector.reciprocal(s2[:, :], s1[:, :]))
                    link(nc.vector.tensor_tensor(to, to, s2[:, :].unsqueeze(2).broadcast_to(wide), ALU.mult))

                @block.scalar
                def _(act):
                    act.wait_ge(step, 4)
                    nc.scalar.activation(tmp[:, :, :], to, ACT.Square).then_inc(sq, 1)
                    act.wait_ge(step, 6)
                    nc.scalar.activation(s1[:, :], s2[:, :], ACT.Sqrt).then_inc(rt, 1)
            clear([step, sq, rt])

        layernorm(f01, fcur[:, :, :], xc[:, :, :])

        def store_table(frm):
            s = sem("table_stored_again")
            with nc.Block() as block:
                @block.sync
                def _(sp):
                    sp.dma_start(table_v, frm).then_inc(s, 16)
                    sp.wait_ge(s, 16)
            clear([s])

        store_table(xc[:, :, :])

        HQ = HALF * P
        assert KS == HC2
        AT = SLOTS * TILES * KS
        HT = AT + SLOTS * TILES * DE
        XW = HT + 2 * HALF * P
        rows = f01_raw[:, 0:AT].rearrange("p (u k f) -> p u k f", u=SLOTS, k=TILES)
        attr = f01_raw[:, AT:HT].rearrange("p (u k f) -> p u k f", u=SLOTS, k=TILES)
        hotT = f01_raw[:, HT:XW].bitcast(BF16).rearrange("p (q h e) -> p q h e", q=2, h=2)
        xwin = f01_raw[:, XW:XW + SLOTS * 3 * D].bitcast(BF16).rearrange("p (u c h f) -> p u c h f", u=SLOTS, c=3, h=2)
        xrest = msg[:, 0, 0:2, :]
        psH = ps[2][:, 1, :].bitcast(BF16)
        rowsT = tmp_raw[:, 0:2 * HQ].rearrange("p (q e) -> p q e", q=2)
        h1T = tmp_raw[:, 2 * HQ:4 * HQ].rearrange("p (q e) -> p q e", q=2)
        h2pre = tmp_raw[:, 4 * HQ:5 * HQ].rearrange("p (k f) -> p k f", k=HALF)
        h2 = tmp_raw[:, 5 * HQ:6 * HQ].rearrange("p (k f) -> p k f", k=HALF)
        PARTS = 3 * H + 1
        parts = tmp_raw[:, 6 * HQ:6 * HQ + HALF * PARTS].bitcast(BF16).rearrange("p (q k f) -> p q k f", q=2, k=HALF)
        zeros = tmp_raw[:, 6 * HQ + HALF * PARTS:6 * HQ + HALF * PARTS + 2 * P]
        hotsrc = parts48[:, :, :, :].rearrange("p u k f -> p (u k f)")[:, 0:2 * TILES * 2 * P].rearrange("p (u k a e) -> p u k a e", u=2, k=TILES, a=2)

        gathered, attr_in, idx_ready, group_free = (slot_sems(f"l1_{n}") for n in ("gathered", "attr", "idx", "free"))
        zeroed, filled, scattered, picked, carried = (sem(f"count_{n}") for n in ("zeroed", "filled", "scattered", "picked", "carried"))
        place_t = sb("place_t", [P, SPT], I32)
        times_t = sb("times_t", [P, SPT])
        hot_turned, hotT_ready, window_step = sem("l1_hot_turned"), sem("l1_hotT"), sem("l1_window_step")
        (transposed, rowsT_ready, lin1, h1T_ready, lin2, h2pre_ready, h2_ready, rest_ready, mid_ready, parts_ready,
         hot_ready, summed_q, added, step, window, taken, attr_placed, cnt_hot, cnt_sum, cnt_added) = (
            sem(f"l1_{n}") for n in ("transposed", "rowsT", "lin1", "h1T", "lin2", "h2pre", "h2", "rest", "mid", "parts",
                                     "onehot", "summed", "added", "step", "window", "slot_taken", "attr_placed",
                                     "cnt_hot", "cnt_sum", "cnt_added"))
        NT = NG // SLOTS
        GPT = SLOTS * TILES
        addr_flat = addr[:, :, :].rearrange("p g k -> p (g k)")
        times_flat = times[:, :, :].rearrange("p g k -> p (g k)")
        TG = max(n for n in range(SLOTS, 29, SLOTS) if NG % n == 0)
        USES = TG // SLOTS
        QB = 2 * TG
        SUMMED = 2 * START
        with nc.Block() as block:
            @block.vector
            def _(dve):
                nc.vector.memset(sweep0[:, :], 0.0)
                nc.vector.memset(f01_raw[:, AT:HT], 0.0)

        with nc.Fori(0, sweeps):
            with nc.Block() as block:
                @block.sync
                def _(sp):
                    def load(g, u, p):
                        sp.dma_start(attr[0:p, u, :, :].rearrange("p k f -> p (k f)"),
                                     edge_attr[bass.ds(g * GROUP, p * TILES), :].rearrange("(p k) f -> p (k f)", k=TILES)).then_inc(attr_in[u], 16)

                    zero_piece = zeros.unsqueeze(1).broadcast_to([P, CHB * SUP // (2 * P), 2 * P])
                    FPT = FILLS // FTURNS
                    for u in range(SLOTS):
                        sp.wait_ge(attr_placed, u + 1)
                        load(u, u, P)
                    sp.wait_ge(zeroed, 1)
                    sp.dma_start(dense[DENSE:DENSE + P, :], zeros[:, 0:1]).then_inc(filled, 16)
                    with sp.Fori(0, FTURNS) as t:
                        for u in range(SLOTS):
                            sp.wait_ge(attr_placed, t * SLOTS + (u + SLOTS + 1))
                            load((t + 1) * SLOTS + u, u, P)
                            for c in range(u * FPT // SLOTS, (u + 1) * FPT // SLOTS):
                                sp.dma_start(dense_z[bass.ds(t * FPT + c, 1), :, :].rearrange("c p (a f) -> (c p) a f", f=2 * P), zero_piece).then_inc(filled, 16)
                    with sp.Fori(FTURNS + 1, NT - 1) as t:
                        for u in range(SLOTS):
                            sp.wait_ge(attr_placed, t * SLOTS + (u + 1))
                            load(t * SLOTS + u, u, P)
                    for u in range(SLOTS):
                        g = (NT - 1) * SLOTS + u
                        sp.wait_ge(attr_placed, g + 1)
                        if g < GFULL:
                            load(g, u, P)
                        elif g == GFULL and TP:
                            load(g, u, TP)
                        else:
                            load(0, u, P if GFULL else TP)

                @block.gpsimd
                def _(pool):
                    def gather_turn(t, after=lambda n: None):
                        for u in range(SLOTS):
                            pool.wait_ge(idx_ready[u], t + 1)
                            pool.wait_ge(group_free[u], t + 1)
                            pool.sem_inc(taken, 1)
                            for k in range(TILES):
                                pool.indirect_dma_start(
                                    out=rows[:, u, k, 0:D], out_offset=None, in_=table,
                                    in_offset=bass.IndirectOffsetOnAxis(ap=idx[:, u, k:k + 1], axis=0),
                                ).then_inc(gathered[u], 16)
                                after(u * TILES + k)

                    with pool.Fori(0, NT - CTURNS) as t:
                        gather_turn(t)
                    pool.wait_ge(filled, 16 * (FILLS + 1))
                    pool.sem_inc(carried, 1)
                    with pool.Fori(0, CTURNS) as t:
                        nc.gpsimd.tensor_copy(place_t[:, :], addr_flat[:, bass.ds(t * SPT, SPT)]).then_inc(picked, 1)
                        nc.gpsimd.tensor_copy(times_t[:, :], times_flat[:, bass.ds(t * SPT, SPT)]).then_inc(picked, 1)
                        pool.wait_ge(picked, t * 2 + 2)

                        def scatter(n):
                            for k in range(-(-n * SPT // GPT), -(-(n + 1) * SPT // GPT)):
                                if k:
                                    pool.wait_ge(scattered, t * (16 * SPT) + 16 * k)
                                pool.sem_inc(carried, 1)
                                pool.indirect_dma_start(
                                    out=dense, out_offset=bass.IndirectOffsetOnAxis(ap=place_t[:, k:k + 1], axis=0),
                                    in_=times_t[:, k:k + 1], in_offset=None, compute_op=ALU.add).then_inc(scattered, 16)

                        gather_turn(t + (NT - CTURNS), scatter)
                        pool.wait_ge(scattered, t * (16 * SPT) + 16 * SPT)
                        pool.sem_inc(carried, 1)

                @block.scalar
                def _(act):
                    act.sem_inc(rowsT_ready, START)
                    act.sem_inc(hotT_ready, START)
                    act.sem_inc(h1T_ready, START)
                    act.sem_inc(h2_ready, START)
                    act.sem_inc(mid_ready, START)

                    def set_indices(t, j):
                        g, u = t * TG + j, j % SLOTS
                        act.wait_ge(group_free[u], t * USES + (j // SLOTS + 1))
                        nc.scalar.copy(idx[:, u, :], src_i[:, bass.ds(g, 1), :].rearrange("p a k -> p (a k)")).then_inc(idx_ready[u], 1)

                    for u in range(SLOTS):
                        set_indices(0, u)
                    with act.Fori(0, NG // TG) as t:
                        for i in range(QB + 3):
                            if 3 <= i <= QB + 2:
                                q, j = t * QB + i - 3, (i - 3) % 2
                                act.wait_ge(h2pre_ready, q + START + 1)
                                act.wait_ge(parts_ready, q + START)
                                act.wait_ge(summed_q, q + SUMMED - 1)
                                nc.scalar.activation(h2[:, :, :], h2pre, ACT.Relu)
                                nc.scalar.activation(parts[:, j, :, 0:H], h2pre, ACT.Relu).then_inc(h2_ready, 1)
                            if 2 <= i <= QB + 1:
                                q, j = t * QB + i - 2, i % 2
                                act.wait_ge(lin1, q + START + 1)
                                act.wait_ge(lin2, q + START - 1)
                                nc.scalar.activation(h1T[:, j, :], ps1[:, :], ACT.Relu, bias=b1_c[:, 0:1]).then_inc(h1T_ready, 1)
                            if 1 <= i <= QB:
                                q, j = t * QB + i - 1, (i - 1) % 2
                                act.wait_ge(transposed, q + START + 1)
                                act.wait_ge(lin1, q + START - 1)
                                nc.scalar.copy(rowsT[:, j, :], psT).then_inc(rowsT_ready, 1)
                            if i < QB:
                                q = t * QB + i
                                act.wait_ge(hot_turned, q + START + 1)
                                act.wait_ge(transposed, q + START - 1)
                                nc.scalar.copy(hotT[:, i % 2, :, :].rearrange("p h e -> p (h e)"), psH).then_inc(hotT_ready, 1)
                            if 3 <= i <= QB + 2:
                                q, j = t * QB + i - 3, (i - 3) % 2
                                act.wait_ge(rest_ready, q + START + 1)
                                nc.scalar.copy(parts[:, j, :, H:2 * H], h2[:, :, :]).then_inc(mid_ready, 1)
                            if 2 <= i <= QB and i % 2 == 0:
                                set_indices(t, i // 2 - 1 + SLOTS)

                @block.vector
                def _(dve):
                    nc.vector.memset(zeros, 0.0).then_inc(zeroed, 1)
                    dve.sem_inc(h2pre_ready, START)
                    dve.sem_inc(rest_ready, START)
                    dve.sem_inc(parts_ready, START)
                    dve.sem_inc(added, START)
                    dve.sem_inc(attr_placed, SLOTS)
                    dve.sem_inc(cnt_hot, START)
                    dve.sem_inc(cnt_added, START)
                    nc.vector.tensor_scalar(base[:, :], base0[:, :], sweep0[:, 0:1], None, ALU.add).then_inc(window, 1)
                    dve.wait_ge(window, 1)
                    nc.vector.tensor_scalar(base_blk[:, :], base[0:1, :], 1.0 / P, None, ALU.mult).then_inc(window, 1)
                    nc.vector.tensor_scalar(sweep0[:, :], sweep0[:, :], float(WIN), None, ALU.add).then_inc(window, 1)
                    nc.vector.memset(outdeg[:, :], 0.0).then_inc(window, 1)
                    nc.vector.memset(parts[:, :, :, 3 * H:3 * H + 1], 1.0).then_inc(window, 1)
                    nc.vector.memset(psT, 0.0).then_inc(window, 1)
                    dve.wait_ge(window, 6)

                    def make_onehots(g, u):
                        dve.wait_ge(summed_q, g * 2 + (SUMMED - 6))
                        nc.vector.tensor_scalar(dloc[:, u, :], dst_f[:, bass.ds(g, 1), :].rearrange("p a k -> p (a k)"),
                                                base[:, bass.ds(g, 1)], None, ALU.subtract).then_inc(window_step, 1)
                        blk = dve.value_load(base_blk[0:1, bass.ds(g, 1)], min_val=0, max_val=NB - 1)
                        x_here = xc_raw[:, bass.ds(blk * D, 2 * D)].rearrange("p (h f) -> p h f", h=2)
                        nc.vector.tensor_copy(xwin[:, u, 0, :, :], x_here).then_inc(window_step, 1)
                        dve.wait_ge(window_step, g * 4 + 2)
                        nc.vector.tensor_tensor(xrest, x_here, xwin[:, u, 0, :, :], ALU.subtract).then_inc(window_step, 1)
                        onehots(onehot_b[:, u, 0:HALF, :], dloc[:, u, 0:HALF])
                        dve.wait_ge(window_step, g * 4 + 3)
                        nc.vector.tensor_copy(xwin[:, u, 1, :, :], xrest).then_inc(window_step, 1)
                        onehots(onehot_b[:, u, HALF:TILES, :], dloc[:, u, HALF:TILES])
                        dve.wait_ge(window_step, g * 4 + 4)
                        nc.vector.tensor_tensor(xwin[:, u, 2, :, :], xrest, xwin[:, u, 1, :, :], ALU.subtract).then_inc(hot_ready, 1)
                        dve.wait_ge(hot_ready, g + 1)

                    make_onehots(0, 0)
                    with dve.Fori(0, NG // TG) as t:
                        for i in range(QB + 4):
                            if i < QB and i % 2 == 0:
                                u = i // 2 % SLOTS
                                g = t * TG + i // 2
                                uses = t * USES + i // 2 // SLOTS
                                dve.wait_ge(attr_in[u], uses * 16 + 16)
                                dve.wait_ge(group_free[u], uses + 1)
                                nc.vector.tensor_copy(rows[:, u, :, D:KS], attr[:, u, :, :]).then_inc(attr_placed, 1)
                                nc.vector.tensor_copy(lol[:, u, :], src_lo[:, bass.ds(g, 1), :].rearrange("p a k -> p (a k)")).then_inc(step, 1)
                                nc.vector.tensor_copy(hil[:, u, :], src_hi[:, bass.ds(g, 1), :].rearrange("p a k -> p (a k)")).then_inc(step, 1)
                            if 3 <= i <= QB + 2:
                                q, j = t * QB + i - 3, (i - 3) % 2
                                dve.wait_ge(lin2, q + START + 1)
                                dve.wait_ge(h2_ready, q + START)
                                nc.vector.tensor_tensor(h2pre, ps2.rearrange("p (k f) -> p k f", k=HALF),
                                                        b2_r[:, :].unsqueeze(1).broadcast_to([P, HALF, H]), ALU.add).then_inc(h2pre_ready, 1)
                            if i < QB:
                                g, u = t * TG + i // 2, i // 2 % SLOTS
                                if i % 2 == 0:
                                    make_onehots(g + 1, (u + 1) % SLOTS)
                                else:
                                    dve.wait_ge(step, g * 2 + 2)
                                    dve.wait_ge(cnt_sum, g + (START - 1))
                                    onehots(hotsrc[:, i // 2 % 2, :, 0, :], lol[:, u, :])
                                    onehots(hotsrc[:, i // 2 % 2, :, 1, 0:NB], hil[:, u, :]).then_inc(cnt_hot, 1)
                            if 3 <= i <= QB + 2:
                                dve.wait_ge(h2_ready, q + START + 1)
                                nc.vector.tensor_tensor(h2, h2, parts[:, j, :, 0:H], ALU.subtract).then_inc(rest_ready, 1)
                            if 4 <= i <= QB + 2 and i % 2 == 0:
                                g = t * TG + (i - 4) // 2
                                dve.wait_ge(cnt_sum, g + (START + 1))
                                dve.wait_ge(cnt_added, g + START)
                                nc.vector.tensor_tensor(outdeg[:, :], outdeg[:, :], cnt_ps[:, 0:NB], ALU.add).then_inc(cnt_added, 1)
                            if i >= 5 and i % 2:
                                g = t * TG + (i - 5) // 2
                                blk = dve.value_load(base_blk[0:1, bass.ds(g, 1)], min_val=0, max_val=NB - 1)
                                here = acc[:, bass.ds(blk * HC, 2 * HC)].rearrange("p (a f) -> p a f", a=2)
                                dve.wait_ge(summed_q, g * 2 + (SUMMED + 2))
                                for c, (lo, hi) in enumerate(((0, H), (H, 2 * H), (2 * H, 3 * H + 1))):
                                    dve.wait_ge(added, g * 3 + (c + START))
                                    o = HC - (hi - lo) if c == 2 else 0
                                    nc.vector.tensor_tensor(here[:, :, o:o + hi - lo], here[:, :, o:o + hi - lo], sums[:, :, lo:hi], ALU.add).then_inc(added, 1)
                            if 3 <= i <= QB + 2:
                                dve.wait_ge(mid_ready, q + START + 1)
                                nc.vector.tensor_tensor(parts[:, j, :, 2 * H:3 * H], h2, parts[:, j, :, H:2 * H], ALU.subtract).then_inc(parts_ready, 1)

                @block.tensor
                def _(pe):
                    pe.sem_inc(transposed, START)
                    pe.sem_inc(lin1, START)
                    pe.sem_inc(lin2, START)
                    pe.sem_inc(summed_q, SUMMED)
                    pe.sem_inc(hot_turned, START)
                    pe.sem_inc(cnt_sum, START)
                    for u in range(SLOTS):
                        pe.sem_inc(group_free[u], 1)
                    with pe.Fori(0, NG // TG) as t:
                        for i in range(QB + 4):
                            if 3 <= i <= QB + 2:
                                q, j = t * QB + i - 3, (i - 3) % 2
                                pe.wait_ge(h1T_ready, q + START + 1)
                                pe.wait_ge(h2pre_ready, q + START)
                                for k in range(HALF):
                                    m = nc.tensor.matmul(ps2[:, k * H:(k + 1) * H], h1T[:, j, k * P:(k + 1) * P], W2_s[:, :], start=True, stop=True)
                                m.then_inc(lin2, 1)
                            if 2 <= i <= QB + 1:
                                q, j = t * QB + i - 2, i % 2
                                pe.wait_ge(rowsT_ready, q + START + 1)
                                pe.wait_ge(h1T_ready, q + START)
                                nc.tensor.matmul(ps1[:, :], W1_s[:, :], rowsT[:, j, :], start=True, stop=True).then_inc(lin1, 1)
                            if 1 <= i <= QB:
                                g, j = (i - 1) // 2, (i - 1) % 2
                                q, u, k0 = t * QB + i - 1, g % SLOTS, HALF * j
                                if j == 0:
                                    pe.wait_ge(gathered[u], t * (USES * 16 * TILES) + (g // SLOTS + 1) * 16 * TILES)
                                    pe.wait_ge(attr_placed, t * TG + (g + SLOTS + 1))
                                pe.wait_ge(hotT_ready, q + START + 1)
                                pe.wait_ge(rowsT_ready, q + START)
                                for c in range(3):
                                    for h in range(2):
                                        nc.tensor.matmul(psT[HC2:HC2 + D, :], xwin[:, u, c, h, :], hotT[:, j, h, :],
                                                         start=c + h == 0, stop=c + h == 3, skip_group_check=True)
                                for k in range(HALF):
                                    m = nc.tensor.transpose(psT[0:KS, k * P:(k + 1) * P], rows[:, u, k0 + k, :], ident[:, :])
                                m.then_inc(transposed, 1)
                                if j == 1:
                                    pe.wait_ge(transposed, q + START + 1)
                                    pe.sem_inc(group_free[u], 1)
                            if i < QB:
                                q, u, k0 = t * QB + i, i // 2 % SLOTS, HALF * (i % 2)
                                if i % 2 == 0:
                                    pe.wait_ge(hot_ready, t * TG + (i // 2 + 1))
                                pe.wait_ge(hotT_ready, q + START)
                                for k in range(HALF):
                                    for h in range(2):
                                        m = nc.tensor.transpose(psH[:, h * HQ + k * P:h * HQ + (k + 1) * P], onehot_b[:, u, k0 + k, h * P:(h + 1) * P], ident_b[:, :])
                                m.then_inc(hot_turned, 1)
                            if 4 <= i:
                                g, j = (i - 4) // 2, i % 2
                                q, u, k0 = t * QB + i - 4, g % SLOTS, HALF * j
                                if j == 0:
                                    pe.wait_ge(added, t * (TG * 3) + (g * 3 + START))
                                pe.wait_ge(parts_ready, q + START + 1)
                                for k in range(HALF):
                                    for h in range(2):
                                        m = nc.tensor.matmul(sums[:, h, 0:PARTS], onehot_b[:, u, k0 + k, h * P:(h + 1) * P], parts[:, j, k, :],
                                                             start=k0 + k == 0, stop=k0 + k == TILES - 1)
                                m.then_inc(summed_q, 1)
                            if 2 <= i <= QB and i % 2 == 0:
                                g, v = t * TG + i // 2 - 1, (i // 2 - 1) % 2
                                pe.wait_ge(cnt_hot, g + (START + 1))
                                pe.wait_ge(cnt_added, g + START)
                                for k in range(TILES):
                                    m = nc.tensor.matmul(cnt_ps[:, 0:NB], hotsrc[:, v, k, 0, :], hotsrc[:, v, k, 1, 0:NB],
                                                         start=k == 0, stop=k == TILES - 1)
                                m.then_inc(cnt_sum, 1)
            clear([*attr_in, *idx_ready, *group_free, transposed, rowsT_ready, lin1, h1T_ready, lin2, h2pre_ready, h2_ready,
                   rest_ready, mid_ready, parts_ready, hot_ready, summed_q, added, step, window, taken, attr_placed,
                   cnt_hot, cnt_sum, cnt_added, hot_turned, hotT_ready, window_step, zeroed, filled, picked, carried], [*gathered, scattered])


        CH = 7
        TURNS = NB // CH
        assert NB % CH == 0 and TURNS % 2 == 0

        def node_linear(width, frm, weight, to):
            stage = work[:, 0:CH * width].rearrange("p (c f) -> p c f", c=CH)
            stageT = [work[0:width, 1024 + v * CH * P:1024 + (v + 1) * CH * P] for v in range(2)]
            carried, carried_pe = sem("linear_carried"), sem("linear_carried_pe")
            staged, turned, kept, mapped, placed = (sem(f"linear_{n}") for n in ("staged", "turned", "kept", "mapped", "placed"))
            F = min(CH, 4)

            def turns(eng, turn):
                if TURNS > 2:
                    with eng.Fori(0, TURNS // 2 - 1) as h:
                        turn(h * 2, 0, True)
                        turn(h * 2 + 1, 1, True)
                turn(TURNS - 2, 0, True)
                turn(TURNS - 1, 1, False)

            with nc.Block() as block:
                @block.vector
                def _(dve):
                    def turn(c, v, more):
                        if more:
                            dve.wait_ge(turned, c + 1)
                            dve.sem_inc(carried, 1)
                            nc.vector.tensor_copy(stage, frm((c + 1) * CH, CH)).then_inc(staged, 1)
                        dve.wait_ge(mapped, c + 3)
                        dve.sem_inc(carried, 1)
                        nc.vector.tensor_copy(to(c * CH, CH), ps[0][:, v, 0:CH * D].rearrange("p (c f) -> p c f", c=CH)).then_inc(placed, 1)

                    nc.vector.tensor_copy(stage, frm(0, CH)).then_inc(staged, 1)
                    turns(dve, turn)

                @block.tensor
                def _(pe):
                    def transposes(v):
                        pe.sem_inc(carried_pe, 1)
                        for b in range(CH):
                            m = nc.tensor.transpose(ps[1 + v][0:width, b // 4, b % 4 * P:(b % 4 + 1) * P], stage[:, b, :], ident[:, :])
                        m.then_inc(turned, 1)

                    def turn(c, v, more):
                        if more:
                            pe.wait_ge(staged, c + 2)
                            pe.wait_ge(kept, c + 1)
                            transposes(1 - v)
                        pe.wait_ge(kept, c + 2)
                        pe.wait_ge(placed, c + 1)
                        for b in range(CH):
                            m = nc.tensor.matmul(ps[0][:, v, b * D:(b + 1) * D], stageT[v][:, b * P:(b + 1) * P], weight[:, :], start=True, stop=True)
                        m.then_inc(mapped, 1)

                    pe.sem_inc(placed, 2)
                    pe.sem_inc(kept, 1)
                    pe.sem_inc(mapped, 2)
                    pe.wait_ge(staged, 1)
                    transposes(0)
                    turns(pe, turn)

                @block.scalar
                def _(act):
                    def turn(c, v, more):
                        act.wait_ge(turned, c + 1)
                        act.wait_ge(mapped, c + 1)
                        m = nc.scalar.copy(stageT[v][:, 0:F * P], ps[1 + v][0:width, 0, 0:F * P])
                        if CH > F:
                            m = nc.scalar.copy(stageT[v][:, F * P:CH * P], ps[1 + v][0:width, 1, 0:(CH - F) * P])
                        m.then_inc(kept, 1)

                    turns(act, turn)
            clear([staged, turned, kept, mapped, placed, carried, carried_pe])

        wide = [P, NB, D]

        def steps(body):
            step, asked, rooted = sem("steps_step"), sem("steps_asked"), sem("steps_rooted")
            roots = []
            with nc.Block() as block:
                @block.vector
                def _(dve):
                    n = [0]

                    def link(ins):
                        n[0] += 1
                        ins.then_inc(step, 1)
                        dve.wait_ge(step, n[0])

                    def root(v):
                        roots.append((n[0], v))
                        dve.sem_inc(asked, 1)
                        dve.wait_ge(rooted, len(roots))
                        link(nc.vector.reciprocal(v, v))

                    body(link, root)

                @block.scalar
                def _(act):
                    for i, (at, v) in enumerate(roots):
                        act.wait_ge(asked, i + 1)
                        act.wait_ge(step, at)
                        nc.scalar.activation(v, v, ACT.Sqrt).then_inc(rooted, 1)
            clear([step, asked, rooted])

        acc1 = acc[:, 0:NB * HC].rearrange("p (b f) -> p b f", f=HC)
        c1 = sb("c1", [P, NB])
        c2 = sb("c2", [P, NB])
        steps(lambda link, root: link(nc.vector.tensor_copy(indeg[:, :], acc1[:, :, H])))
        node_linear(H, lambda b, n: acc1[:, bass.ds(b, n), 0:H], W3_s, lambda b, n: f01[:, bass.ds(b, n), :])

        def over(v):
            return v.unsqueeze(2).broadcast_to(wide)

        def along(v):
            return v.unsqueeze(1).broadcast_to(wide)

        def l1_out(link, root):
            link(nc.vector.tensor_tensor(tmp, over(indeg[:, :]), along(b3_r[:, :]), ALU.mult))
            link(nc.vector.tensor_tensor(f01, f01, tmp, ALU.add))
            link(nc.vector.tensor_scalar(c1[:, :], indeg[:, :], 1.0, None, ALU.max))
            link(nc.vector.reciprocal(c1[:, :], c1[:, :]))
            link(nc.vector.tensor_tensor(f01, f01, over(c1[:, :]), ALU.mult))
            link(nc.vector.tensor_tensor(f01, f01, xc[:, :, :], ALU.add))

        steps(l1_out)
        layernorm(xc[:, :, :], f01, xc[:, :, :])

        def l2_in(link, root):
            link(nc.vector.tensor_scalar(c1[:, :], outdeg[:, :], 1.0, None, ALU.max))
            root(c1[:, :])
            link(nc.vector.tensor_tensor(f01, xc[:, :, :], over(c1[:, :]), ALU.mult))
            link(nc.vector.memset(acc[:, 0:(NB + 1) * D], 0.0))
            link(nc.vector.memset(sweep0[:, :], 0.0))

        steps(l2_in)
        store_table(f01)
        aggregate_counted(f01)

        def l2_mid(link, root):
            link(nc.vector.tensor_scalar(c1[:, :], indeg[:, :], 1.0, None, ALU.max))
            root(c1[:, :])
            link(nc.vector.tensor_scalar(c2[:, :], indeg[:, :], 0.5, None, ALU.is_lt))
            link(nc.vector.tensor_tensor(accD, accD, over(c1[:, :]), ALU.mult))
            link(nc.vector.tensor_tensor(tmp, xc[:, :, :], over(c2[:, :]), ALU.mult))
            link(nc.vector.tensor_tensor(tmp, tmp, accD, ALU.add))

        steps(l2_mid)
        node_linear(D, lambda b, n: tmp[:, bass.ds(b, n), :], L2_t, lambda b, n: f01[:, bass.ds(b, n), :])

        def l2_out(link, root):
            link(nc.vector.tensor_tensor(f01, f01, along(l2b_r[:, :]), ALU.add))
            link(nc.vector.tensor_scalar(f01, f01, 0.0, None, ALU.max))

        steps(l2_out)
        layernorm(xc[:, :, :], f01, xc[:, :, :])

        node_linear(D, lambda b, n: xc[:, bass.ds(b, n), :], L3_s, lambda b, n: f01[:, bass.ds(b, n), :])

        def l3_in(link, root):
            link(nc.vector.tensor_scalar(c2[:, :], indeg[:, :], 1.0, None, ALU.add))
            root(c2[:, :])
            link(nc.vector.tensor_tensor(f01, f01, over(c2[:, :]), ALU.mult))
            link(nc.vector.tensor_copy(accD, f01))
            link(nc.vector.memset(acc[:, NB * D:(NB + 1) * D], 0.0))
            link(nc.vector.memset(sweep0[:, :], 0.0))

        steps(l3_in)
        store_table(f01)
        aggregate_counted(f01)

        fsum, fvar = sb("fsum", [P, D]), sb("fvar", [P, D])

        def column_sums(i, part):
            with nc.Block() as block:
                @block.tensor
                def _(pe):
                    nc.tensor.matmul(ps[i][:, 0, 0:D], ones[:, :], part[:, :], start=True, stop=True)

        def bn_mean(link, root):
            link(nc.vector.tensor_tensor(accD, accD, over(c2[:, :]), ALU.mult))
            link(nc.vector.tensor_tensor(accD, accD, along(l3b_r[:, :]), ALU.add))
            link(nc.vector.tensor_scalar(accD[:, NB - 1, :], accD[:, NB - 1, :], valid[:, 0:1], None, ALU.mult))
            link(nc.vector.tensor_reduce(fsum[:, :], accD.rearrange("p b f -> p f b"), AX, ALU.add))

        def bn_var(link, root):
            link(nc.vector.tensor_scalar(fsum[:, :], ps[0][:, 0, 0:D], 1.0 / N, None, ALU.mult))
            link(nc.vector.tensor_tensor(accD, accD, along(fsum[:, :]), ALU.subtract))
            link(nc.vector.tensor_scalar(accD[:, NB - 1, :], accD[:, NB - 1, :], valid[:, 0:1], None, ALU.mult))
            link(nc.vector.tensor_tensor(tmp, accD, accD, ALU.mult))
            link(nc.vector.tensor_reduce(fvar[:, :], tmp.rearrange("p b f -> p f b"), AX, ALU.add))

        def bn_out(link, root):
            link(nc.vector.tensor_scalar(fvar[:, :], ps[1][:, 0, 0:D], 1.0 / N, EPS, ALU.mult, ALU.add))
            root(fvar[:, :])
            link(nc.vector.tensor_tensor(fvar[:, :], fvar[:, :], gam_r[:, :], ALU.mult))
            link(nc.vector.tensor_tensor(accD, accD, along(fvar[:, :]), ALU.mult))
            link(nc.vector.tensor_tensor(accD, accD, along(bet_r[:, :]), ALU.add))
            link(nc.vector.tensor_scalar(accD, accD, 0.0, None, ALU.max))

        steps(bn_mean)
        column_sums(0, fsum)
        steps(bn_var)
        column_sums(1, fvar)
        steps(bn_out)
        layernorm(xc[:, :, :], accD, xc[:, :, :])

        store = sem("out_stored")
        with nc.Block() as block:
            @block.sync
            def _(sp):
                sp.dma_start(out[0:NFULL * P, :].rearrange("(b p) f -> p b f", p=P), xc[:, 0:NFULL, :]).then_inc(store, 16)
                if NREST:
                    sp.dma_start(out[NFULL * P:N, :], xc[0:NREST, NFULL, :]).then_inc(store, 16)
                sp.wait_ge(store, 32 if NREST else 16)


_INS = ["x", "src", "dst", "edge_attr_16", "edge_weight", "L1_gnn_W1", "L1_gnn_b1", "L1_gnn_W2", "L1_gnn_b2",
        "L1_gnn_W3", "L1_gnn_b3", "L2_gnn_W", "L2_gnn_b", "L3_gnn_W", "L3_gnn_b", "L3_gnn_gamma", "L3_gnn_beta"]


def kernel(**inputs):
    import numpy as np
    import concourse.bacc as bacc
    from concourse import mybir as mb
    from concourse.bass_utils import run_bass_kernel_spmd

    nc = bacc.Bacc("TRN2", target_bir_lowering=False, num_devices=1)
    arrays, args = {}, []
    for name in _INS:
        a = np.ascontiguousarray(inputs[name])
        arrays[f"in_{name}"] = a
        args.append(nc.dram_tensor(f"in_{name}", a.shape, mb.dt.from_np(a.dtype), kind="ExternalInput").ap())
    out = nc.dram_tensor("out", inputs["x"].shape, mb.dt.float32, kind="ExternalOutput").ap()
    build(nc, *args, out)
    return run_bass_kernel_spmd(nc, [arrays], core_ids=[0]).results[0]["out"]
```
